# Optimizing a Trainium2 kernel written in Bass

```python
import numpy as np
import jax
import jax.numpy as jnp

def _softmax(x, axis=-1):
    return jax.nn.softmax(x, axis=axis)

def _gelu(x):
    return jax.nn.gelu(x, approximate=True)

def _silu(x):
    return jax.nn.silu(x)

def _sigmoid(x):
    return jax.nn.sigmoid(x)

def _layernorm(x, axis=-1, eps=1e-05):
    m = jnp.mean(x, axis=axis, keepdims=True)
    v = jnp.var(x, axis=axis, keepdims=True)
    return (x - m) / jnp.sqrt(v + eps)

def _scatter_add(tgt, idx, src, axis=0):
    return tgt.at[idx].add(src)

def _segment_sum(src, seg, n):
    return jax.ops.segment_sum(src, seg, n)
kernel_name = 'mk_decoder_preln_d1_seqx_r4_007509'

def setup_inputs(seed: int=0):
    np.random.seed(seed)
    _w = jnp.asarray

    def _rec_inputs():
        import jax
        import jax.numpy as jnp
        _rk = jax.random.key(seed)
        x = 2.818e-05 + 1 * jax.random.normal(jax.random.fold_in(_rk, 1), (4, 512, 512), jnp.float32)
        _lenS = 512 - jax.random.randint(jax.random.fold_in(_rk, 7), (4,), 0, max(1, 512 // 4) + 1, jnp.int32)
        _lenS2 = 512 - jax.random.randint(jax.random.fold_in(_rk, 8), (4,), 0, max(1, 512 // 4) + 1, jnp.int32)
        _ctx_1024P = jax.random.normal(jax.random.fold_in(_rk, 11), (4, 16, 256), jnp.float32)
        _ctx_1024c = jax.random.dirichlet(jax.random.fold_in(_rk, 511), 0.3 * jnp.ones((16,), jnp.float32), (4, 512))
        _ctx_1024t = jnp.einsum('bsk,bkd->bsd', _ctx_1024c, _ctx_1024P)
        _ctx_1024t = _ctx_1024t * jax.lax.rsqrt(jnp.mean(jnp.square(_ctx_1024t)) + 1e-12) * 0.953939
        ctx_1024 = 7.22013e-05 + 1.00017 * (_ctx_1024t + 0.3 * jax.random.normal(jax.random.fold_in(_rk, 611), (4, 512, 256), jnp.float32))
        return (x, ctx_1024)
    x, ctx_1024 = _rec_inputs()

    def _L0_attn_setup():
        import jax, jax.numpy as jnp
        import numpy as np
        H = 16
        CHUNK = 64
        EPS = 1e-05

        def _forward(x, wq, wk, wv, wo, fq1_w, fq1_b, fq2_w, fq2_b, fk1_w, fk1_b, fk2_w, fk2_b, norm_w):
            B, L, D = x.shape
            dk = D // H

            def proj(w):
                return (x @ w.T).reshape(B, L, H, dk).transpose(0, 2, 1, 3)
            q, k, v = (proj(wq), proj(wk), proj(wv))
            q = (q @ fq1_w.T + fq1_b) * (q @ fq2_w.T + fq2_b)
            k = (k @ fk1_w.T + fk1_b) * (k @ fk2_w.T + fk2_b)
            scale = dk ** (-0.5)
            n = L // CHUNK
            qc = q.reshape(B, H, n, CHUNK, dk) * scale
            kc = k.reshape(B, H, n, CHUNK, dk)
            vc = v.reshape(B, H, n, CHUNK, dk)
            kv = jnp.einsum('bhncd,bhnce->bhnde', kc, vc)
            kv = jnp.cumsum(kv, axis=2)
            kv = jnp.concatenate([jnp.zeros_like(kv[:, :, :1]), kv[:, :, :-1]], axis=2)
            inter = jnp.einsum('bhncd,bhnde->bhnce', qc, kv)
            s = jnp.einsum('bhncd,bhnmd->bhncm', qc, kc)
            mask = jnp.tril(jnp.ones((CHUNK, CHUNK), bool))
            s = jnp.where(mask, s, 0.0)
            intra = jnp.einsum('bhncm,bhnmd->bhncd', s, vc)
            o = (inter + intra).reshape(B, H, L, dk)
            o = o * jax.lax.rsqrt(jnp.mean(o * o, axis=-1, keepdims=True) + EPS) * norm_w
            o = o.transpose(0, 2, 1, 3).reshape(B, L, D)
            return o @ wo.T
        key = jax.random.key(seed)
        ks = jax.random.split(key, 16)
        B, L, D = (2, 1024, 512)
        dk = D // H
        g = 2 ** (-2.5)

        def xav(k, n):
            lim = g * np.sqrt(6.0 / (2 * n))
            return jax.random.uniform(k, (n, n), jnp.float32, -lim, lim)
        return {'x': jax.random.normal(ks[0], (B, L, D), jnp.float32), 'wq': xav(ks[1], D), 'wk': xav(ks[2], D), 'wv': xav(ks[3], D), 'wo': xav(ks[4], D), 'fq1_w': xav(ks[5], dk), 'fq1_b': jnp.zeros((dk,), jnp.float32), 'fq2_w': xav(ks[6], dk), 'fq2_b': jnp.zeros((dk,), jnp.float32), 'fk1_w': xav(ks[7], dk), 'fk1_b': jnp.zeros((dk,), jnp.float32), 'fk2_w': xav(ks[8], dk), 'fk2_b': jnp.zeros((dk,), jnp.float32), 'norm_w': jnp.ones((dk,), jnp.float32)}
    _L0_attn_all = _L0_attn_setup()
    _L0_attn_in = {k: v for k, v in _L0_attn_all.items() if k in ('wq', 'wk', 'wv', 'wo', 'fq1_w', 'fq1_b', 'fq2_w', 'fq2_b', 'fk1_w', 'fk1_b', 'fk2_w', 'fk2_b', 'norm_w')}
    del _L0_attn_all

    def _L0_xattn_setup():
        import jax, jax.numpy as jnp
        import numpy as np
        B_, L_, D_MODEL = (4, 512, 256)
        D_STATE, D_CONV, EXPAND = (16, 4, 2)
        D_INNER = EXPAND * D_MODEL
        DT_RANK = (D_MODEL + 15) // 16

        def silu(x):
            return x * jax.nn.sigmoid(x)
        key = jax.random.key(seed)
        ks = jax.random.split(key, 10)
        f32 = jnp.float32
        hidden_states = jax.random.normal(ks[0], (B_, L_, D_MODEL), dtype=f32)
        z = jax.random.normal(ks[1], (B_, D_INNER, L_), dtype=f32)
        in_proj_w = jax.random.normal(ks[2], (D_INNER, D_MODEL), dtype=f32) * 0.02
        conv_w = jax.random.normal(ks[3], (D_INNER, 1, D_CONV), dtype=f32) * 0.1
        conv_b = jax.random.normal(ks[4], (D_INNER,), dtype=f32) * 0.02
        x_proj_w = jax.random.normal(ks[5], (DT_RANK + 2 * D_STATE, D_INNER), dtype=f32) * 0.02
        dt_proj_w = jax.random.uniform(ks[6], (D_INNER, DT_RANK), dtype=f32, minval=-DT_RANK ** (-0.5), maxval=DT_RANK ** (-0.5))
        dt = jnp.exp(jax.random.uniform(ks[7], (D_INNER,), dtype=f32, minval=np.log(0.001), maxval=np.log(0.1)))
        dt_proj_b = jnp.log(jnp.expm1(dt))
        A_log = jnp.log(jnp.broadcast_to(jnp.arange(1, D_STATE + 1, dtype=f32), (D_INNER, D_STATE)))
        D = jnp.ones((D_INNER,), f32)
        return {'hidden_states': hidden_states, 'z': z, 'in_proj_w': in_proj_w, 'conv_w': conv_w, 'conv_b': conv_b, 'x_proj_w': x_proj_w, 'dt_proj_w': dt_proj_w, 'dt_proj_b': dt_proj_b, 'A_log': A_log, 'D': D}
    _L0_xattn_all = _L0_xattn_setup()
    _L0_xattn_in = {k: v for k, v in _L0_xattn_all.items() if k in ('in_proj_w', 'conv_w', 'conv_b', 'x_proj_w', 'dt_proj_w', 'dt_proj_b', 'A_log', 'D')}
    del _L0_xattn_all

    def _L0_ffn_setup():
        import jax, jax.numpy as jnp
        import numpy as np
        D_MODEL = 512
        HIDDEN = 4 * D_MODEL
        B, S = (2, 1024)

        def bit_linear(x, w, b):
            gamma_x = jnp.clip(jnp.max(jnp.abs(x), axis=-1, keepdims=True), 1e-05, None)
            scale_x = 127.0 / gamma_x
            x_dq = jnp.clip(jnp.round(x * scale_x), -128.0, 127.0) / scale_x
            x_ste = x + jax.lax.stop_gradient(x_dq - x)
            gamma_w = jnp.clip(jnp.mean(jnp.abs(w)), 1e-05, None)
            w_dq = jnp.clip(jnp.round(w / gamma_w), -1.0, 1.0) * gamma_w
            w_ste = w + jax.lax.stop_gradient(w_dq - w)
            return jnp.einsum('bsd,hd->bsh', x_ste, w_ste) + b
        key = jax.random.key(seed)
        ks = jax.random.split(key, 7)
        std = 0.02
        return {'x': jax.random.normal(ks[0], (B, S, D_MODEL), dtype=jnp.float32), 'gate_w': jax.random.normal(ks[1], (HIDDEN, D_MODEL), dtype=jnp.float32) * std, 'gate_b': jnp.zeros((HIDDEN,), dtype=jnp.float32), 'val_w': jax.random.normal(ks[2], (HIDDEN, D_MODEL), dtype=jnp.float32) * std, 'val_b': jnp.zeros((HIDDEN,), dtype=jnp.float32), 'out_w': jax.random.normal(ks[3], (D_MODEL, HIDDEN), dtype=jnp.float32) * std, 'out_b': jnp.zeros((D_MODEL,), dtype=jnp.float32)}
    _L0_ffn_all = _L0_ffn_setup()
    _L0_ffn_in = {k: v for k, v in _L0_ffn_all.items() if k in ('gate_w', 'gate_b', 'val_w', 'val_b', 'out_w', 'out_b')}
    del _L0_ffn_all
    return {'x': x, 'ctx_1024': ctx_1024, 'L0_attn_wq': _L0_attn_in['wq'], 'L0_attn_wk': _L0_attn_in['wk'], 'L0_attn_wv': _L0_attn_in['wv'], 'L0_attn_wo': _L0_attn_in['wo'], 'L0_attn_fq1_w': _L0_attn_in['fq1_w'], 'L0_attn_fq1_b': _L0_attn_in['fq1_b'], 'L0_attn_fq2_w': _L0_attn_in['fq2_w'], 'L0_attn_fq2_b': _L0_attn_in['fq2_b'], 'L0_attn_fk1_w': _L0_attn_in['fk1_w'], 'L0_attn_fk1_b': _L0_attn_in['fk1_b'], 'L0_attn_fk2_w': _L0_attn_in['fk2_w'], 'L0_attn_fk2_b': _L0_attn_in['fk2_b'], 'L0_attn_norm_w': _L0_attn_in['norm_w'], 'L0_xattn_in_proj_w': _L0_xattn_in['in_proj_w'], 'L0_xattn_conv_w': _L0_xattn_in['conv_w'], 'L0_xattn_conv_b': _L0_xattn_in['conv_b'], 'L0_xattn_x_proj_w': _L0_xattn_in['x_proj_w'], 'L0_xattn_dt_proj_w': _L0_xattn_in['dt_proj_w'], 'L0_xattn_dt_proj_b': _L0_xattn_in['dt_proj_b'], 'L0_xattn_A_log': _L0_xattn_in['A_log'], 'L0_xattn_D': _L0_xattn_in['D'], 'L0_ffn_gate_w': _L0_ffn_in['gate_w'], 'L0_ffn_gate_b': _L0_ffn_in['gate_b'], 'L0_ffn_val_w': _L0_ffn_in['val_w'], 'L0_ffn_val_b': _L0_ffn_in['val_b'], 'L0_ffn_out_w': _L0_ffn_in['out_w'], 'L0_ffn_out_b': _L0_ffn_in['out_b']}

def reference(x, ctx_1024, L0_attn_wq, L0_attn_wk, L0_attn_wv, L0_attn_wo, L0_attn_fq1_w, L0_attn_fq1_b, L0_attn_fq2_w, L0_attn_fq2_b, L0_attn_fk1_w, L0_attn_fk1_b, L0_attn_fk2_w, L0_attn_fk2_b, L0_attn_norm_w, L0_xattn_in_proj_w, L0_xattn_conv_w, L0_xattn_conv_b, L0_xattn_x_proj_w, L0_xattn_dt_proj_w, L0_xattn_dt_proj_b, L0_xattn_A_log, L0_xattn_D, L0_ffn_gate_w, L0_ffn_gate_b, L0_ffn_val_w, L0_ffn_val_b, L0_ffn_out_w, L0_ffn_out_b):
    import jax
    import jax.numpy as jnp

    def _L0_attn_ref(x, wq, wk, wv, wo, fq1_w, fq1_b, fq2_w, fq2_b, fk1_w, fk1_b, fk2_w, fk2_b, norm_w):
        import jax, jax.numpy as jnp
        import numpy as np
        H = 16
        CHUNK = 64
        EPS = 1e-05

        def _forward(x, wq, wk, wv, wo, fq1_w, fq1_b, fq2_w, fq2_b, fk1_w, fk1_b, fk2_w, fk2_b, norm_w):
            B, L, D = x.shape
            dk = D // H

            def proj(w):
                return (x @ w.T).reshape(B, L, H, dk).transpose(0, 2, 1, 3)
            q, k, v = (proj(wq), proj(wk), proj(wv))
            q = (q @ fq1_w.T + fq1_b) * (q @ fq2_w.T + fq2_b)
            k = (k @ fk1_w.T + fk1_b) * (k @ fk2_w.T + fk2_b)
            scale = dk ** (-0.5)
            n = L // CHUNK
            qc = q.reshape(B, H, n, CHUNK, dk) * scale
            kc = k.reshape(B, H, n, CHUNK, dk)
            vc = v.reshape(B, H, n, CHUNK, dk)
            kv = jnp.einsum('bhncd,bhnce->bhnde', kc, vc)
            kv = jnp.cumsum(kv, axis=2)
            kv = jnp.concatenate([jnp.zeros_like(kv[:, :, :1]), kv[:, :, :-1]], axis=2)
            inter = jnp.einsum('bhncd,bhnde->bhnce', qc, kv)
            s = jnp.einsum('bhncd,bhnmd->bhncm', qc, kc)
            mask = jnp.tril(jnp.ones((CHUNK, CHUNK), bool))
            s = jnp.where(mask, s, 0.0)
            intra = jnp.einsum('bhncm,bhnmd->bhncd', s, vc)
            o = (inter + intra).reshape(B, H, L, dk)
            o = o * jax.lax.rsqrt(jnp.mean(o * o, axis=-1, keepdims=True) + EPS) * norm_w
            o = o.transpose(0, 2, 1, 3).reshape(B, L, D)
            return o @ wo.T
        return _forward(x, wq, wk, wv, wo, fq1_w, fq1_b, fq2_w, fq2_b, fk1_w, fk1_b, fk2_w, fk2_b, norm_w)

    def _L0_xattn_ref(hidden_states, z, in_proj_w, conv_w, conv_b, x_proj_w, dt_proj_w, dt_proj_b, A_log, D):
        import jax, jax.numpy as jnp
        import numpy as np
        B_, L_, D_MODEL = (4, 512, 256)
        D_STATE, D_CONV, EXPAND = (16, 4, 2)
        D_INNER = EXPAND * D_MODEL
        DT_RANK = (D_MODEL + 15) // 16

        def silu(x):
            return x * jax.nn.sigmoid(x)
        Bsz, L, _ = hidden_states.shape
        d_inner, _, d_conv = conv_w.shape
        dt_rank = dt_proj_w.shape[1]
        d_state = A_log.shape[1]
        x = jnp.einsum('bld,ed->bel', hidden_states, in_proj_w)
        xc = jax.lax.conv_general_dilated(x, conv_w, window_strides=(1,), padding=[(d_conv - 1, 0)], feature_group_count=d_inner, dimension_numbers=('NCH', 'OIH', 'NCH'))
        x = silu(xc + conv_b[None, :, None])
        x_dbl = jnp.einsum('bdl,ed->bel', x, x_proj_w)
        dt_low, Bm, Cm = jnp.split(x_dbl, [dt_rank, dt_rank + d_state], axis=1)
        dt = jnp.einsum('brl,dr->bdl', dt_low, dt_proj_w)
        dt = jax.nn.softplus(dt + dt_proj_b[None, :, None])
        A = -jnp.exp(A_log)
        dt_t = jnp.moveaxis(dt, -1, 0)
        B_t = jnp.moveaxis(Bm, -1, 0)
        C_t = jnp.moveaxis(Cm, -1, 0)
        u_t = jnp.moveaxis(x, -1, 0)

        def step(state, inp):
            d, b, c, u = inp
            dA = jnp.exp(d[..., None] * A)
            state = state * dA + (d * u)[..., None] * b[:, None, :]
            y = jnp.einsum('bdn,bn->bd', state, c)
            return (state, y)
        state0 = jnp.zeros((Bsz, d_inner, d_state), x.dtype)
        _, ys = jax.lax.scan(step, state0, (dt_t, B_t, C_t, u_t))
        y = jnp.moveaxis(ys, 0, 2)
        y = y + D[None, :, None] * x
        y = y * silu(z)
        return jnp.swapaxes(y, 1, 2)

    def _L0_ffn_ref(x, gate_w, gate_b, val_w, val_b, out_w, out_b):
        import jax, jax.numpy as jnp
        import numpy as np
        D_MODEL = 512
        HIDDEN = 4 * D_MODEL
        B, S = (2, 1024)

        def bit_linear(x, w, b):
            gamma_x = jnp.clip(jnp.max(jnp.abs(x), axis=-1, keepdims=True), 1e-05, None)
            scale_x = 127.0 / gamma_x
            x_dq = jnp.clip(jnp.round(x * scale_x), -128.0, 127.0) / scale_x
            x_ste = x + jax.lax.stop_gradient(x_dq - x)
            gamma_w = jnp.clip(jnp.mean(jnp.abs(w)), 1e-05, None)
            w_dq = jnp.clip(jnp.round(w / gamma_w), -1.0, 1.0) * gamma_w
            w_ste = w + jax.lax.stop_gradient(w_dq - w)
            return jnp.einsum('bsd,hd->bsh', x_ste, w_ste) + b
        gate = jax.nn.silu(bit_linear(x, gate_w, gate_b))
        val = bit_linear(x, val_w, val_b)
        return bit_linear(gate * val, out_w, out_b)
    x = x + _L0_attn_ref(_layernorm(x, axis=-1), L0_attn_wq, L0_attn_wk, L0_attn_wv, L0_attn_wo, L0_attn_fq1_w, L0_attn_fq1_b, L0_attn_fq2_w, L0_attn_fq2_b, L0_attn_fk1_w, L0_attn_fk1_b, L0_attn_fk2_w, L0_attn_fk2_b, L0_attn_norm_w)
    x = x + _L0_xattn_ref(ctx_1024, _layernorm(x, axis=-1), L0_xattn_in_proj_w, L0_xattn_conv_w, L0_xattn_conv_b, L0_xattn_x_proj_w, L0_xattn_dt_proj_w, L0_xattn_dt_proj_b, L0_xattn_A_log, L0_xattn_D)
    x = x + _L0_ffn_ref(_layernorm(x, axis=-1), L0_ffn_gate_w, L0_ffn_gate_b, L0_ffn_val_w, L0_ffn_val_b, L0_ffn_out_w, L0_ffn_out_b)
    return x

_drawn_inputs = setup_inputs


def setup_inputs(seed=0):
    import zlib

    import numpy as np

    out = dict(_drawn_inputs(seed))
    spreads = {'L0_attn_fq1_b': (0.0, 0.61),
     'L0_attn_fq2_b': (0.0, 0.543),
     'L0_attn_fk1_b': (0.0, 0.618),
     'L0_attn_fk2_b': (0.0, 0.638),
     'L0_attn_norm_w': (1.0, 0.6),
     'L0_xattn_D': (1.0, 0.6),
     'L0_ffn_gate_b': (0.0, 2.0),
     'L0_ffn_val_b': (0.0, 2.0),
     'L0_ffn_out_b': (0.0, 0.8)}
    factors = {'ctx_1024': 2.902,
     'L0_attn_wq': 5.859,
     'L0_attn_wk': 4.72,
     'L0_attn_wv': 3.632,
     'L0_attn_wo': 3.537,
     'L0_attn_fq1_w': 5.841,
     'L0_attn_fq2_w': 8.0,
     'L0_attn_fk1_w': 8.0,
     'L0_attn_fk2_w': 7.071,
     'L0_xattn_in_proj_w': 2.907,
     'L0_xattn_conv_w': 2.965,
     'L0_xattn_conv_b': 8.0,
     'L0_xattn_x_proj_w': 8.0,
     'L0_xattn_dt_proj_w': 8.0,
     'L0_xattn_dt_proj_b': 8.0,
     'L0_xattn_A_log': 8.0,
     'L0_ffn_gate_w': 8.0,
     'L0_ffn_val_w': 8.0,
     'L0_ffn_out_w': 8.0}
    for name, (base, spread) in spreads.items():
        noise = np.random.default_rng([zlib.crc32(name.encode()), seed]).standard_normal(out[name].shape)
        drawn = base * np.exp(spread * noise) if base else spread * noise
        out[name] = jnp.asarray(drawn.astype(out[name].dtype))
    for name, factor in factors.items():
        out[name] = (out[name] * factor).astype(out[name].dtype)
    return out
```

```python
from contextlib import ExitStack

import concourse.bass as bass
from concourse import mybir

fp32 = mybir.dt.float32
bf16 = mybir.dt.bfloat16
fp8 = mybir.dt.float8e4
ALU = mybir.AluOpType
ACT = mybir.ActivationFunctionType
AX = mybir.AxisListType

P = 128
BATCH, L, D = 4, 512, 512
CTX = 256
HEADS, DK = 16, 32
GROUPS = HEADS * DK // P
HPG = P // DK
TT = L // P
KT = D // P
N = 16
RANK = 16
TAPS = 4
HID = 2048
HC = HID // 512
HK = HID // P
WCH = 24
WPC = WCH // 3
SCALE = DK ** -0.5
EPS = 1e-5
MAGIC = 12582912.0
SMALL = 2.0 ** -6
SLOTS = N
W_IN, W_MISC, W_ATTN = 16 * 8, 16 * 12, 16 * 4
SETUP_V = 17


class Signal:

    def __init__(self, ctx, nc, name, per_row):
        self.sem = ctx.enter_context(nc.semaphore(name))
        self.per_row = per_row

    def at(self, b, n=None):
        return self.sem, b * self.per_row + (self.per_row if n is None else n)


class Banks:

    def __init__(self, ctx, nc, name, count, products):
        self.banks = [ctx.enter_context(nc.psum_tensor(f"{name}{k}", [P, 512], fp32)) for k in range(count)]
        self.full_sem = [ctx.enter_context(nc.semaphore(f"{name}{k}_full")) for k in range(count)]
        self.drained_sem = [ctx.enter_context(nc.semaphore(f"{name}{k}_drained")) for k in range(count)]
        self.place = {key: (j % count, j // count) for j, key in enumerate(products)}
        assert len(self.place) == len(products)
        self.per_row = [len(range(k, len(products), count)) for k in range(count)]

    def bank(self, *key):
        return self.banks[self.place[key][0]]

    def full(self, *key):
        return self.full_sem[self.place[key][0]]

    def drained(self, *key):
        return self.drained_sem[self.place[key][0]]

    def free_at(self, b, *key):
        k, r = self.place[key]
        return self.drained_sem[k], b * self.per_row[k] + r

    def full_at(self, b, *key):
        k, r = self.place[key]
        return self.full_sem[k], b * self.per_row[k] + r + 1

    def drained_at(self, b, *key):
        k, r = self.place[key]
        return self.drained_sem[k], b * self.per_row[k] + r + 1


    def all_drained_at(self, b, *keys):
        last = {}
        for key in keys:
            k, r = self.place[key]
            last[k] = max(last.get(k, -1), r)
        return [(self.drained_sem[k], b * self.per_row[k] + r + 1) for k, r in last.items()]


def attn_products():
    out = [("xin", e) for e in range(KT)] + [("xdbl",)] + [("dt", e) for e in range(KT)]
    out += [("xnT", k) for k in range(KT)] + [("q", 0), ("k", 0), ("v", 0)]
    for g in range(GROUPS):
        if g:
            out += [("ms", g - 1)]
        out += [(m, g) for m in ("q1", "q2", "k1", "k2")]
        if g + 1 < GROUPS:
            out += [("q", g + 1)]
        out += [("kfT", g), ("kv", g), ("S", g, 0), ("S", g, 1)]
        if g + 1 < GROUPS:
            out += [("k", g + 1)]
        out += [("S", g, 2), ("S", g, 3)]
        if g + 1 < GROUPS:
            out += [("v", g + 1)]
    out += [("ms", GROUPS - 1)] + [("wo", t) for t in range(TT)] + [("yT", t) for t in range(TT)]
    return out


def ffn_products():
    def hidden(t):
        return [(m, t, c) for c in range(HC) for m in ("G", "V")]

    def down(t):
        return [("hT", t, 0), ("hT", t, 1), ("O", t)]

    out = [("rT",)] + [("xqT", k) for k in range(KT)] + hidden(0)
    for t in range(1, TT):
        out += hidden(t) + down(t - 1)
    return out + down(TT - 1)


def decoder_layer(nc, x, ctxT, wqT, wkT, wvT, woT, fmaps, fbias, normw, inT, convw, convb, xpT, dtpT, dtb, alog,
                  dskip, wffn, brow, outb, ident, ident16, id96, causal, headones, rowpick, out):
    ctx = ExitStack()
    with ctx:
        def sb(name, shape, dt=fp32):
            return ctx.enter_context(nc.sbuf_tensor(name, shape, dt))

        def signal(name, per_row):
            return Signal(ctx, nc, name, per_row)

        def once(name):
            return ctx.enter_context(nc.semaphore(name))

        WQ, WK, WV, WO = (sb(n, [P, KT, D]) for n in ("WQ", "WK", "WV", "WO"))
        FM = sb("FM", [P, 4, P])
        FB = sb("FB", [P, 4])
        FBS = sb("FBS", [P, 1])
        NW = sb("NW", [P, 1])
        WIN = sb("WIN", [P, CTX // P, D])
        CW = sb("CW", [P, KT, TAPS])
        CB = sb("CB", [P, KT])
        WXP = sb("WXP", [P, KT, 2 * N + RANK])
        WDT = sb("WDT", [2 * N + RANK, D])
        DTB = sb("DTB", [P, KT])
        ACOL = sb("ACOL", [P, KT, N])
        DSK = sb("DSK", [P, KT])
        W8 = sb("W8", [P, WCH, 1024], fp8)
        BROW = sb("BROW", [P, HID], bf16)
        RP = sb("RP", [P, TT, 2, 64], bf16)
        RT = sb("RT", [P, TT, P], bf16)
        ZROW = sb("ZROW", [32, P], bf16)
        OUTB = sb("OUTB", [P, D])
        IDF = sb("IDF", [P, P])
        IDB = sb("IDB", [P, P], bf16)
        ID96 = sb("ID96", [96, 32], bf16)
        CAUSAL = sb("CAUSAL", [P, P])
        HONES = sb("HONES", [P, P])
        ONES = sb("ONES", [P, P])
        PICK = sb("PICK", [P, 3])
        EPSC = sb("EPSC", [P, 1])
        ZERO = sb("ZERO", [P, 1])
        ONEC = sb("ONEC", [P, 1])
        CT = sb("CT", [P, CTX // P, L])
        XBC = sb("XBC", [2 * N + RANK, L])
        BC3 = sb("BC3", [96, L], bf16)
        DT = sb("DT", [P, KT, L])
        DU = sb("DU", [P, KT, L])
        DBU = sb("DBU", [P, KT, L])
        YACC = sb("YACC", [P, KT, L])
        DA = [sb(f"DA{i}", [P, KT, L]) for i in range(2)]
        HB = [sb(f"HB{i}", [P, KT, L]) for i in range(2)]
        U, EX = HB
        X1 = sb("X1", [P, TT, D])
        X2 = sb("X2", [P, TT, D])
        XNT = sb("XNT", [P, KT, L])
        BCR = XNT[0:32, 0, :]
        BC2 = XNT[0:32, 1, 0:L // 2].bitcast(bf16)
        OT = sb("OT", [P, KT, L])
        ARENA = sb("ARENA", [P, 6144])

        def part(off, n, dt=fp32):
            a = ARENA[:, off:off + n]
            return a if dt == fp32 else a.bitcast(dt)

        QT, KTT, T1, T2, QF, KF = (part(512 * i, 512) for i in range(6))
        KFN = part(3072, 512).rearrange("p (c d) -> p c d", c=TT)
        V = [part(3584 + 512 * i, 512).rearrange("p (c d) -> p c d", c=TT) for i in range(2)]
        ST = [part(4608 + 512 * i, 512) for i in range(2)]
        KVB = part(5632, 384).rearrange("p (c d) -> p c d", c=3)
        XQ = part(0, 1024, bf16).rearrange("p (t d) -> p t d", t=TT)
        HQ = part(0, 1024, bf16)
        XQT = part(1024, 1024, bf16).rearrange("p (k t) -> p k t", k=KT)
        G = [part(2048 + 512 * i, 512) for i in range(2)]
        HT = part(3072, 1024, bf16).rearrange("p (k t) -> p k t", k=HK)
        H = [part(4096, 2048), XNT[:, :, :].rearrange("p a b -> p (a b)")]
        FENCE = sb("FENCE", [P, 1])
        BST = sb("BST", [P, TT, 6])
        MV = sb("MV", [P, TT, 2])
        LNV = sb("LNV", [P, TT])
        RSTD = sb("RSTD", [P, TT])
        NMR = sb("NMR", [P, TT])
        AMX = sb("AMX", [P, TT])
        AMC = sb("AMC", [P, TT])
        RIN = sb("RIN", [P, TT])
        SXQ = sb("SXQ", [P, TT])
        SDQ = sb("SDQ", [P, 2, TT])
        RSC = sb("RSC", [P, TT, 2])
        RS2 = sb("RS2", [P, TT, 2])
        RS3 = sb("RS3", [P, TT, 2])
        HAM = sb("HAM", [P, 4, TT])
        SHO = sb("SHO", [P, TT])
        ABS = sb("ABS", [P, WCH])
        ASUM = sb("ASUM", [P, 3])
        GAM = sb("GAM", [P, 3])
        GAH = sb("GAH", [P, 3])
        GAN = sb("GAN", [P, 3])
        GAI = sb("GAI", [P, 3])
        GA127 = sb("GA127", [P, 3])
        TERN = sb("TERN", [P, 1024], bf16)

        A = Banks(ctx, nc, "bankA", 3, attn_products())
        F = Banks(ctx, nc, "bankF", 3, ffn_products())
        OBANK = F.banks[2]
        PB = ctx.enter_context(nc.psum_tensor("PB", [P, 512], fp32))
        PC = ctx.enter_context(nc.psum_tensor("PC", [P, 512], fp32))

        w_in = once("w_in")
        w_attn = once("w_attn")
        w_misc = once("w_misc")
        x_loaded = signal("x_loaded", 16)
        ctx_loaded = signal("ctx_loaded", 16)
        out_stored = signal("out_stored", 16 * TT)
        setup_v = once("setup_v")
        setup_a = once("setup_a")
        w_stage = [once(f"w_stage{i}") for i in range(2)]
        abs_done = once("abs_done")
        tern_step = once("tern_step")
        tern_done = once("tern_done")
        gsum_full = once("gsum_full")
        gam_step = once("gam_step")
        tap_done = signal("tap_done", KT)
        conv_step = signal("conv_step", KT * (TAPS - 2))
        u_ready = signal("u_ready", KT)
        split_step = signal("split_step", 5)
        bc_parts = signal("bc_parts", 1)
        dt_raw = signal("dt_raw", KT)
        ex_ready = signal("ex_ready", 1)
        ln_ready = signal("ln_ready", 1)
        sp_step = signal("sp_step", 5)
        dt_ready = signal("dt_ready", 1)
        du_ready = signal("du_ready", 1)
        y_init = signal("y_init", 1)
        da_ready = signal("da_ready", N)
        b_bcast = signal("b_bcast", N)
        c_bcast = signal("c_bcast", N)
        dbu_done = signal("dbu_done", N)
        scan_done = signal("scan_done", N)
        hc_done = signal("hc_done", N)
        ysum_done = signal("ysum_done", N)
        ln_stats = [signal(f"ln{i}_stats", 2 * TT) for i in range(3)]
        ln_log = [signal(f"ln{i}_log", 1) for i in range(3)]
        ln_rstd = [signal(f"ln{i}_rstd", 1) for i in range(3)]
        nmr_step = signal("nmr_step", 1)
        xn_ready = signal("xn_ready", TT)
        kv_step = signal("kv_step", GROUPS)
        kv_ready = signal("kv_ready", GROUPS)
        o_full = signal("o_full", GROUPS)
        o_drained = signal("o_drained", GROUPS)
        sq_ready = signal("sq_ready", GROUPS)
        ms_log = signal("ms_log", GROUPS)
        rms_ready = signal("rms_ready", GROUPS)
        sz_ready = signal("sz_ready", TT)
        yg_ready = signal("yg_ready", 1)
        xn2_ready = signal("xn2_ready", TT)
        q_step = signal("q_step", 8)
        xr_ready = signal("xr_ready", 4)
        xq_ready = signal("xq_ready", TT)
        rp_step = signal("rp_step", 5)
        h_step = signal("h_step", 5 * TT)
        hr_ready = signal("hr_ready", TT)
        hq_ready = signal("hq_ready", TT)
        x3_ready = signal("x3_ready", TT)

        block = ctx.enter_context(nc.Block())

        @block.sync
        def _(sp):
            for dst, src in ((CT[:, :, :], ctxT[0].rearrange("(k p) t -> p k t", p=P)),):
                sp.dma_start(dst, src).then_inc(ctx_loaded.sem, 16)
            for dst, src in ((WIN[:, :, :], inT.rearrange("(k p) n -> p k n", p=P)),
                             (CW[:, :, :], convw), (CB[:, :], convb),
                             (WXP[:, :, :], xpT.rearrange("(k p) n -> p k n", p=P)),
                             (WDT[2 * N:, :], dtpT), (DTB[:, :], dtb), (ACOL[:, :, :], alog), (DSK[:, :], dskip)):
                sp.dma_start(dst, src).then_inc(w_in, 16)
            sp.dma_start(X1[:, :, :], x[0].rearrange("(t p) d -> p t d", p=P)).then_inc(x_loaded.sem, 16)
            for dst, src in ((IDF[:, :], ident), (IDB[:, :], ident16), (ID96[:, :], id96), (CAUSAL[:, :], causal),
                             (HONES[:, :], headones), (PICK[:, :], rowpick), (FM[:, :, :], fmaps),
                             (FB[:, :], fbias), (NW[:, :], normw), (OUTB[:, :], outb.partition_broadcast(P)),
                             (ARENA[0:64, 0:HID], brow[0].partition_broadcast(64)),
                             (ARENA[64:P, 0:HID], brow[1].partition_broadcast(64))):
                sp.dma_start(dst, src).then_inc(w_misc, 16)
            for dst, src in ((WQ, wqT), (WK, wkT), (WV, wvT), (WO, woT)):
                sp.dma_start(dst[:, :, :], src.rearrange("(k p) n -> p k n", p=P)).then_inc(w_attn, 16)
            for i in range(2 * WCH):
                if 2 <= i < WCH + 2:
                    sp.wait_ge(abs_done, i - 1)
                elif i >= WCH + 2:
                    sp.wait_ge(tern_done, i - WCH - 1)
                sp.dma_start(X2[:, 2 * (i % 2):2 * (i % 2) + 2, :].rearrange("p a b -> p (a b)"),
                             wffn[i % WCH]).then_inc(w_stage[i % 2], 16)
            with sp.Fori(1, BATCH) as b:
                sp.wait_ge(*A.full_at(b - 1, "xin", KT - 1))
                sp.dma_start(CT[:, :, :], ctxT[b].rearrange("(k p) t -> p k t", p=P)).then_inc(ctx_loaded.sem, 16)
                sp.wait_ge(*A.drained_at(b - 1, "yT", TT - 1))
                sp.dma_start(X1[:, :, :], x[b].rearrange("(t p) d -> p t d", p=P)).then_inc(x_loaded.sem, 16)
                for t in range(TT):
                    sp.wait_ge(*x3_ready.at(b - 1, t + 1))
                    sp.dma_start(out[b - 1, t * P:(t + 1) * P, :], X2[:, t, :]).then_inc(out_stored.sem, 16)
            for t in range(TT):
                sp.wait_ge(*x3_ready.at(BATCH - 1, t + 1))
                sp.dma_start(out[BATCH - 1, t * P:(t + 1) * P, :], X2[:, t, :]).then_inc(out_stored.sem, 16)
            sp.wait_ge(*out_stored.at(BATCH - 1))

        @block.tensor
        def _(pe):
            def product(ring, b, key, terms, ready=()):
                pe.wait_ge(*ring.free_at(b, *key))
                for r in ready:
                    pe.wait_ge(*r)
                for n, (o, lhs, rhs, start) in enumerate(terms):
                    last = pe.matmul(o, lhs, rhs, start=start, stop=n == len(terms) - 1)
                last.then_inc(ring.full(*key), 1)

            def over_k(o, pairs):
                return [(o, lhs, rhs, n == 0) for n, (lhs, rhs) in enumerate(pairs)]

            def xin(b, e):
                o = A.bank("xin", e)
                product(A, b, ("xin", e), over_k(o[:, :], [(WIN[:, k, e * P:(e + 1) * P], CT[:, k, :])
                                                           for k in range(CTX // P)]),
                        [ctx_loaded.at(b)])

            def xdbl(b):
                product(A, b, ("xdbl",), over_k(A.bank("xdbl")[0:2 * N + RANK, :],
                                                [(WXP[:, k, :], U[:, k, :]) for k in range(KT)]),
                        [u_ready.at(b)])

            def step_size(b, e):
                product(A, b, ("dt", e), over_k(A.bank("dt", e)[:, :],
                                                [(WDT[2 * N:, e * P:(e + 1) * P], XBC[2 * N:, :])]),
                        [A.drained_at(b, "xdbl")])

            def normed_T(b, k):
                o = A.bank("xnT", k)
                pe.wait_ge(*A.free_at(b, "xnT", k))
                pe.wait_ge(*xn_ready.at(b))
                for t in range(TT):
                    last = pe.transpose(o[:, t * P:(t + 1) * P], OT[:, t, k * P:(k + 1) * P], IDF[:, :])
                last.then_inc(A.full("xnT", k), 1)

            def qk(b, name, g):
                w = {"q": WQ, "k": WK}[name]
                product(A, b, (name, g), over_k(A.bank(name, g)[:, :],
                                                [(w[:, k, g * P:(g + 1) * P], XNT[:, k, :]) for k in range(KT)]),
                        A.all_drained_at(b, *(("xnT", k) for k in range(KT))))

            def v(b, g):
                o = A.bank("v", g)
                pe.wait_ge(*A.free_at(b, "v", g))
                for t in range(TT):
                    for k in range(KT):
                        last = pe.matmul(o[:, t * P:(t + 1) * P], XNT[:, k, t * P:(t + 1) * P],
                                         WV[:, k, g * P:(g + 1) * P], start=k == 0, stop=k == KT - 1)
                last.then_inc(A.full("v", g), 1)

            def feature(b, i, g):
                name = ("q1", "q2", "k1", "k2")[i]
                src, of = ((QT, "q"), (KTT, "k"))[i // 2]
                product(A, b, (name, g), over_k(A.bank(name, g)[:, :], [(FM[:, i, :], src)]),
                        [A.drained_at(b, of, g)])

            def keys_T(b, g):
                o = A.bank("kfT", g)
                pe.wait_ge(*A.free_at(b, "kfT", g))
                pe.wait_ge(*A.drained_at(b, "k2", g))
                for c in range(TT):
                    last = pe.transpose(o[:, c * P:(c + 1) * P], KF[:, c * P:(c + 1) * P], IDF[:, :])
                last.then_inc(A.full("kfT", g), 1)

            def kv(b, g):
                o = A.bank("kv", g)
                pe.wait_ge(*A.free_at(b, "kv", g))
                pe.wait_ge(*A.drained_at(b, "kfT", g))
                pe.wait_ge(*A.drained_at(b, "v", g))
                for c in range(TT - 1):
                    last = pe.matmul(o[:, c * P:(c + 1) * P], KFN[:, c, :], V[g % 2][:, c, :], start=True, stop=True)
                last.then_inc(A.full("kv", g), 1)

            def scores(b, g, h):
                o = A.bank("S", g, h)
                rows = slice(DK * h, DK * (h + 1))
                pe.wait_ge(*A.free_at(b, "S", g, h))
                pe.wait_ge(*A.drained_at(b, "k2", g))
                for c in range(TT):
                    last = pe.matmul(o[:, c * P:(c + 1) * P], KF[rows, c * P:(c + 1) * P],
                                     QF[rows, c * P:(c + 1) * P], start=True, stop=True)
                last.then_inc(A.full("S", g, h), 1)

            def attend(b, g, pair):
                o = OBANK
                if pair == 0:
                    pe.wait_ge(*o_drained.at(b, g))
                    pe.wait_ge(*kv_ready.at(b, g + 1))
                    for c in range(1, TT):
                        pe.matmul(o[:, c * P:(c + 1) * P], KVB[:, c - 1, :], QF[:, c * P:(c + 1) * P],
                                  start=c == 1, stop=False, skip_group_check=True)
                heads = (2 * pair, 2 * pair + 1)
                for h in heads:
                    pe.wait_ge(*A.drained_at(b, "S", g, h))
                for c in range(TT):
                    for h in heads:
                        rows = slice(DK * h, DK * (h + 1))
                        last = pe.matmul(o[rows, c * P:(c + 1) * P], V[g % 2][:, c, rows],
                                         ST[h % 2][:, c * P:(c + 1) * P], start=False, stop=True,
                                         skip_group_check=True)
                if pair:
                    last.then_inc(o_full.sem, 1)

            def mean_square(b, g):
                product(A, b, ("ms", g), over_k(A.bank("ms", g)[:, :], [(HONES[:, :], T1)]),
                        [sq_ready.at(b, g + 1)])

            def project(b, t):
                product(A, b, ("wo", t), over_k(A.bank("wo", t)[:, :],
                                                [(OT[:, k, t * P:(t + 1) * P], WO[:, k, :]) for k in range(KT)]),
                        [o_drained.at(b)])

            def mixer_T(b, t):
                o = A.bank("yT", t)
                pe.wait_ge(*A.free_at(b, "yT", t))
                pe.wait_ge(*yg_ready.at(b))
                for e in range(KT):
                    last = pe.transpose(o[:, e * P:(e + 1) * P], YACC[:, e, t * P:(t + 1) * P], IDF[:, :])
                last.then_inc(A.full("yT", t), 1)

            def spread_b(b, n):
                pe.wait_ge(*dbu_done.at(b, n))
                if n == 0:
                    pe.wait_ge(*bc_parts.at(b))
                pe.matmul(PB[:, :], ID96[:, n:n + 1].broadcast_to([96, P]), BC3[:, :],
                          start=True, stop=True).then_inc(b_bcast.sem, 1)

            def spread_c(b, n):
                pe.wait_ge(*hc_done.at(b, n))
                pe.matmul(PC[:, :], ID96[:, N + n:N + n + 1].broadcast_to([96, P]), BC3[:, :],
                          start=True, stop=True).then_inc(c_bcast.sem, 1)

            def scales_T(f):
                o = F.bank("rT")[:, :].bitcast(bf16)
                pe.wait_ge(*F.free_at(f, "rT"))
                pe.wait_ge(*rp_step.at(f))
                for t in range(TT):
                    last = pe.transpose(o[:, t * P:(t + 1) * P], RP[:, t, :, :].rearrange("p g r -> p (g r)"),
                                        IDB[:, :])
                last.then_inc(F.full("rT"), 1)

            def rows_T(f, k):
                o = F.bank("xqT", k)[:, :].bitcast(bf16)
                pe.wait_ge(*F.free_at(f, "xqT", k))
                pe.wait_ge(*xq_ready.at(f))
                for t in range(TT):
                    last = pe.transpose(o[:, t * P:(t + 1) * P], XQ[:, t, k * P:(k + 1) * P], IDB[:, :])
                last.then_inc(F.full("xqT", k), 1)

            def hidden(f, t):
                if t == 0:
                    for r in F.all_drained_at(f, ("rT",), *(("xqT", k) for k in range(KT))):
                        pe.wait_ge(*r)
                for c in range(HC):
                    for i, m in enumerate(("G", "V")):
                        o = F.bank(m, t, c)[:, :]
                        rows = slice(64 * i, 64 * i + 32)
                        pe.wait_ge(*F.free_at(f, m, t, c))
                        pe.matmul(o, RT[rows, t, :], BROW[rows, c * 512:(c + 1) * 512], start=True, stop=False)
                        for k in range(KT):
                            w = W8[:, WPC * i + 2 * k + c // 2, (c % 2) * 512:(c % 2) * 512 + 512]
                            last = pe.matmul(o, XQT[:, k, t * P:(t + 1) * P], w, start=False, stop=k == KT - 1)
                        last.then_inc(F.full(m, t, c), 1)

            def down(f, t):
                for j in range(2):
                    o = F.bank("hT", t, j)[:, :].bitcast(bf16)
                    pe.wait_ge(*F.free_at(f, "hT", t, j))
                    pe.wait_ge(*hq_ready.at(f, t + 1))
                    for k in range(HK // 2):
                        kk = j * HK // 2 + k
                        last = pe.transpose(o[:, k * P:(k + 1) * P], HQ[:, kk * P:(kk + 1) * P], IDB[:, :])
                    last.then_inc(F.full("hT", t, j), 1)
                o = F.bank("O", t)[:, :]
                for r in F.all_drained_at(f, ("hT", t, 0), ("hT", t, 1)):
                    pe.wait_ge(*r)
                pe.wait_ge(*F.free_at(f, "O", t))
                pe.matmul(o[:, 0:2], ZROW[:, :], ZROW[:, 0:2], start=True, stop=False,
                          skip_group_check=True)
                for k in range(HK):
                    last = pe.matmul(o, HT[:, k, :], W8[:, 2 * WPC + k // 2, (k % 2) * 512:(k % 2) * 512 + 512],
                                     start=False, stop=k == HK - 1, skip_group_check=True)
                last.then_inc(F.full("O", t), 1)

            def row(b, f=None):
                ffn = f is not None
                for e in range(KT):
                    xin(b, e)
                if ffn:
                    scales_T(f)
                    for k in range(KT):
                        rows_T(f, k)
                    hidden(f, 0)
                xdbl(b)
                if ffn:
                    hidden(f, 1)
                    down(f, 0)
                for e in range(KT):
                    step_size(b, e)
                if ffn:
                    for t in range(2, TT):
                        hidden(f, t)
                        down(f, t - 1)
                    down(f, TT - 1)
                if not ffn:
                    pe.wait_ge(w_misc, W_MISC)
                    pe.wait_ge(setup_v, SETUP_V)
                    pe.wait_ge(w_attn, W_ATTN)
                for k in range(KT):
                    normed_T(b, k)
                qk(b, "q", 0)
                qk(b, "k", 0)
                v(b, 0)
                spread_b(b, 0)
                spread_c(b, 0)
                for g in range(GROUPS):
                    n = 4 * g
                    more = g + 1 < GROUPS
                    if g:
                        mean_square(b, g - 1)
                    if g == 2 and not ffn:
                        pe.wait_ge(gam_step, 1)
                        pe.matmul(F.banks[0][:, 0:3], ONES[:, :], ASUM[:, :], start=True, stop=True)\
                          .then_inc(gsum_full, 1)
                    for i in range(4):
                        feature(b, i, g)
                        if i == 1:
                            spread_b(b, n + 1)
                    spread_c(b, n + 1)
                    if more:
                        qk(b, "q", g + 1)
                    spread_b(b, n + 2)
                    keys_T(b, g)
                    spread_c(b, n + 2)
                    kv(b, g)
                    scores(b, g, 0)
                    scores(b, g, 1)
                    spread_b(b, n + 3)
                    if more:
                        qk(b, "k", g + 1)
                    spread_c(b, n + 3)
                    attend(b, g, 0)
                    scores(b, g, 2)
                    scores(b, g, 3)
                    if more:
                        spread_b(b, n + 4)
                        v(b, g + 1)
                    attend(b, g, 1)
                    if more:
                        spread_c(b, n + 4)
                mean_square(b, GROUPS - 1)
                for t in range(TT):
                    project(b, t)
                for t in range(TT):
                    mixer_T(b, t)

            pe.wait_ge(w_in, W_IN)
            row(0)
            with pe.Fori(1, BATCH) as b:
                row(b, b - 1)
            last_ffn = BATCH - 1
            scales_T(last_ffn)
            for k in range(KT):
                rows_T(last_ffn, k)
            hidden(last_ffn, 0)
            for t in range(1, TT):
                hidden(last_ffn, t)
                down(last_ffn, t - 1)
            down(last_ffn, TT - 1)

        @block.scalar
        def _(act):
            def drain(b, ring, key, dst, src):
                act.wait_ge(*ring.full_at(b, *key))
                act.activation(dst, src, ACT.Copy).then_inc(ring.drained(*key), 1)

            def tap(b, e):
                act.wait_ge(*A.full_at(b, "xin", e))
                if e == 0:
                    act.wait_ge(*ysum_done.at(b, 0))
                act.activation(U[:, e, :], A.bank("xin", e)[:, :], ACT.Identity, bias=CB[:, e:e + 1],
                               scale=CW[:, e, TAPS - 1:TAPS]).then_inc(tap_done.sem, 1)

            def silu_u(b, e):
                act.wait_ge(*A.drained_at(b, "xin", e))
                act.activation(U[:, e, :], U[:, e, :], ACT.Silu).then_inc(u_ready.sem, 1)

            def rstd(b, i):
                act.wait_ge(*ln_stats[i].at(b))
                act.activation(LNV[:, :], MV[:, :, 1], ACT.Ln, bias=EPSC[:, :]).then_inc(ln_log[i].sem, 1)
                act.wait_ge(*ln_log[i].at(b))
                act.activation(RSTD[:, :], LNV[:, :], ACT.Exp, scale=-0.5).then_inc(ln_rstd[i].sem, 1)

            def step_size(b, e):
                act.wait_ge(*A.full_at(b, "dt", e))
                act.activation(EX[:, e, :], A.bank("dt", e)[:, :], ACT.Abs, bias=DTB[:, e:e + 1])\
                   .then_inc(dt_raw.sem, 1)
                act.activation(DT[:, e, :], A.bank("dt", e)[:, :], ACT.Relu, bias=DTB[:, e:e + 1])\
                   .then_inc(A.drained("dt", e), 1)

            def logs(b):
                act.wait_ge(*dt_raw.at(b))
                act.activation(EX[:, :, :], EX[:, :, :], ACT.Exp, scale=-1.0).then_inc(ex_ready.sem, 1)
                act.wait_ge(*ex_ready.at(b))
                act.wait_ge(*scan_done.at(b, 0))
                act.activation(DBU[:, :, :], EX[:, :, :], ACT.Ln, bias=ONEC[:, :]).then_inc(ln_ready.sem, 1)

            def decay(b, n):
                if n == 0:
                    act.wait_ge(*dt_ready.at(b))
                act.wait_ge(*scan_done.at(b, max(n - 1, 0)))
                for e in range(KT):
                    last = act.activation(DA[n % 2][:, e, 1:], DT[:, e, 1:], ACT.Exp, scale=ACOL[:, e, n:n + 1])
                last.then_inc(da_ready.sem, 1)

            def values(b, g):
                drain(b, A, ("v", g), V[g % 2].rearrange("p c d -> p (c d)"), A.bank("v", g)[:, :])

            def first_factor(b, g, i):
                name, dst = (("q1", T1), ("k1", T2))[i]
                act.wait_ge(*A.full_at(b, name, g))
                if i and g:
                    act.wait_ge(*o_drained.at(b, g))
                act.activation(dst, A.bank(name, g)[:, :], ACT.Identity, bias=FB[:, 2:3] if i else FBS[:, :],
                               scale=1.0 if i else SCALE).then_inc(A.drained(name, g), 1)

            def square(b, g):
                act.wait_ge(*o_full.at(b, g + 1))
                act.activation(T1, OBANK[:, :], ACT.Square).then_inc(sq_ready.sem, 1)

            def rms(b, g):
                act.wait_ge(*A.full_at(b, "ms", g))
                act.activation(T2, A.bank("ms", g)[:, :], ACT.Ln, bias=EPSC[:, :], scale=1.0 / DK)\
                   .then_inc(A.drained("ms", g), 1)
                act.wait_ge(*A.drained_at(b, "ms", g))
                act.activation(T2, T2, ACT.Exp, scale=-0.5).then_inc(rms_ready.sem, 1)

            def gate_z(b, t):
                act.wait_ge(*nmr_step.at(b, 1))
                act.activation(XNT[:, t, :], X1[:, t, :], ACT.Silu, bias=NMR[:, t:t + 1],
                               scale=RSTD[:, t:t + 1]).then_inc(sz_ready.sem, 1)

            def rows_T(f):
                drain(f, F, ("rT",), RT[:, :, :].rearrange("p t r -> p (t r)"),
                      F.bank("rT")[:, :].bitcast(bf16)[:, 0:TT * P])
                for k in range(KT):
                    drain(f, F, ("xqT", k), XQT[:, k, :], F.bank("xqT", k)[:, :].bitcast(bf16)[:, 0:L])

            def hidden_T(f, t):
                for j in range(2):
                    half = HK // 2
                    drain(f, F, ("hT", t, j), HT[:, j * half:(j + 1) * half, :].rearrange("p k t -> p (k t)"),
                          F.bank("hT", t, j)[:, :].bitcast(bf16)[:, 0:half * P])

            def gate(f, t):
                for c in range(HC):
                    n = t * HC + c
                    act.wait_ge(*F.full_at(f, "G", t, c))
                    if n >= 2:
                        act.wait_ge(*F.drained_at(f, "V", (n - 2) // HC, (n - 2) % HC))
                    act.activation(G[n % 2], F.bank("G", t, c)[:, :], ACT.Silu, scale=SDQ[:, 0, t:t + 1])\
                       .then_inc(F.drained("G", t, c), 1)

            def abs_sums(i):
                act.wait_ge(w_stage[i % 2], 16 * (i // 2 + 1))
                act.wait_ge(abs_done, i)
                act.activation(TERN[:, :], X2[:, 2 * (i % 2):2 * (i % 2) + 2, :].rearrange("p a b -> p (a b)"),
                               ACT.Abs, accum_out=ABS[:, i:i + 1]).then_inc(abs_done, 1)

            def row(b, f=None):
                ffn = f is not None
                for e in range(3):
                    tap(b, e)
                if ffn:
                    rstd(f, 2)
                silu_u(b, 0)
                tap(b, 3)
                for e in range(1, KT):
                    silu_u(b, e)
                if ffn:
                    rows_T(f)
                    gate(f, 0)
                drain(b, A, ("xdbl",), XBC[:, :], A.bank("xdbl")[0:2 * N + RANK, :])
                if ffn:
                    gate(f, 1)
                    hidden_T(f, 0)
                for e in range(KT):
                    step_size(b, e)
                if ffn:
                    gate(f, 2)
                logs(b)
                if ffn:
                    hidden_T(f, 1)
                    gate(f, 3)
                    hidden_T(f, 2)
                    hidden_T(f, 3)
                rstd(b, 0)
                decay(b, 0)
                decay(b, 1)
                for k in range(KT):
                    drain(b, A, ("xnT", k), XNT[:, k, :], A.bank("xnT", k)[:, :])
                drain(b, A, ("q", 0), QT, A.bank("q", 0)[:, :])
                drain(b, A, ("k", 0), KTT, A.bank("k", 0)[:, :])
                values(b, 0)
                for n in range(SLOTS):
                    g, r = divmod(n, 4)
                    more = g + 1 < GROUPS
                    if n >= 1 and n + 1 < N:
                        decay(b, n + 1)
                    if r == 0:
                        if g:
                            rms(b, g - 1)
                        first_factor(b, g, 0)
                        first_factor(b, g, 1)
                    if r == 1:
                        if more:
                            drain(b, A, ("q", g + 1), QT, A.bank("q", g + 1)[:, :])
                        drain(b, A, ("kfT", g), KFN.rearrange("p c d -> p (c d)"), A.bank("kfT", g)[:, :])
                    if r == 2 and more:
                        drain(b, A, ("k", g + 1), KTT, A.bank("k", g + 1)[:, :])
                    if r == 3:
                        if more:
                            values(b, g + 1)
                        square(b, g)
                    if not ffn and n < 6:
                        for i in range(4 * n, 4 * n + 4):
                            abs_sums(i)
                rms(b, GROUPS - 1)
                rstd(b, 1)
                for t in range(TT):
                    gate_z(b, t)

            act.wait_ge(w_in, W_IN)
            act.activation(ACOL[:, :, :], ACOL[:, :, :], ACT.Exp).then_inc(setup_a, 1)
            act.wait_ge(setup_v, 4)
            row(0)
            with act.Fori(1, BATCH) as b:
                row(b, b - 1)
            f = BATCH - 1
            rstd(f, 2)
            rows_T(f)
            gate(f, 0)
            gate(f, 1)
            hidden_T(f, 0)
            gate(f, 2)
            hidden_T(f, 1)
            gate(f, 3)
            hidden_T(f, 2)
            hidden_T(f, 3)

        @block.gpsimd
        def _(pool):
            def row(b, f=None):
                pool.wait_ge(*u_ready.at(b))
                if f is not None:
                    pool.wait_ge(*A.full_at(f, "yT", TT - 1))
                pool.tensor_tensor(YACC[:, :, :], U[:, :, :], DSK[:, :].unsqueeze(2).broadcast_to([P, KT, L]),
                                   ALU.mult).then_inc(y_init.sem, 1)
                pool.wait_ge(*y_init.at(b))
                for n in range(N):
                    pool.wait_ge(*hc_done.at(b, n + 1))
                    if n:
                        pool.wait_ge(*ysum_done.at(b, n))
                    pool.tensor_tensor(YACC[:, :, :], YACC[:, :, :], HB[n % 2][:, :, :], ALU.add)\
                        .then_inc(ysum_done.sem, 1)

            pool.wait_ge(w_in, W_IN)
            row(0)
            with pool.Fori(1, BATCH) as b:
                row(b, b - 1)

        @block.vector
        def _(dve):
            def setup():
                done = 0

                def step(ins, hold=True):
                    nonlocal done
                    done += 1
                    ins.then_inc(setup_v, 1)
                    if hold:
                        dve.wait_ge(setup_v, done)

                step(dve.memset(EPSC[:, :], EPS), False)
                step(dve.memset(ONEC[:, :], 1.0), False)
                step(dve.memset(ONES[:, :], 1.0), False)
                step(dve.memset(DA[0][:, :, 0:1], 0.0), False)
                step(dve.memset(DA[1][:, :, 0:1], 0.0), False)
                step(dve.memset(RP[:, :, :, :], 0.0), False)
                dve.wait_ge(setup_a, 1)
                step(dve.tensor_scalar(ACOL[:, :, :], ACOL[:, :, :], -1.0, None, ALU.mult), False)
                return step

            def more_setup(step):
                dve.wait_ge(w_misc, W_MISC)
                step(dve.tensor_scalar(FBS[:, :], FB[:, 0:1], SCALE, None, ALU.mult), False)
                b, r = ARENA[:, 0:HID], ARENA[:, HID:2 * HID]
                p1 = ARENA[:, 2 * HID:2 * HID + HID // 2].bitcast(bf16)
                p2 = ARENA[:, 2 * HID + HID // 2:3 * HID].bitcast(bf16)
                step(dve.tensor_copy(p1, b))
                step(dve.tensor_tensor(r, b, p1, ALU.subtract))
                step(dve.tensor_copy(p2, r))
                step(dve.tensor_tensor(b, r, p2, ALU.subtract))
                step(dve.tensor_scalar(BROW[:, :], p1, PICK[:, 0:1], None, ALU.mult))
                step(dve.scalar_tensor_tensor(BROW[:, :], p2, PICK[:, 1:2], BROW[:, :], ALU.mult, ALU.add))
                step(dve.scalar_tensor_tensor(BROW[:, :], b, PICK[:, 2:3], BROW[:, :], ALU.mult, ALU.add), False)
                dve.wait_ge(w_attn, W_ATTN)
                step(dve.tensor_scalar(WO[:, :, :], WO[:, :, :], NW[:, 0:1], None, ALU.mult), False)
                step(dve.memset(ZROW[:, :], 0.0), False)

            def flat(a):
                return a[:, :, :].rearrange("p a b -> p (a b)")

            def stats(b, i, src):
                for t in range(TT):
                    dve.bn_stats(BST[:, t, :], src[:, t, :]).then_inc(ln_stats[i].sem, 1)
                dve.wait_ge(*ln_stats[i].at(b, TT))
                dve.memset(FENCE[:, :], 0.0)
                for t in range(TT):
                    dve.bn_aggr(MV[:, t, :], BST[:, t, :]).then_inc(ln_stats[i].sem, 1)

            def normed(b, i, src, ready):
                dve.wait_ge(*ln_rstd[i].at(b))
                for t in range(TT):
                    dve.tensor_scalar(OT[:, t, :], src[:, t, :], MV[:, t, 0:1], RSTD[:, t:t + 1],
                                      ALU.subtract, ALU.mult).then_inc(ready.sem, 1)

            def conv(b, e):
                dve.wait_ge(*tap_done.at(b, e + 1))
                x_in = A.bank("xin", e)
                for s in range(1, TAPS):
                    if s > 1:
                        dve.wait_ge(*conv_step.at(b, e * (TAPS - 2) + s - 1))
                    ins = dve.scalar_tensor_tensor(U[:, e, s:], x_in[:, 0:L - s], CW[:, e, TAPS - 1 - s:TAPS - s],
                                                   U[:, e, s:], ALU.mult, ALU.add)
                    ins.then_inc(conv_step.sem if s < TAPS - 1 else A.drained("xin", e), 1)

            def split(b):
                dve.wait_ge(*A.drained_at(b, "xdbl"))
                dve.tensor_copy(BC3[0:32, :], XBC[0:32, :]).then_inc(split_step.sem, 1)
                dve.wait_ge(*split_step.at(b, 1))
                dve.tensor_tensor(BCR, XBC[0:32, :], BC3[0:32, :], ALU.subtract).then_inc(split_step.sem, 1)
                dve.wait_ge(*split_step.at(b, 2))
                dve.tensor_copy(BC2, BCR).then_inc(split_step.sem, 1)
                dve.wait_ge(*split_step.at(b, 3))
                dve.tensor_tensor(BCR, BCR, BC2, ALU.subtract).then_inc(split_step.sem, 1)
                dve.tensor_copy(BC3[32:64, :], BC2).then_inc(split_step.sem, 1)
                dve.wait_ge(*split_step.at(b, 4))
                dve.tensor_copy(BC3[64:96, :], BCR).then_inc(bc_parts.sem, 1)

            def softplus_series(b):
                e, s = flat(EX), flat(DU)
                dve.wait_ge(*ex_ready.at(b))
                dve.tensor_scalar(s, e, 1.0 / 3, -0.5, ALU.mult, ALU.add).then_inc(sp_step.sem, 1)
                dve.wait_ge(*sp_step.at(b, 1))
                dve.tensor_tensor(s, s, e, ALU.mult).then_inc(sp_step.sem, 1)
                dve.wait_ge(*sp_step.at(b, 2))
                dve.scalar_tensor_tensor(s, s, 1.0, e, ALU.add, ALU.mult).then_inc(sp_step.sem, 1)

            def softplus(b):
                e, s, lg = flat(EX), flat(DU), flat(DBU)
                dve.wait_ge(*ln_ready.at(b))
                dve.scalar_tensor_tensor(lg, e, SMALL, lg, ALU.is_lt, ALU.add).then_inc(sp_step.sem, 1)
                dve.wait_ge(*sp_step.at(b, 4))
                dve.tensor_tensor(s, s, lg, ALU.min).then_inc(sp_step.sem, 1)
                dve.wait_ge(*sp_step.at(b, 5))
                dve.wait_ge(*A.drained_at(b, "dt", KT - 1))
                dve.tensor_tensor(flat(DT), flat(DT), s, ALU.add).then_inc(dt_ready.sem, 1)
                dve.wait_ge(*dt_ready.at(b))
                dve.tensor_tensor(s, flat(DT), flat(U), ALU.mult).then_inc(du_ready.sem, 1)

            def over_e(bank):
                return bank[:, :].unsqueeze(1).broadcast_to([P, KT, L])

            def inputs_b(b, n):
                dve.wait_ge(*b_bcast.at(b, n + 1))
                if n == 0:
                    dve.wait_ge(*du_ready.at(b))
                dve.tensor_tensor(DBU[:, :, :], DU[:, :, :], over_e(PB), ALU.mult).then_inc(dbu_done.sem, 1)

            def scan(b, n):
                dve.wait_ge(*dbu_done.at(b, n + 1))
                dve.wait_ge(*da_ready.at(b, n + 1))
                if n < 2:
                    dve.wait_ge(*y_init.at(b))
                else:
                    dve.wait_ge(*ysum_done.at(b, n - 1))
                dve.tensor_tensor_scan(flat(HB[n % 2]), flat(DA[n % 2]), flat(DBU), 0.0, ALU.mult, ALU.add)\
                   .then_inc(scan_done.sem, 1)

            def outputs_c(b, n):
                dve.wait_ge(*scan_done.at(b, n + 1))
                dve.wait_ge(*c_bcast.at(b, n + 1))
                dve.tensor_tensor(HB[n % 2][:, :, :], HB[n % 2][:, :, :], over_e(PC), ALU.mult)\
                   .then_inc(hc_done.sem, 1)

            def feature(b, g, i):
                two, one, bias, t, dst = (("q2", "q1", 1, T1, QF), ("k2", "k1", 3, T2, KF))[i]
                dve.wait_ge(*A.full_at(b, two, g))
                dve.wait_ge(*A.drained_at(b, one, g))
                dve.scalar_tensor_tensor(dst, A.bank(two, g)[:, :], FB[:, bias:bias + 1], t, ALU.add, ALU.mult)\
                   .then_inc(A.drained(two, g), 1)

            def states(b, g):
                dve.wait_ge(*A.full_at(b, "kv", g))
                kv = A.bank("kv", g)[:, 0:3 * P].rearrange("p (c d) -> p c d", c=TT - 1)
                dve.tensor_tensor(KVB, kv, HONES[:, :].unsqueeze(1).broadcast_to([P, TT - 1, P]), ALU.mult)\
                   .then_inc(A.drained("kv", g), 1)
                dve.wait_ge(*A.drained_at(b, "kv", g))
                dve.tensor_tensor(KVB[:, 1, :], KVB[:, 1, :], KVB[:, 0, :], ALU.add).then_inc(kv_step.sem, 1)
                dve.wait_ge(*kv_step.at(b, g + 1))
                dve.tensor_tensor(KVB[:, 2, :], KVB[:, 2, :], KVB[:, 1, :], ALU.add).then_inc(kv_ready.sem, 1)

            def masked(b, g, c):
                dve.wait_ge(*A.full_at(b, "S", g, c))
                dve.tensor_tensor(ST[c % 2].rearrange("p (h q) -> p h q", h=HPG),
                                  A.bank("S", g, c)[:, :].rearrange("p (h q) -> p h q", h=HPG),
                                  CAUSAL[:, :].unsqueeze(1).broadcast_to([P, HPG, P]), ALU.mult)\
                   .then_inc(A.drained("S", g, c), 1)

            def head_norm(b, g):
                dve.wait_ge(*rms_ready.at(b, g + 1))
                dve.tensor_tensor(OT[:, g, :], OBANK[:, :], T2, ALU.mult).then_inc(o_drained.sem, 1)

            def row_scales(f):
                dve.wait_ge(*xn2_ready.at(f))
                dve.tensor_reduce(AMX[:, :], OT[:, :, :], AX.X, ALU.max, apply_absolute_value=True)\
                   .then_inc(q_step.sem, 1)
                dve.wait_ge(*q_step.at(f, 1))
                dve.tensor_scalar(AMC[:, :], AMX[:, :], 1e-5, None, ALU.max).then_inc(q_step.sem, 1)
                dve.wait_ge(*q_step.at(f, 2))
                dve.reciprocal(RIN[:, :], AMC[:, :]).then_inc(q_step.sem, 1)
                dve.wait_ge(*q_step.at(f, 3))
                dve.tensor_scalar(SXQ[:, :], RIN[:, :], 127.0, None, ALU.mult).then_inc(q_step.sem, 1)
                dve.wait_ge(*q_step.at(f, 4))
                for i in range(2):
                    dve.tensor_scalar(SDQ[:, i, :], AMC[:, :], GA127[:, i:i + 1], None, ALU.mult)\
                       .then_inc(q_step.sem, 1)
                    dve.tensor_scalar(RSC[:, :, i], SXQ[:, :], GAI[:, i:i + 1], None, ALU.mult)\
                       .then_inc(q_step.sem, 1)

            def scale_parts(f):
                def times3(a):
                    return a.unsqueeze(3).broadcast_to([P, TT, 2, 3])

                dve.wait_ge(*q_step.at(f))
                dve.tensor_copy(RP[:, :, :, 0:3], times3(RSC[:, :, :])).then_inc(rp_step.sem, 1)
                dve.wait_ge(*rp_step.at(f, 1))
                dve.tensor_tensor(RS2[:, :, :], RSC[:, :, :], RP[:, :, :, 0], ALU.subtract).then_inc(rp_step.sem, 1)
                dve.wait_ge(*rp_step.at(f, 2))
                dve.tensor_copy(RP[:, :, :, 3:6], times3(RS2[:, :, :])).then_inc(rp_step.sem, 1)
                dve.wait_ge(*rp_step.at(f, 3))
                dve.tensor_tensor(RS3[:, :, :], RS2[:, :, :], RP[:, :, :, 3], ALU.subtract).then_inc(rp_step.sem, 1)
                dve.wait_ge(*rp_step.at(f, 4))
                dve.tensor_copy(RP[:, :, :, 6:9], times3(RS3[:, :, :])).then_inc(rp_step.sem, 1)

            def quantise_rows(f):
                for t in range(TT):
                    dve.tensor_scalar(OT[:, t, :], OT[:, t, :], SXQ[:, t:t + 1], MAGIC, ALU.mult, ALU.add)\
                       .then_inc(xr_ready.sem, 1)
                for t in range(TT):
                    dve.wait_ge(*xr_ready.at(f, t + 1))
                    dve.tensor_scalar(XQ[:, t, :], OT[:, t, :], -MAGIC, 127.0, ALU.add, ALU.min)\
                       .then_inc(xq_ready.sem, 1)

            def gated(f, t):
                for c in range(HC):
                    dve.wait_ge(*F.full_at(f, "V", t, c))
                    dve.wait_ge(*F.drained_at(f, "G", t, c))
                    dve.scalar_tensor_tensor(H[t % 2][:, c * 512:(c + 1) * 512], F.bank("V", t, c)[:, :],
                                             SDQ[:, 1, t:t + 1], G[(t * HC + c) % 2], ALU.mult, ALU.mult)\
                       .then_inc(F.drained("V", t, c), 1)

            def quantise_hidden(f, t):
                h, s = H[t % 2], 5 * t
                for r in F.all_drained_at(f, *(("V", t, c) for c in range(HC))):
                    dve.wait_ge(*r)
                dve.tensor_reduce(HAM[:, 0, t:t + 1], h, AX.X, ALU.max, apply_absolute_value=True)\
                   .then_inc(h_step.sem, 1)
                dve.wait_ge(*h_step.at(f, s + 1))
                dve.tensor_scalar(HAM[:, 1, t:t + 1], HAM[:, 0, t:t + 1], 1e-5, None, ALU.max).then_inc(h_step.sem, 1)
                dve.wait_ge(*h_step.at(f, s + 2))
                dve.reciprocal(HAM[:, 2, t:t + 1], HAM[:, 1, t:t + 1]).then_inc(h_step.sem, 1)
                dve.wait_ge(*h_step.at(f, s + 3))
                dve.tensor_scalar(HAM[:, 3, t:t + 1], HAM[:, 2, t:t + 1], 127.0, None, ALU.mult)\
                   .then_inc(h_step.sem, 1)
                dve.tensor_scalar(SHO[:, t:t + 1], HAM[:, 1, t:t + 1], GA127[:, 2:3], None, ALU.mult)\
                   .then_inc(h_step.sem, 1)
                dve.wait_ge(*h_step.at(f, s + 5))
                dve.tensor_scalar(h, h, HAM[:, 3, t:t + 1], MAGIC, ALU.mult, ALU.add).then_inc(hr_ready.sem, 1)
                dve.wait_ge(*hr_ready.at(f, t + 1))
                if t:
                    dve.wait_ge(*F.full_at(f, "hT", t - 1, 1))
                dve.tensor_scalar(HQ, h, -MAGIC, 127.0, ALU.add, ALU.min).then_inc(hq_ready.sem, 1)

            def result(f, t):
                dve.wait_ge(*F.full_at(f, "O", t))
                dve.scalar_tensor_tensor(X2[:, t, :], F.bank("O", t)[:, :], SHO[:, t:t + 1], X2[:, t, :],
                                         ALU.mult, ALU.add).then_inc(F.drained("O", t), 1)
                dve.wait_ge(*F.drained_at(f, "O", t))
                dve.tensor_tensor(X2[:, t, :], X2[:, t, :], OUTB[:, :], ALU.add).then_inc(x3_ready.sem, 1)

            def ternary_scales():
                dve.wait_ge(abs_done, WCH)
                dve.tensor_reduce(ASUM[:, :], ABS[:, :].rearrange("p (w c) -> p w c", w=3), AX.X, ALU.add)\
                   .then_inc(gam_step, 1)
                dve.wait_ge(gsum_full, 1)
                dve.tensor_scalar(GAM[:, :], F.banks[0][:, 0:3], 1.0 / (HID * D), 1e-5, ALU.mult, ALU.max)\
                   .then_inc(gam_step, 1)
                dve.wait_ge(gam_step, 2)
                dve.tensor_scalar(GAH[:, :], GAM[:, :], 0.5, None, ALU.mult).then_inc(gam_step, 1)
                dve.tensor_scalar(GAN[:, :], GAM[:, :], -0.5, None, ALU.mult).then_inc(gam_step, 1)
                dve.reciprocal(GAI[:, :], GAM[:, :]).then_inc(gam_step, 1)
                dve.tensor_scalar(GA127[:, :], GAM[:, :], 1.0 / 127, None, ALU.mult).then_inc(gam_step, 1)
                dve.wait_ge(gam_step, 6)

            def ternary(j):
                i, w = WCH + j, j // WPC
                src = X2[:, 2 * (i % 2):2 * (i % 2) + 2, :].rearrange("p a b -> p (a b)")
                dve.wait_ge(w_stage[i % 2], 16 * (i // 2 + 1))
                dve.wait_ge(tern_done, j)
                dve.tensor_scalar(TERN[:, :], src, GAN[:, w:w + 1], None, ALU.is_lt).then_inc(tern_step, 1)
                dve.wait_ge(tern_step, j + 1)
                dve.scalar_tensor_tensor(W8[:, j, :], src, GAH[:, w:w + 1], TERN[:, :], ALU.is_gt, ALU.subtract,
                                         saturate=False).then_inc(tern_done, 1)

            def row(b, f=None):
                ffn = f is not None
                if ffn:
                    for r in A.all_drained_at(f, *(("yT", t) for t in range(TT))):
                        dve.wait_ge(*r)
                    stats(f, 2, X2)
                conv(b, 0)
                conv(b, 1)
                if ffn:
                    normed(f, 2, X2, xn2_ready)
                    row_scales(f)
                    scale_parts(f)
                    quantise_rows(f)
                conv(b, 2)
                conv(b, 3)
                if ffn:
                    gated(f, 0)
                    quantise_hidden(f, 0)
                split(b)
                if ffn:
                    dve.wait_ge(*bc_parts.at(b))
                    gated(f, 1)
                    quantise_hidden(f, 1)
                    result(f, 0)
                    gated(f, 2)
                    quantise_hidden(f, 2)
                softplus_series(b)
                softplus(b)
                if ffn:
                    result(f, 1)
                    gated(f, 3)
                    quantise_hidden(f, 3)
                    result(f, 2)
                dve.wait_ge(*x_loaded.at(b))
                stats(b, 0, X1)
                normed(b, 0, X1, xn_ready)
                if ffn:
                    result(f, 3)
                for n in range(SLOTS):
                    g, r = divmod(n, 4)
                    inputs_b(b, n)
                    if r == 0 and g:
                        head_norm(b, g - 1)
                    if r == 2:
                        states(b, g)
                    if r == 3:
                        masked(b, g, 2)
                    scan(b, n)
                    if r == 0:
                        feature(b, g, 0)
                    if r == 2:
                        masked(b, g, 0)
                    outputs_c(b, n)
                    if r == 0:
                        feature(b, g, 1)
                    if r == 2:
                        masked(b, g, 1)
                    if r == 3:
                        masked(b, g, 3)
                    if not ffn:
                        if n == 7:
                            ternary_scales()
                        if n > 7:
                            for j in range(3 * (n - 8), 3 * (n - 7)):
                                ternary(j)
                head_norm(b, GROUPS - 1)
                for t in range(TT):
                    dve.wait_ge(*A.full_at(b, "wo", t))
                    dve.tensor_tensor(X1[:, t, :], A.bank("wo", t)[:, :], X1[:, t, :], ALU.add)\
                       .then_inc(A.drained("wo", t), 1)
                for r in A.all_drained_at(b, *(("wo", t) for t in range(TT))):
                    dve.wait_ge(*r)
                stats(b, 1, X1)
                dve.wait_ge(*ln_rstd[1].at(b))
                dve.scalar_tensor_tensor(NMR[:, :], MV[:, :, 0], -1.0, RSTD[:, :], ALU.mult, ALU.mult)\
                   .then_inc(nmr_step.sem, 1)
                dve.wait_ge(*sz_ready.at(b))
                dve.wait_ge(*ysum_done.at(b))
                dve.tensor_tensor(flat(YACC), flat(YACC), flat(XNT), ALU.mult).then_inc(yg_ready.sem, 1)
                if ffn:
                    dve.wait_ge(*out_stored.at(f))
                for t in range(TT):
                    dve.wait_ge(*A.full_at(b, "yT", t))
                    dve.tensor_tensor(X2[:, t, :], A.bank("yT", t)[:, :], X1[:, t, :], ALU.add)\
                       .then_inc(A.drained("yT", t), 1)

            step = setup()
            more_setup(step)
            row(0)
            with dve.Fori(1, BATCH) as b:
                row(b, b - 1)
            f = BATCH - 1
            for r in A.all_drained_at(f, *(("yT", t) for t in range(TT))):
                dve.wait_ge(*r)
            stats(f, 2, X2)
            normed(f, 2, X2, xn2_ready)
            row_scales(f)
            scale_parts(f)
            quantise_rows(f)
            gated(f, 0)
            quantise_hidden(f, 0)
            for t in range(1, TT):
                gated(f, t)
                quantise_hidden(f, t)
                result(f, t - 1)
            result(f, TT - 1)


def kernel(**inputs):
    import ml_dtypes
    import numpy as np
    import concourse.bacc as bacc
    from concourse.bass_utils import run_bass_kernel_spmd

    a = {k: np.asarray(v) for k, v in inputs.items()}
    at = {k[8:]: v for k, v in a.items() if k.startswith("L0_attn_")}
    mx = {k[9:]: v for k, v in a.items() if k.startswith("L0_xattn_")}
    ff = {k[7:]: v for k, v in a.items() if k.startswith("L0_ffn_")}

    def columns(v):
        return np.swapaxes(v.reshape(KT, P, *v.shape[1:]), 0, 1)

    fmaps = np.zeros((P, 4, P), np.float32)
    for i, n in enumerate(("fq1", "fq2", "fk1", "fk2")):
        for h in range(HPG):
            fmaps[DK * h:DK * (h + 1), i, DK * h:DK * (h + 1)] = at[n + "_w"].T

    def up(w):
        return w.T.reshape(KT, P, 2, 1024).transpose(0, 2, 1, 3).reshape(WPC, P, 1024)

    def downwards(w):
        return w.T.reshape(WPC, 2, P, D).transpose(0, 2, 1, 3).reshape(WPC, P, 1024)

    part_of_row = np.arange(P) % 64
    rows = dict(
        x=a["x"], ctxT=a["ctx_1024"].transpose(0, 2, 1), wqT=at["wq"].T, wkT=at["wk"].T, wvT=at["wv"].T,
        woT=at["wo"].T, fmaps=fmaps,
        fbias=np.stack([np.tile(at[n + "_b"], HPG) for n in ("fq1", "fq2", "fk1", "fk2")], axis=1),
        normw=np.tile(at["norm_w"], HPG)[:, None],
        inT=mx["in_proj_w"].T, convw=columns(mx["conv_w"][:, 0, :]), convb=columns(mx["conv_b"]),
        xpT=np.concatenate([mx["x_proj_w"][RANK:], mx["x_proj_w"][:RANK]], axis=0).T, dtpT=mx["dt_proj_w"].T,
        dtb=columns(mx["dt_proj_b"]), alog=columns(mx["A_log"]), dskip=columns(mx["D"]),
        wffn=np.concatenate([up(ff["gate_w"]), up(ff["val_w"]), downwards(ff["out_w"])], axis=0),
        brow=np.stack([ff["gate_b"], ff["val_b"]]), outb=ff["out_b"],
        ident=np.eye(P, dtype=np.float32), ident16=np.eye(P, dtype=ml_dtypes.bfloat16),
        id96=np.tile(np.eye(32, dtype=ml_dtypes.bfloat16), (3, 1)),
        causal=np.triu(np.ones((P, P), np.float32)),
        headones=np.kron(np.eye(HPG, dtype=np.float32), np.ones((DK, DK), np.float32)),
        rowpick=((part_of_row[:, None] < 9) & (part_of_row[:, None] % 3 == np.arange(3))).astype(np.float32),
    )
    nc = bacc.Bacc("TRN2", target_bir_lowering=False, num_devices=1)
    arrays, args = {}, {}
    for name, v in rows.items():
        v = np.ascontiguousarray(v)
        arrays[f"in_{name}"] = v
        args[name] = nc.dram_tensor(f"in_{name}", v.shape, mybir.dt.from_np(v.dtype), kind="ExternalInput").ap()
    args["out"] = nc.dram_tensor("out_dram", (BATCH, L, D), fp32, kind="ExternalOutput").ap()
    decoder_layer(nc, **args)
    return run_bass_kernel_spmd(nc, [arrays], core_ids=[0]).results[0]["out_dram"]
```

```python
from contextlib import ExitStack

import concourse.bass as bass
from concourse import mybir

fp32 = mybir.dt.float32
bf16 = mybir.dt.bfloat16
fp8 = mybir.dt.float8e4
ALU = mybir.AluOpType
ACT = mybir.ActivationFunctionType
AX = mybir.AxisListType

P = 128
BATCH, L, D = 4, 512, 512
CTX = 256
HEADS, DK = 16, 32
GROUPS = HEADS * DK // P
HPG = P // DK
TT = L // P
KT = D // P
N = 16
RANK = 16
TAPS = 4
HID = 2048
HC = HID // 512
HK = HID // P
WCH = 24
WPC = WCH // 3
SCALE = DK ** -0.5
EPS = 1e-5
MAGIC = 12582912.0
THIRD_ROOT = 3.0 ** -0.5
SMALL = 2.0 ** -6
SLOTS = N
W_IN, W_MISC, W_ATTN = 16 * 9, 16 * 11, 16 * 4
SETUP_V = 19


class Signal:

    def __init__(self, ctx, nc, name, per_row):
        self.sem = ctx.enter_context(nc.semaphore(name))
        self.per_row = per_row

    def at(self, b, n=None):
        return self.sem, b * self.per_row + (self.per_row if n is None else n)


class Banks:

    def __init__(self, ctx, nc, name, count, products):
        self.banks = [ctx.enter_context(nc.psum_tensor(f"{name}{k}", [P, 512], fp32)) for k in range(count)]
        self.full_sem = [ctx.enter_context(nc.semaphore(f"{name}{k}_full")) for k in range(count)]
        self.drained_sem = [ctx.enter_context(nc.semaphore(f"{name}{k}_drained")) for k in range(count)]
        self.place = {key: (j % count, j // count) for j, key in enumerate(products)}
        assert len(self.place) == len(products)
        self.per_row = [len(range(k, len(products), count)) for k in range(count)]

    def bank(self, *key):
        return self.banks[self.place[key][0]]

    def full(self, *key):
        return self.full_sem[self.place[key][0]]

    def drained(self, *key):
        return self.drained_sem[self.place[key][0]]

    def opens(self, *key):
        return self.place[key][1] == 0

    def free_at(self, b, *key):
        k, r = self.place[key]
        return self.drained_sem[k], b * self.per_row[k] + r

    def full_at(self, b, *key):
        k, r = self.place[key]
        return self.full_sem[k], b * self.per_row[k] + r + 1

    def drained_at(self, b, *key):
        k, r = self.place[key]
        return self.drained_sem[k], b * self.per_row[k] + r + 1


    def all_drained_at(self, b, *keys):
        last = {}
        for key in keys:
            k, r = self.place[key]
            last[k] = max(last.get(k, -1), r)
        return [(self.drained_sem[k], b * self.per_row[k] + r + 1) for k, r in last.items()]


def row_products():
    out = [("xin", e) for e in range(KT)] + [("xdbl",)] + [("dt", e) for e in range(KT)]
    out += [("xnT", k) for k in range(KT)] + [("q", 0), ("k", 0), ("v", 0)]
    for g in range(GROUPS):
        out += [(m, g) for m in ("q1", "q2", "k1", "k2")]
        if g + 1 < GROUPS:
            out += [("q", g + 1)]
        if g:
            out += [("ms", g - 1)]
        out += [("kfT", g), ("S", g, 0), ("S", g, 1), ("kv", g)]
        if g + 1 < GROUPS:
            out += [("k", g + 1)]
        out += [("S", g, 2), ("S", g, 3)]
        if g + 1 < GROUPS:
            out += [("v", g + 1)]
    return out


def end_products():
    out = [("ms",)] + [("wo", t) for t in range(TT)] + [("yT", t) for t in range(TT)]
    out += [("rT",)] + [("xqT", k) for k in range(KT)]
    for t in range(TT):
        for c in range(HC):
            out += [("G", t, c), ("V", t, c)]
            if t and c in (1, 2):
                out += [("hT", t - 1, c - 1)]
        if t:
            out += [("O", t - 1)]
    return out + [("hT", TT - 1, 0), ("hT", TT - 1, 1), ("O", TT - 1)]


def decoder_layer(nc, x, ctxT, wqT, wkT, wvT, woT, fmaps, fbias, normw, inT, convw, convb, xpT, dtpT, dtb, alog,
                  dskip, wffn, brow, outb, ident, ident16, id96, causal, headones, rowpick, out):
    ctx = ExitStack()
    with ctx:
        def sb(name, shape, dt=fp32):
            return ctx.enter_context(nc.sbuf_tensor(name, shape, dt))

        def signal(name, per_row):
            return Signal(ctx, nc, name, per_row)

        def once(name):
            return ctx.enter_context(nc.semaphore(name))

        WQ, WK, WV, WO = (sb(n, [P, KT, D]) for n in ("WQ", "WK", "WV", "WO"))
        FM = sb("FM", [P, 4, P])
        FB = sb("FB", [P, 4])
        FBS = sb("FBS", [P, 1])
        NW = sb("NW", [P, 1])
        WIN = sb("WIN", [P, CTX // P, D])
        CW = sb("CW", [P, KT, TAPS])
        CB = sb("CB", [P, KT])
        WXP = sb("WXP", [P, KT, 2 * N + RANK])
        WDT = sb("WDT", [2 * N + RANK, D])
        DTB = sb("DTB", [P, KT])
        ACOL = sb("ACOL", [P, KT, N])
        DSK = sb("DSK", [P, KT])
        W8 = sb("W8", [P, WCH, 1024], fp8)
        BROW = sb("BROW", [P, HID], bf16)
        RP = sb("RP", [P, TT, 2, 64], bf16)
        RT = sb("RT", [P, TT, P], bf16)
        ZROW = sb("ZROW", [32, P], bf16)
        OUTB = sb("OUTB", [P, D])
        IDF = sb("IDF", [P, P])
        IDB = sb("IDB", [P, P], bf16)
        ID96 = sb("ID96", [96, 32], bf16)
        CAUSAL = sb("CAUSAL", [P, P])
        HONES = sb("HONES", [P, P])
        ONES = sb("ONES", [P, P])
        PICK = sb("PICK", [P, 3])
        EPSC = sb("EPSC", [P, 1])
        MAGICC = sb("MAGICC", [P, 1])
        SHIFTC = sb("SHIFTC", [P, 1])
        ONEC = sb("ONEC", [P, 1])
        CT = sb("CT", [P, CTX // P, L])
        XBC = sb("XBC", [2 * N + RANK, L])
        BC3 = sb("BC3", [96, L], bf16)
        DT = sb("DT", [P, KT, L])
        DU = sb("DU", [P, KT, L])
        DBU = sb("DBU", [P, KT, L])
        YACC = sb("YACC", [P, KT, L])
        DA = [sb(f"DA{i}", [P, KT, L]) for i in range(2)]
        HB = [sb(f"HB{i}", [P, KT, L]) for i in range(2)]
        U, EX = HB
        X1 = sb("X1", [P, TT, D])
        X2 = sb("X2", [P, TT, D])
        XNT = sb("XNT", [P, KT, L])
        OT = sb("OT", [P, KT, L])
        ARENA = sb("ARENA", [P, 6144])

        def part(off, n, dt=fp32):
            a = ARENA[:, off:off + n]
            return a if dt == fp32 else a.bitcast(dt)

        QT, KTT, T1, T2, QF, KF = (part(512 * i, 512) for i in range(6))
        KFN = part(3072, 512).rearrange("p (c d) -> p c d", c=TT)
        V = [part(3584 + 512 * i, 512).rearrange("p (c d) -> p c d", c=TT) for i in range(2)]
        ST = [part(4608 + 512 * i, 512) for i in range(2)]
        BCR = ST[0][0:32, :]
        BC2 = ST[1][0:32, 0:L // 2].bitcast(bf16)
        XB = part(2560, 2048).rearrange("p (t d) -> p t d", t=TT)
        Z = part(0, 2048).rearrange("p (t d) -> p t d", t=TT)
        KVB = part(5632, 384).rearrange("p (c d) -> p c d", c=3)
        XQ = part(0, 1024, bf16).rearrange("p (t d) -> p t d", t=TT)
        HQ = part(0, 1024, bf16)
        XQT = part(1024, 1024, bf16).rearrange("p (k t) -> p k t", k=KT)
        G = [part(2048 + 512 * i, 512) for i in range(2)]
        HT = part(3072, 1024, bf16).rearrange("p (k t) -> p k t", k=HK)
        H = part(4096, 2048)
        FENCE = sb("FENCE", [P, 1])
        BST = sb("BST", [P, TT, 6])
        MV = sb("MV", [P, TT, 2])
        LNV = sb("LNV", [P, TT])
        RSTD = sb("RSTD", [P, TT])
        NMR = sb("NMR", [P, TT])
        AMX = sb("AMX", [P, TT])
        AMC = sb("AMC", [P, TT])
        RIN = sb("RIN", [P, TT])
        SXQ = sb("SXQ", [P, TT])
        SDQ = sb("SDQ", [P, 2, TT])
        RSC = sb("RSC", [P, TT, 2])
        RS2 = sb("RS2", [P, TT, 2])
        RS3 = sb("RS3", [P, TT, 2])
        HAM = sb("HAM", [P, 4, TT])
        SHO = sb("SHO", [P, TT])
        ABS = sb("ABS", [P, WCH])
        ASUM = sb("ASUM", [P, 3])
        GAM = sb("GAM", [P, 3])
        GAH = sb("GAH", [P, 3])
        GAN = sb("GAN", [P, 3])
        GAI = sb("GAI", [P, 3])
        GA127 = sb("GA127", [P, 3])
        TERN = sb("TERN", [P, 1024], bf16)

        A = Banks(ctx, nc, "bankA", 3, row_products())
        F = Banks(ctx, nc, "bankF", 3, end_products())
        OBANK = F.banks[2]
        PB = ctx.enter_context(nc.psum_tensor("PB", [P, 512], fp32))
        PC = ctx.enter_context(nc.psum_tensor("PC", [P, 512], fp32))

        w_in = once("w_in")
        w_attn = once("w_attn")
        w_misc = once("w_misc")
        x_loaded = signal("x_loaded", 16)
        xb_loaded = signal("xb_loaded", 16)
        ctx_loaded = signal("ctx_loaded", 16)
        out_stored = signal("out_stored", 16 * TT)
        setup_v = once("setup_v")
        setup_a = once("setup_a")
        w_stage = [once(f"w_stage{i}") for i in range(2)]
        abs_done = once("abs_done")
        tern_step = once("tern_step")
        tern_done = once("tern_done")
        gsum_full = once("gsum_full")
        gam_step = once("gam_step")
        tap_done = signal("tap_done", KT)
        conv_step = signal("conv_step", KT * (TAPS - 2))
        u_ready = signal("u_ready", KT)
        split_step = signal("split_step", 5)
        bc_parts = signal("bc_parts", 1)
        dt_raw = signal("dt_raw", KT)
        ex_ready = signal("ex_ready", KT)
        series_ready = signal("series_ready", KT)
        ln_ready = signal("ln_ready", KT)
        sp_step = signal("sp_step", 3 * KT)
        dt_ready = signal("dt_ready", KT)
        du_ready = signal("du_ready", KT)
        y_init = signal("y_init", 1)
        da_ready = signal("da_ready", N)
        b_bcast = signal("b_bcast", N)
        c_bcast = signal("c_bcast", N)
        dbu_done = signal("dbu_done", N)
        scan_done = signal("scan_done", N)
        hc_done = signal("hc_done", N)
        ysum_done = signal("ysum_done", N)
        ln_stats = [signal(f"ln{i}_stats", 2 * TT) for i in range(3)]
        ln_log = [signal(f"ln{i}_log", 1) for i in range(3)]
        ln_rstd = [signal(f"ln{i}_rstd", 1) for i in range(3)]
        nmr_step = signal("nmr_step", 1)
        xn_ready = signal("xn_ready", TT)
        kv_step = signal("kv_step", GROUPS)
        kv_ready = signal("kv_ready", GROUPS)
        o_full = signal("o_full", GROUPS)
        o_drained = signal("o_drained", GROUPS)
        sq_ready = signal("sq_ready", GROUPS)
        ms_log = signal("ms_log", GROUPS)
        rms_ready = signal("rms_ready", GROUPS)
        sz_ready = signal("sz_ready", TT)
        yg_ready = signal("yg_ready", 1)
        xn2_ready = signal("xn2_ready", TT)
        q_step = signal("q_step", 8)
        xr_ready = signal("xr_ready", 4)
        xq_ready = signal("xq_ready", TT)
        rp_step = signal("rp_step", 5)
        h_step = signal("h_step", 5 * TT)
        hr_ready = signal("hr_ready", TT)
        hq_ready = signal("hq_ready", TT)
        bias_added = signal("bias_added", 1)

        block = ctx.enter_context(nc.Block())

        @block.sync
        def _(sp):
            for dst, src in ((CT[:, :, :], ctxT[0].rearrange("(k p) t -> p k t", p=P)),):
                sp.dma_start(dst, src).then_inc(ctx_loaded.sem, 16)
            for dst, src in ((WIN[:, :, :], inT.rearrange("(k p) n -> p k n", p=P)),
                             (CW[:, :, :], convw), (CB[:, :], convb),
                             (WXP[:, :, :], xpT.rearrange("(k p) n -> p k n", p=P)),
                             (WDT[2 * N:, :], dtpT), (DTB[:, :], dtb), (ACOL[:, :, :], alog), (DSK[:, :], dskip),
                             (ID96[:, :], id96)):
                sp.dma_start(dst, src).then_inc(w_in, 16)
            sp.dma_start(XB, x[0].rearrange("(t p) d -> p t d", p=P)).then_inc(xb_loaded.sem, 16)
            for dst, src in ((IDF[:, :], ident), (IDB[:, :], ident16), (CAUSAL[:, :], causal),
                             (HONES[:, :], headones), (PICK[:, :], rowpick), (FM[:, :, :], fmaps),
                             (FB[:, :], fbias), (NW[:, :], normw), (OUTB[:, :], outb.partition_broadcast(P)),
                             (ARENA[0:64, 0:HID], brow[0].partition_broadcast(64)),
                             (ARENA[64:P, 0:HID], brow[1].partition_broadcast(64))):
                sp.dma_start(dst, src).then_inc(w_misc, 16)
            for dst, src in ((WQ, wqT), (WK, wkT), (WV, wvT), (WO, woT)):
                sp.dma_start(dst[:, :, :], src.rearrange("(k p) n -> p k n", p=P)).then_inc(w_attn, 16)
            sp.dma_start(X1[:, :, :], x[0].rearrange("(t p) d -> p t d", p=P)).then_inc(x_loaded.sem, 16)
            for i in range(2 * WCH):
                if 2 <= i < WCH + 2:
                    sp.wait_ge(abs_done, i - 1)
                elif i >= WCH + 2:
                    sp.wait_ge(tern_done, i - WCH - 1)
                sp.dma_start(X2[:, 2 * (i % 2):2 * (i % 2) + 2, :].rearrange("p a b -> p (a b)"),
                             wffn[i % WCH]).then_inc(w_stage[i % 2], 16)
            with sp.Fori(1, BATCH) as b:
                sp.wait_ge(*A.full_at(b - 1, "xin", KT - 1))
                sp.dma_start(CT[:, :, :], ctxT[b].rearrange("(k p) t -> p k t", p=P)).then_inc(ctx_loaded.sem, 16)
                sp.wait_ge(*o_full.at(b - 1))
                sp.dma_start(XB, x[b].rearrange("(t p) d -> p t d", p=P)).then_inc(xb_loaded.sem, 16)
                sp.wait_ge(*F.drained_at(b - 1, "yT", TT - 1))
                sp.dma_start(X1[:, :, :], x[b].rearrange("(t p) d -> p t d", p=P)).then_inc(x_loaded.sem, 16)
                for t in range(TT):
                    sp.wait_ge(*F.drained_at(b - 1, "O", t))
                    sp.dma_start(out[b - 1, t * P:(t + 1) * P, :], X2[:, t, :]).then_inc(out_stored.sem, 16)
            for t in range(TT):
                sp.wait_ge(*F.drained_at(BATCH - 1, "O", t))
                sp.dma_start(out[BATCH - 1, t * P:(t + 1) * P, :], X2[:, t, :]).then_inc(out_stored.sem, 16)
            sp.wait_ge(*out_stored.at(BATCH - 1))

        @block.tensor
        def _(pe):
            def wait_bank(free, *ready):
                pe.wait_ge(*free)
                for r in ready:
                    if r[0] is not free[0]:
                        pe.wait_ge(*r)

            def product(ring, b, key, terms, ready=()):
                if ring is F and ring.opens(*key):
                    for r in ready:
                        pe.wait_ge(*r)
                else:
                    wait_bank(ring.free_at(b, *key), *ready)
                for n, (o, lhs, rhs, start) in enumerate(terms):
                    last = pe.matmul(o, lhs, rhs, start=start, stop=n == len(terms) - 1)
                last.then_inc(ring.full(*key), 1)

            def over_k(o, pairs):
                return [(o, lhs, rhs, n == 0) for n, (lhs, rhs) in enumerate(pairs)]

            def xin(b, e):
                o = A.bank("xin", e)
                product(A, b, ("xin", e), over_k(o[:, :], [(WIN[:, k, e * P:(e + 1) * P], CT[:, k, :])
                                                           for k in range(CTX // P)]),
                        [ctx_loaded.at(b)])

            def xdbl(b):
                product(A, b, ("xdbl",), over_k(A.bank("xdbl")[0:2 * N + RANK, :],
                                                [(WXP[:, k, :], U[:, k, :]) for k in range(KT)]),
                        [u_ready.at(b)])

            def step_size(b, e):
                product(A, b, ("dt", e), over_k(A.bank("dt", e)[:, :],
                                                [(WDT[2 * N:, e * P:(e + 1) * P], XBC[2 * N:, :])]),
                        [A.drained_at(b, "xdbl")])

            def normed_T(b, k):
                o = A.bank("xnT", k)
                pe.wait_ge(*A.free_at(b, "xnT", k))
                pe.wait_ge(*xn_ready.at(b))
                for t in range(TT):
                    last = pe.transpose(o[:, t * P:(t + 1) * P], XB[:, t, k * P:(k + 1) * P], IDF[:, :])
                last.then_inc(A.full("xnT", k), 1)

            def qk(b, name, g):
                w = {"q": WQ, "k": WK}[name]
                product(A, b, (name, g), over_k(A.bank(name, g)[:, :],
                                                [(w[:, k, g * P:(g + 1) * P], XNT[:, k, :]) for k in range(KT)]),
                        A.all_drained_at(b, *(("xnT", k) for k in range(KT))))

            def v(b, g):
                o = A.bank("v", g)
                pe.wait_ge(*A.free_at(b, "v", g))
                for t in range(TT):
                    for k in range(KT):
                        last = pe.matmul(o[:, t * P:(t + 1) * P], XNT[:, k, t * P:(t + 1) * P],
                                         WV[:, k, g * P:(g + 1) * P], start=k == 0, stop=k == KT - 1)
                last.then_inc(A.full("v", g), 1)

            def feature(b, i, g):
                name = ("q1", "q2", "k1", "k2")[i]
                src, of = ((QT, "q"), (KTT, "k"))[i // 2]
                product(A, b, (name, g), over_k(A.bank(name, g)[:, :], [(FM[:, i, :], src)]),
                        [A.drained_at(b, of, g)])

            def keys_T(b, g):
                o = A.bank("kfT", g)
                wait_bank(A.free_at(b, "kfT", g), A.drained_at(b, "k2", g))
                for c in range(TT):
                    last = pe.transpose(o[:, c * P:(c + 1) * P], KF[:, c * P:(c + 1) * P], IDF[:, :])
                last.then_inc(A.full("kfT", g), 1)

            def kv(b, g):
                o = A.bank("kv", g)
                wait_bank(A.free_at(b, "kv", g), A.drained_at(b, "kfT", g), A.drained_at(b, "v", g))
                for c in range(TT - 1):
                    last = pe.matmul(o[:, c * P:(c + 1) * P], KFN[:, c, :], V[g % 2][:, c, :], start=True, stop=True)
                last.then_inc(A.full("kv", g), 1)

            def scores(b, g, h):
                o = A.bank("S", g, h)
                rows = slice(DK * h, DK * (h + 1))
                wait_bank(A.free_at(b, "S", g, h), A.drained_at(b, "k2", g))
                for c in range(TT):
                    last = pe.matmul(o[:, c * P:(c + 1) * P], KF[rows, c * P:(c + 1) * P],
                                     QF[rows, c * P:(c + 1) * P], start=True, stop=True)
                last.then_inc(A.full("S", g, h), 1)

            def attend(b, g, pair):
                o = OBANK
                if pair == 0:
                    pe.wait_ge(*o_drained.at(b, g))
                    pe.wait_ge(*kv_ready.at(b, g + 1))
                    for c in range(1, TT):
                        pe.matmul(o[:, c * P:(c + 1) * P], KVB[:, c - 1, :], QF[:, c * P:(c + 1) * P],
                                  start=c == 1, stop=False, skip_group_check=True)
                heads = (2 * pair, 2 * pair + 1)
                for h in heads:
                    pe.wait_ge(*A.drained_at(b, "S", g, h))
                for c in range(TT):
                    for h in heads:
                        rows = slice(DK * h, DK * (h + 1))
                        last = pe.matmul(o[rows, c * P:(c + 1) * P], V[g % 2][:, c, rows],
                                         ST[h % 2][:, c * P:(c + 1) * P], start=False, stop=True,
                                         skip_group_check=True)
                if pair:
                    last.then_inc(o_full.sem, 1)

            def mean_square(b, g):
                ring, key = (F, ("ms",)) if g == GROUPS - 1 else (A, ("ms", g))
                product(ring, b, key, over_k(ring.bank(*key)[:, :], [(HONES[:, :], OT[:, g, :])]),
                        [sq_ready.at(b, g + 1)])

            def project(b, t):
                product(F, b, ("wo", t), over_k(F.bank("wo", t)[:, :],
                                                [(OT[:, k, t * P:(t + 1) * P], WO[:, k, :]) for k in range(KT)]),
                        [o_drained.at(b)])

            def mixer_T(b, t):
                o = F.bank("yT", t)
                pe.wait_ge(*F.free_at(b, "yT", t))
                pe.wait_ge(*yg_ready.at(b))
                for e in range(KT):
                    last = pe.transpose(o[:, e * P:(e + 1) * P], YACC[:, e, t * P:(t + 1) * P], IDF[:, :])
                last.then_inc(F.full("yT", t), 1)

            def spread_b(b, n):
                pe.wait_ge(*dbu_done.at(b, n))
                if n == 0:
                    pe.wait_ge(*bc_parts.at(b))
                pe.matmul(PB[:, :], ID96[:, n:n + 1].broadcast_to([96, P]), BC3[:, :],
                          start=True, stop=True).then_inc(b_bcast.sem, 1)

            def spread_c(b, n):
                pe.wait_ge(*hc_done.at(b, n))
                pe.matmul(PC[:, :], ID96[:, N + n:N + n + 1].broadcast_to([96, P]), BC3[:, :],
                          start=True, stop=True).then_inc(c_bcast.sem, 1)

            def scales_T(f):
                o = F.bank("rT")[:, :].bitcast(bf16)
                pe.wait_ge(*F.free_at(f, "rT"))
                pe.wait_ge(*rp_step.at(f))
                for t in range(TT):
                    last = pe.transpose(o[:, t * P:(t + 1) * P], RP[:, t, :, :].rearrange("p g r -> p (g r)"),
                                        IDB[:, :])
                last.then_inc(F.full("rT"), 1)

            def rows_T(f, k):
                o = F.bank("xqT", k)[:, :].bitcast(bf16)
                pe.wait_ge(*F.free_at(f, "xqT", k))
                pe.wait_ge(*xq_ready.at(f))
                for t in range(TT):
                    last = pe.transpose(o[:, t * P:(t + 1) * P], XQ[:, t, k * P:(k + 1) * P], IDB[:, :])
                last.then_inc(F.full("xqT", k), 1)

            def hidden(f, t):
                if t == 0:
                    for r in F.all_drained_at(f, ("rT",), *(("xqT", k) for k in range(KT))):
                        pe.wait_ge(*r)
                for c in range(HC):
                    for i, m in enumerate(("G", "V")):
                        o = F.bank(m, t, c)[:, :]
                        rows = slice(64 * i, 64 * i + 32)
                        pe.wait_ge(*F.free_at(f, m, t, c))
                        pe.matmul(o, RT[rows, t, :], BROW[rows, c * 512:(c + 1) * 512], start=True, stop=False)
                        for k in range(KT):
                            w = W8[:, WPC * i + 2 * k + c // 2, (c % 2) * 512:(c % 2) * 512 + 512]
                            last = pe.matmul(o, XQT[:, k, t * P:(t + 1) * P], w, start=False, stop=k == KT - 1)
                        last.then_inc(F.full(m, t, c), 1)
                    if t and c in (1, 2):
                        hidden_T(f, t - 1, c - 1)

            def hidden_T(f, t, j):
                o = F.bank("hT", t, j)[:, :].bitcast(bf16)
                pe.wait_ge(*F.free_at(f, "hT", t, j))
                pe.wait_ge(*hq_ready.at(f, t + 1))
                for k in range(HK // 2):
                    kk = j * HK // 2 + k
                    last = pe.transpose(o[:, k * P:(k + 1) * P], HQ[:, kk * P:(kk + 1) * P], IDB[:, :])
                last.then_inc(F.full("hT", t, j), 1)

            def down(f, t):
                o = F.bank("O", t)[:, :]
                for r in F.all_drained_at(f, ("hT", t, 0), ("hT", t, 1)):
                    pe.wait_ge(*r)
                pe.wait_ge(*F.free_at(f, "O", t))
                pe.matmul(o[:, 0:2], ZROW[:, :], ZROW[:, 0:2], start=True, stop=False,
                          skip_group_check=True)
                for k in range(HK):
                    last = pe.matmul(o, HT[:, k, :], W8[:, 2 * WPC + k // 2, (k % 2) * 512:(k % 2) * 512 + 512],
                                     start=False, stop=k == HK - 1, skip_group_check=True)
                last.then_inc(F.full("O", t), 1)

            def step(b, f):
                new, old = b is not None, f is not None

                def spread(n):
                    if new:
                        spread_b(b, n)
                        spread_c(b, n)

                if new:
                    xin(b, 0)
                if old:
                    mean_square(f, GROUPS - 1)
                if new:
                    xin(b, 1)
                    xin(b, 2)
                if old:
                    project(f, 0)
                if new:
                    xin(b, 3)
                if old:
                    project(f, 1)
                    project(f, 2)
                if new:
                    xdbl(b)
                if old:
                    project(f, 3)
                if new:
                    for e in range(KT):
                        step_size(b, e)
                spread(0)
                if new:
                    if not old:
                        pe.wait_ge(w_misc, W_MISC)
                    for k in range(KT):
                        normed_T(b, k)
                    if not old:
                        pe.wait_ge(w_attn, W_ATTN)
                    qk(b, "q", 0)
                if old:
                    for t in range(TT):
                        mixer_T(f, t)
                if new:
                    qk(b, "k", 0)
                if new:
                    spread_b(b, 1)
                if old:
                    scales_T(f)
                    for k in range(KT):
                        rows_T(f, k)
                if new:
                    spread_c(b, 1)
                if old:
                    hidden(f, 0)
                spread(2)
                if old:
                    hidden(f, 1)
                    down(f, 0)
                spread(3)
                if old:
                    hidden(f, 2)
                    down(f, 1)
                spread(4)
                if old:
                    hidden(f, 3)
                    down(f, 2)
                if new:
                    v(b, 0)
                spread(5)
                if old:
                    hidden_T(f, TT - 1, 0)
                    hidden_T(f, TT - 1, 1)
                    down(f, TT - 1)
                if not new:
                    return
                if not old:
                    pe.wait_ge(setup_v, SETUP_V)
                for g in range(GROUPS):
                    n = 5 + 3 * g
                    more = g + 1 < GROUPS
                    feature(b, 0, g)
                    feature(b, 1, g)
                    spread_b(b, n + 1)
                    feature(b, 2, g)
                    feature(b, 3, g)
                    if more:
                        qk(b, "q", g + 1)
                    if g:
                        mean_square(b, g - 1)
                    spread_c(b, n + 1)
                    keys_T(b, g)
                    scores(b, g, 0)
                    scores(b, g, 1)
                    kv(b, g)
                    if more:
                        spread_b(b, n + 2)
                        qk(b, "k", g + 1)
                        spread_c(b, n + 2)
                    attend(b, g, 0)
                    scores(b, g, 2)
                    scores(b, g, 3)
                    if more:
                        spread_b(b, n + 3)
                        v(b, g + 1)
                    attend(b, g, 1)
                    if g == 0 and not old:
                        pe.wait_ge(gam_step, 1)
                        pe.matmul(F.banks[0][:, 0:3], ONES[:, :], ASUM[:, :], start=True, stop=True)\
                          .then_inc(gsum_full, 1)
                    if more:
                        spread_c(b, n + 3)

            pe.wait_ge(w_in, W_IN)
            step(0, None)
            pe.wait_ge(gam_step, 2)
            with pe.Fori(1, BATCH) as b:
                step(b, b - 1)
            step(None, BATCH - 1)

        @block.scalar
        def _(act):
            def drain(b, ring, key, dst, src):
                act.wait_ge(*ring.full_at(b, *key))
                act.activation(dst, src, ACT.Copy).then_inc(ring.drained(*key), 1)

            def tap(b, e, first):
                act.wait_ge(*A.full_at(b, "xin", e))
                if e == 0 and not first:
                    act.wait_ge(*ysum_done.at(b - 1, N - 1))
                act.activation(U[:, e, :], A.bank("xin", e)[:, :], ACT.Identity, bias=CB[:, e:e + 1],
                               scale=CW[:, e, TAPS - 1:TAPS]).then_inc(tap_done.sem, 1)

            def silu_u(b, e):
                act.wait_ge(*A.drained_at(b, "xin", e))
                act.activation(U[:, e, :], U[:, e, :], ACT.Silu).then_inc(u_ready.sem, 1)

            def rstd(b, i):
                act.wait_ge(*ln_stats[i].at(b))
                act.activation(LNV[:, :], MV[:, :, 1], ACT.Ln, bias=EPSC[:, :]).then_inc(ln_log[i].sem, 1)
                act.wait_ge(*ln_log[i].at(b))
                act.activation(RSTD[:, :], LNV[:, :], ACT.Exp, scale=-0.5).then_inc(ln_rstd[i].sem, 1)

            def step_size(b, e):
                act.wait_ge(*A.full_at(b, "dt", e))
                if e == 0:
                    act.wait_ge(*ysum_done.at(b, 0))
                act.activation(EX[:, e, :], A.bank("dt", e)[:, :], ACT.Abs, bias=DTB[:, e:e + 1])\
                   .then_inc(dt_raw.sem, 1)
                act.activation(DT[:, e, :], A.bank("dt", e)[:, :], ACT.Relu, bias=DTB[:, e:e + 1])\
                   .then_inc(A.drained("dt", e), 1)
                act.wait_ge(*dt_raw.at(b, e + 1))
                act.activation(EX[:, e, :], EX[:, e, :], ACT.Exp, scale=-1.0).then_inc(ex_ready.sem, 1)

            def logs(b, e):
                if e == 0:
                    act.wait_ge(*scan_done.at(b, 0))
                act.wait_ge(*ex_ready.at(b, e + 1))
                act.activation(DU[:, e, :], EX[:, e, :], ACT.Square, bias=SHIFTC[:, :], scale=THIRD_ROOT)\
                   .then_inc(series_ready.sem, 1)
                act.activation(DBU[:, e, :], EX[:, e, :], ACT.Ln, bias=ONEC[:, :]).then_inc(ln_ready.sem, 1)

            def decay(b, n):
                if n == 0:
                    act.wait_ge(*dt_ready.at(b))
                act.wait_ge(*scan_done.at(b, max(n - 1, 0)))
                for e in range(KT):
                    last = act.activation(DA[n % 2][:, e, 1:], DT[:, e, 1:], ACT.Exp, scale=ACOL[:, e, n:n + 1])
                last.then_inc(da_ready.sem, 1)

            def values(b, g):
                drain(b, A, ("v", g), V[g % 2].rearrange("p c d -> p (c d)"), A.bank("v", g)[:, :])

            def first_factor(b, g, i):
                name, dst = (("q1", T1), ("k1", T2))[i]
                act.wait_ge(*A.full_at(b, name, g))
                act.activation(dst, A.bank(name, g)[:, :], ACT.Identity, bias=FB[:, 2:3] if i else FBS[:, :],
                               scale=1.0 if i else SCALE).then_inc(A.drained(name, g), 1)

            def square(b, g):
                act.wait_ge(*o_full.at(b, g + 1))
                act.activation(OT[:, g, :], OBANK[:, :], ACT.Square).then_inc(sq_ready.sem, 1)

            def rms(b, g):
                ring, key = (F, ("ms",)) if g == GROUPS - 1 else (A, ("ms", g))
                act.wait_ge(*ring.full_at(b, *key))
                act.activation(OT[:, g, :], ring.bank(*key)[:, :], ACT.Ln, bias=EPSC[:, :], scale=1.0 / DK)\
                   .then_inc(ring.drained(*key), 1)
                act.wait_ge(*ring.drained_at(b, *key))
                act.activation(OT[:, g, :], OT[:, g, :], ACT.Exp, scale=-0.5).then_inc(rms_ready.sem, 1)

            def gate_z(b, t):
                act.wait_ge(*nmr_step.at(b, 1))
                act.activation(Z[:, t, :], X1[:, t, :], ACT.Silu, bias=NMR[:, t:t + 1],
                               scale=RSTD[:, t:t + 1]).then_inc(sz_ready.sem, 1)

            def rows_T(f):
                drain(f, F, ("rT",), RT[:, :, :].rearrange("p t r -> p (t r)"),
                      F.bank("rT")[:, :].bitcast(bf16)[:, 0:TT * P])
                for k in range(KT):
                    drain(f, F, ("xqT", k), XQT[:, k, :], F.bank("xqT", k)[:, :].bitcast(bf16)[:, 0:L])

            def hidden_T(f, t, j):
                half = HK // 2
                drain(f, F, ("hT", t, j), HT[:, j * half:(j + 1) * half, :].rearrange("p k t -> p (k t)"),
                      F.bank("hT", t, j)[:, :].bitcast(bf16)[:, 0:half * P])

            def gate(f, t):
                for c in range(HC):
                    n = t * HC + c
                    act.wait_ge(*F.full_at(f, "G", t, c))
                    if n >= 2:
                        act.wait_ge(*F.drained_at(f, "V", (n - 2) // HC, (n - 2) % HC))
                    act.activation(G[n % 2], F.bank("G", t, c)[:, :], ACT.Silu, scale=SDQ[:, 0, t:t + 1])\
                       .then_inc(F.drained("G", t, c), 1)
                    if t and c in (1, 2):
                        hidden_T(f, t - 1, c - 1)
                act.wait_ge(*h_step.at(f, 5 * (t + 1)))
                act.activation(H, H, ACT.Identity, bias=MAGICC[:, :], scale=HAM[:, 3, t:t + 1])\
                   .then_inc(hr_ready.sem, 1)

            def abs_sums(i):
                act.wait_ge(w_stage[i % 2], 16 * (i // 2 + 1))
                act.wait_ge(abs_done, i)
                act.activation(TERN[:, :], X2[:, 2 * (i % 2):2 * (i % 2) + 2, :].rearrange("p a b -> p (a b)"),
                               ACT.Abs, accum_out=ABS[:, i:i + 1]).then_inc(abs_done, 1)

            def step(b, f):
                new, old = b is not None, f is not None
                if new:
                    tap(b, 0, not old)
                if old:
                    rms(f, GROUPS - 1)
                if new:
                    tap(b, 1, not old)
                    tap(b, 2, not old)
                    silu_u(b, 0)
                    tap(b, 3, not old)
                    for e in range(1, KT):
                        silu_u(b, e)
                    drain(b, A, ("xdbl",), XBC[:, :], A.bank("xdbl")[0:2 * N + RANK, :])
                exp_and_log()
                if new:
                    rstd(b, 0)
                    step_size(b, 0)
                    step_size(b, 1)
                    logs(b, 0)
                if old:
                    rstd(f, 1)
                if new:
                    step_size(b, 2)
                    logs(b, 1)
                    step_size(b, 3)
                    logs(b, 2)
                    logs(b, 3)
                    for k in range(KT):
                        drain(b, A, ("xnT", k), XNT[:, k, :], A.bank("xnT", k)[:, :])
                if old:
                    for t in range(TT):
                        gate_z(f, t)
                    exp_and_log()
                if new:
                    decay(b, 0)
                if old:
                    rstd(f, 2)
                if new:
                    decay(b, 1)
                if old:
                    rows_T(f)
                if new:
                    decay(b, 2)
                    weights_beside(2, old)
                if old:
                    gate(f, 0)
                    gate(f, 1)
                if new:
                    exp_and_log()
                    decay(b, 3)
                    weights_beside(3, old)
                    decay(b, 4)
                    weights_beside(4, old)
                if old:
                    gate(f, 2)
                    gate(f, 3)
                if new:
                    exp_and_log()
                if old:
                    hidden_T(f, TT - 1, 0)
                    hidden_T(f, TT - 1, 1)
                if not new:
                    return
                decay(b, 5)
                weights_beside(5, old)
                if not old:
                    act.wait_ge(setup_v, SETUP_V)
                drain(b, A, ("q", 0), QT, A.bank("q", 0)[:, :])
                drain(b, A, ("k", 0), KTT, A.bank("k", 0)[:, :])
                if old:
                    act.wait_ge(*F.full_at(f, "O", TT - 1))
                values(b, 0)
                decay(b, 6)
                weights_beside(6, old)
                for g in range(GROUPS):
                    n = 5 + 3 * g
                    more = g + 1 < GROUPS
                    first_factor(b, g, 0)
                    first_factor(b, g, 1)
                    if g:
                        square(b, g - 1)
                    if more:
                        drain(b, A, ("q", g + 1), QT, A.bank("q", g + 1)[:, :])
                    if g:
                        rms(b, g - 1)
                    drain(b, A, ("kfT", g), KFN.rearrange("p c d -> p (c d)"), A.bank("kfT", g)[:, :])
                    if more:
                        decay(b, n + 2)
                        weights_beside(n + 2, old)
                        drain(b, A, ("k", g + 1), KTT, A.bank("k", g + 1)[:, :])
                        decay(b, n + 3)
                        values(b, g + 1)
                        decay(b, n + 4)
                square(b, GROUPS - 1)

            def weights_beside(n, old):
                if not old and 2 <= n < 8:
                    for i in range(4 * (n - 2), 4 * (n - 1)):
                        abs_sums(i)

            def exp_and_log():
                act.preload_act_table_set("natural_log_exp_and_others")

            act.wait_ge(w_in, W_IN)
            exp_and_log()
            act.activation(ACOL[:, :, :], ACOL[:, :, :], ACT.Exp).then_inc(setup_a, 1)
            act.wait_ge(setup_v, 4)
            step(0, None)
            with act.Fori(1, BATCH) as b:
                step(b, b - 1)
            step(None, BATCH - 1)

        @block.gpsimd
        def _(pool):
            def bias(f):
                pool.wait_ge(*xn2_ready.at(f))
                pool.tensor_tensor(X2[:, :, :], X2[:, :, :], OUTB[:, :].unsqueeze(1).broadcast_to([P, TT, D]),
                                   ALU.add).then_inc(bias_added.sem, 1)

            def row(b, f=None):
                pool.wait_ge(*u_ready.at(b))
                if f is not None:
                    pool.wait_ge(*F.full_at(f, "yT", TT - 1))
                pool.tensor_tensor(YACC[:, :, :], U[:, :, :], DSK[:, :].unsqueeze(2).broadcast_to([P, KT, L]),
                                   ALU.mult).then_inc(y_init.sem, 1)
                pool.wait_ge(*y_init.at(b))
                for n in range(N):
                    pool.wait_ge(*hc_done.at(b, n + 1))
                    if n:
                        pool.wait_ge(*ysum_done.at(b, n))
                    pool.tensor_tensor(YACC[:, :, :], YACC[:, :, :], HB[n % 2][:, :, :], ALU.add)\
                        .then_inc(ysum_done.sem, 1)
                    if n == 0 and f is not None:
                        bias(f)

            pool.wait_ge(w_in, W_IN)
            row(0)
            with pool.Fori(1, BATCH) as b:
                row(b, b - 1)
            bias(BATCH - 1)

        @block.vector
        def _(dve):
            def setup():
                done = 0

                def step(ins, hold=True):
                    nonlocal done
                    done += 1
                    ins.then_inc(setup_v, 1)
                    if hold:
                        dve.wait_ge(setup_v, done)

                step(dve.memset(EPSC[:, :], EPS), False)
                step(dve.memset(ONEC[:, :], 1.0), False)
                step(dve.memset(MAGICC[:, :], MAGIC), False)
                step(dve.memset(SHIFTC[:, :], -0.75 * THIRD_ROOT), False)
                step(dve.memset(ONES[:, :], 1.0), False)
                step(dve.memset(DA[0][:, :, 0:1], 0.0), False)
                step(dve.memset(DA[1][:, :, 0:1], 0.0), False)
                step(dve.memset(RP[:, :, :, :], 0.0), False)
                dve.wait_ge(setup_a, 1)
                step(dve.tensor_scalar(ACOL[:, :, :], ACOL[:, :, :], -1.0, None, ALU.mult), False)
                return step

            def more_setup(step):
                dve.wait_ge(w_misc, W_MISC)
                step(dve.tensor_scalar(FBS[:, :], FB[:, 0:1], SCALE, None, ALU.mult), False)
                b, r = ARENA[:, 0:HID], ARENA[:, HID:2 * HID]
                p1 = ARENA[:, 2 * HID:2 * HID + HID // 2].bitcast(bf16)
                p2 = ARENA[:, 2 * HID + HID // 2:3 * HID].bitcast(bf16)
                step(dve.tensor_copy(p1, b))
                step(dve.tensor_tensor(r, b, p1, ALU.subtract))
                step(dve.tensor_copy(p2, r))
                step(dve.tensor_tensor(b, r, p2, ALU.subtract))
                step(dve.tensor_scalar(BROW[:, :], p1, PICK[:, 0:1], None, ALU.mult))
                step(dve.scalar_tensor_tensor(BROW[:, :], p2, PICK[:, 1:2], BROW[:, :], ALU.mult, ALU.add))
                step(dve.scalar_tensor_tensor(BROW[:, :], b, PICK[:, 2:3], BROW[:, :], ALU.mult, ALU.add), False)
                dve.wait_ge(w_attn, W_ATTN)
                step(dve.tensor_scalar(WO[:, :, :], WO[:, :, :], NW[:, 0:1], None, ALU.mult), False)
                step(dve.memset(ZROW[:, :], 0.0), False)

            def flat(a):
                return a[:, :, :].rearrange("p a b -> p (a b)")

            def stats(b, i, src):
                for t in range(TT):
                    dve.bn_stats(BST[:, t, :], src[:, t, :]).then_inc(ln_stats[i].sem, 1)
                dve.wait_ge(*ln_stats[i].at(b, TT))
                dve.memset(FENCE[:, :], 0.0)
                for t in range(TT):
                    dve.bn_aggr(MV[:, t, :], BST[:, t, :]).then_inc(ln_stats[i].sem, 1)

            def normed(b, i, src, ready):
                dve.wait_ge(*ln_rstd[i].at(b))
                dst = src if i == 0 else OT
                for t in range(TT):
                    dve.tensor_scalar(dst[:, t, :], src[:, t, :], MV[:, t, 0:1], RSTD[:, t:t + 1],
                                      ALU.subtract, ALU.mult).then_inc(ready.sem, 1)

            def conv(b, e):
                dve.wait_ge(*tap_done.at(b, e + 1))
                x_in = A.bank("xin", e)
                for s in range(1, TAPS):
                    if s > 1:
                        dve.wait_ge(*conv_step.at(b, e * (TAPS - 2) + s - 1))
                    ins = dve.scalar_tensor_tensor(U[:, e, s:], x_in[:, 0:L - s], CW[:, e, TAPS - 1 - s:TAPS - s],
                                                   U[:, e, s:], ALU.mult, ALU.add)
                    ins.then_inc(conv_step.sem if s < TAPS - 1 else A.drained("xin", e), 1)

            def split(b):
                dve.wait_ge(*A.drained_at(b, "xdbl"))
                dve.tensor_copy(BC3[0:32, :], XBC[0:32, :]).then_inc(split_step.sem, 1)
                dve.wait_ge(*split_step.at(b, 1))
                dve.tensor_tensor(BCR, XBC[0:32, :], BC3[0:32, :], ALU.subtract).then_inc(split_step.sem, 1)
                dve.wait_ge(*split_step.at(b, 2))
                dve.tensor_copy(BC2, BCR).then_inc(split_step.sem, 1)
                dve.wait_ge(*split_step.at(b, 3))
                dve.tensor_tensor(BCR, BCR, BC2, ALU.subtract).then_inc(split_step.sem, 1)
                dve.tensor_copy(BC3[32:64, :], BC2).then_inc(split_step.sem, 1)
                dve.wait_ge(*split_step.at(b, 4))
                dve.tensor_copy(BC3[64:96, :], BCR).then_inc(bc_parts.sem, 1)

            def softplus(b, i):
                e, s, lg = EX[:, i, :], DU[:, i, :], DBU[:, i, :]
                dve.wait_ge(*series_ready.at(b, i + 1))
                dve.scalar_tensor_tensor(s, s, 1.0 - 0.75 ** 2 / 3, e, ALU.add, ALU.mult).then_inc(sp_step.sem, 1)
                dve.wait_ge(*ln_ready.at(b, i + 1))
                dve.scalar_tensor_tensor(lg, e, SMALL, lg, ALU.is_lt, ALU.add).then_inc(sp_step.sem, 1)
                dve.wait_ge(*sp_step.at(b, 3 * i + 2))
                dve.tensor_tensor(s, s, lg, ALU.min).then_inc(sp_step.sem, 1)
                dve.wait_ge(*sp_step.at(b, 3 * i + 3))
                dve.wait_ge(*A.drained_at(b, "dt", i))
                dve.tensor_tensor(DT[:, i, :], DT[:, i, :], s, ALU.add).then_inc(dt_ready.sem, 1)
                dve.wait_ge(*dt_ready.at(b, i + 1))
                dve.tensor_tensor(s, DT[:, i, :], U[:, i, :], ALU.mult).then_inc(du_ready.sem, 1)

            def over_e(bank):
                return bank[:, :].unsqueeze(1).broadcast_to([P, KT, L])

            def inputs_b(b, n):
                dve.wait_ge(*b_bcast.at(b, n + 1))
                if n == 0:
                    dve.wait_ge(*du_ready.at(b))
                dve.tensor_tensor(DBU[:, :, :], DU[:, :, :], over_e(PB), ALU.mult).then_inc(dbu_done.sem, 1)

            def scan(b, n):
                dve.wait_ge(*dbu_done.at(b, n + 1))
                dve.wait_ge(*da_ready.at(b, n + 1))
                if n < 2:
                    dve.wait_ge(*y_init.at(b))
                else:
                    dve.wait_ge(*ysum_done.at(b, n - 1))
                dve.tensor_tensor_scan(flat(HB[n % 2]), flat(DA[n % 2]), flat(DBU), 0.0, ALU.mult, ALU.add)\
                   .then_inc(scan_done.sem, 1)

            def outputs_c(b, n):
                dve.wait_ge(*scan_done.at(b, n + 1))
                dve.wait_ge(*c_bcast.at(b, n + 1))
                dve.tensor_tensor(HB[n % 2][:, :, :], HB[n % 2][:, :, :], over_e(PC), ALU.mult)\
                   .then_inc(hc_done.sem, 1)

            def feature(b, g, i):
                two, one, bias, t, dst = (("q2", "q1", 1, T1, QF), ("k2", "k1", 3, T2, KF))[i]
                dve.wait_ge(*A.full_at(b, two, g))
                dve.wait_ge(*A.drained_at(b, one, g))
                dve.scalar_tensor_tensor(dst, A.bank(two, g)[:, :], FB[:, bias:bias + 1], t, ALU.add, ALU.mult)\
                   .then_inc(A.drained(two, g), 1)

            def states(b, g):
                dve.wait_ge(*A.full_at(b, "kv", g))
                kv = A.bank("kv", g)[:, 0:3 * P].rearrange("p (c d) -> p c d", c=TT - 1)
                dve.tensor_tensor(KVB, kv, HONES[:, :].unsqueeze(1).broadcast_to([P, TT - 1, P]), ALU.mult)\
                   .then_inc(A.drained("kv", g), 1)
                dve.wait_ge(*A.drained_at(b, "kv", g))
                dve.tensor_tensor(KVB[:, 1, :], KVB[:, 1, :], KVB[:, 0, :], ALU.add).then_inc(kv_step.sem, 1)
                dve.wait_ge(*kv_step.at(b, g + 1))
                dve.tensor_tensor(KVB[:, 2, :], KVB[:, 2, :], KVB[:, 1, :], ALU.add).then_inc(kv_ready.sem, 1)

            def masked(b, g, c):
                dve.wait_ge(*A.full_at(b, "S", g, c))
                dve.tensor_tensor(ST[c % 2].rearrange("p (h q) -> p h q", h=HPG),
                                  A.bank("S", g, c)[:, :].rearrange("p (h q) -> p h q", h=HPG),
                                  CAUSAL[:, :].unsqueeze(1).broadcast_to([P, HPG, P]), ALU.mult)\
                   .then_inc(A.drained("S", g, c), 1)

            def head_norm(b, g):
                dve.wait_ge(*rms_ready.at(b, g + 1))
                dve.tensor_tensor(OT[:, g, :], OBANK[:, :], OT[:, g, :], ALU.mult).then_inc(o_drained.sem, 1)

            def row_scales(f):
                dve.wait_ge(*xn2_ready.at(f))
                dve.tensor_reduce(AMX[:, :], OT[:, :, :], AX.X, ALU.max, apply_absolute_value=True)\
                   .then_inc(q_step.sem, 1)
                dve.wait_ge(*q_step.at(f, 1))
                dve.tensor_scalar(AMC[:, :], AMX[:, :], 1e-5, None, ALU.max).then_inc(q_step.sem, 1)
                dve.wait_ge(*q_step.at(f, 2))
                dve.reciprocal(RIN[:, :], AMC[:, :]).then_inc(q_step.sem, 1)
                dve.wait_ge(*q_step.at(f, 3))
                dve.tensor_scalar(SXQ[:, :], RIN[:, :], 127.0, None, ALU.mult).then_inc(q_step.sem, 1)
                dve.wait_ge(*q_step.at(f, 4))
                for i in range(2):
                    dve.tensor_scalar(SDQ[:, i, :], AMC[:, :], GA127[:, i:i + 1], None, ALU.mult)\
                       .then_inc(q_step.sem, 1)
                    dve.tensor_scalar(RSC[:, :, i], SXQ[:, :], GAI[:, i:i + 1], None, ALU.mult)\
                       .then_inc(q_step.sem, 1)

            def scale_parts(f):
                def times3(a):
                    return a.unsqueeze(3).broadcast_to([P, TT, 2, 3])

                dve.wait_ge(*q_step.at(f))
                dve.tensor_copy(RP[:, :, :, 0:3], times3(RSC[:, :, :])).then_inc(rp_step.sem, 1)
                dve.wait_ge(*rp_step.at(f, 1))
                dve.tensor_tensor(RS2[:, :, :], RSC[:, :, :], RP[:, :, :, 0], ALU.subtract).then_inc(rp_step.sem, 1)
                dve.wait_ge(*rp_step.at(f, 2))
                dve.tensor_copy(RP[:, :, :, 3:6], times3(RS2[:, :, :])).then_inc(rp_step.sem, 1)
                dve.wait_ge(*rp_step.at(f, 3))
                dve.tensor_tensor(RS3[:, :, :], RS2[:, :, :], RP[:, :, :, 3], ALU.subtract).then_inc(rp_step.sem, 1)
                dve.wait_ge(*rp_step.at(f, 4))
                dve.tensor_copy(RP[:, :, :, 6:9], times3(RS3[:, :, :])).then_inc(rp_step.sem, 1)

            def quantise_rows(f):
                for t in range(TT):
                    dve.tensor_scalar(OT[:, t, :], OT[:, t, :], SXQ[:, t:t + 1], MAGIC, ALU.mult, ALU.add)\
                       .then_inc(xr_ready.sem, 1)
                for t in range(TT):
                    dve.wait_ge(*xr_ready.at(f, t + 1))
                    dve.tensor_scalar(XQ[:, t, :], OT[:, t, :], -MAGIC, 127.0, ALU.add, ALU.min)\
                       .then_inc(xq_ready.sem, 1)

            def gated(f, t, c):
                dve.wait_ge(*F.full_at(f, "V", t, c))
                dve.wait_ge(*F.drained_at(f, "G", t, c))
                dve.scalar_tensor_tensor(H[:, c * 512:(c + 1) * 512], F.bank("V", t, c)[:, :],
                                         SDQ[:, 1, t:t + 1], G[(t * HC + c) % 2], ALU.mult, ALU.mult)\
                   .then_inc(F.drained("V", t, c), 1)

            def hidden_scales(f, t):
                s = 5 * t
                for r in F.all_drained_at(f, *(("V", t, c) for c in range(HC))):
                    dve.wait_ge(*r)
                dve.tensor_reduce(HAM[:, 0, t:t + 1], H, AX.X, ALU.max, apply_absolute_value=True)\
                   .then_inc(h_step.sem, 1)
                dve.wait_ge(*h_step.at(f, s + 1))
                dve.tensor_scalar(HAM[:, 1, t:t + 1], HAM[:, 0, t:t + 1], 1e-5, None, ALU.max).then_inc(h_step.sem, 1)
                dve.wait_ge(*h_step.at(f, s + 2))
                dve.reciprocal(HAM[:, 2, t:t + 1], HAM[:, 1, t:t + 1]).then_inc(h_step.sem, 1)
                dve.tensor_scalar(SHO[:, t:t + 1], HAM[:, 1, t:t + 1], GA127[:, 2:3], None, ALU.mult)\
                   .then_inc(h_step.sem, 1)
                dve.wait_ge(*h_step.at(f, s + 4))
                dve.tensor_scalar(HAM[:, 3, t:t + 1], HAM[:, 2, t:t + 1], 127.0, None, ALU.mult)\
                   .then_inc(h_step.sem, 1)

            def quantise_hidden(f, t):
                dve.wait_ge(*hr_ready.at(f, t + 1))
                if t:
                    dve.wait_ge(*F.full_at(f, "hT", t - 1, 1))
                dve.tensor_scalar(HQ, H, -MAGIC, 127.0, ALU.add, ALU.min).then_inc(hq_ready.sem, 1)

            def result(f, t):
                dve.wait_ge(*F.full_at(f, "O", t))
                if t == 0:
                    dve.wait_ge(*bias_added.at(f))
                dve.scalar_tensor_tensor(X2[:, t, :], F.bank("O", t)[:, :], SHO[:, t:t + 1], X2[:, t, :],
                                         ALU.mult, ALU.add).then_inc(F.drained("O", t), 1)


            def absolute_sums():
                dve.wait_ge(abs_done, WCH)
                dve.tensor_reduce(ASUM[:, :], ABS[:, :].rearrange("p (w c) -> p w c", w=3), AX.X, ALU.add)\
                   .then_inc(gam_step, 1)

            def ternary_scales():
                dve.wait_ge(gsum_full, 1)
                dve.tensor_scalar(GAM[:, :], F.banks[0][:, 0:3], 1.0 / (HID * D), 1e-5, ALU.mult, ALU.max)\
                   .then_inc(gam_step, 1)
                dve.wait_ge(gam_step, 2)
                dve.tensor_scalar(GAH[:, :], GAM[:, :], 0.5, None, ALU.mult).then_inc(gam_step, 1)
                dve.tensor_scalar(GAN[:, :], GAM[:, :], -0.5, None, ALU.mult).then_inc(gam_step, 1)
                dve.reciprocal(GAI[:, :], GAM[:, :]).then_inc(gam_step, 1)
                dve.tensor_scalar(GA127[:, :], GAM[:, :], 1.0 / 127, None, ALU.mult).then_inc(gam_step, 1)
                dve.wait_ge(gam_step, 6)

            def ternary(j):
                i, w = WCH + j, j // WPC
                src = X2[:, 2 * (i % 2):2 * (i % 2) + 2, :].rearrange("p a b -> p (a b)")
                dve.wait_ge(w_stage[i % 2], 16 * (i // 2 + 1))
                dve.wait_ge(tern_done, j)
                dve.tensor_scalar(TERN[:, :], src, GAN[:, w:w + 1], None, ALU.is_lt).then_inc(tern_step, 1)
                dve.wait_ge(tern_step, j + 1)
                dve.scalar_tensor_tensor(W8[:, j, :], src, GAH[:, w:w + 1], TERN[:, :], ALU.is_gt, ALU.subtract,
                                         saturate=False).then_inc(tern_done, 1)

            def residual(f, t):
                dve.wait_ge(*F.full_at(f, "wo", t))
                dve.tensor_tensor(X1[:, t, :], F.bank("wo", t)[:, :], X1[:, t, :], ALU.add)\
                   .then_inc(F.drained("wo", t), 1)

            def gate_shift(f):
                dve.wait_ge(*ln_rstd[1].at(f))
                dve.scalar_tensor_tensor(NMR[:, :], MV[:, :, 0], -1.0, RSTD[:, :], ALU.mult, ALU.mult)\
                   .then_inc(nmr_step.sem, 1)

            def gate_mixer(f):
                dve.wait_ge(*sz_ready.at(f))
                dve.wait_ge(*ysum_done.at(f))
                dve.tensor_tensor(YACC[:, :, :], YACC[:, :, :], Z, ALU.mult).then_inc(yg_ready.sem, 1)

            def add_mixer(f):
                for t in range(TT):
                    dve.wait_ge(*F.full_at(f, "yT", t))
                    dve.tensor_tensor(X2[:, t, :], F.bank("yT", t)[:, :], X1[:, t, :], ALU.add)\
                       .then_inc(F.drained("yT", t), 1)

            def step(b, f):
                new, old = b is not None, f is not None

                def tile_with_slot(t, n, beside=None):
                    slot = new and n is not None
                    if old:
                        if t:
                            dve.wait_ge(*hq_ready.at(f, t))
                        gated(f, t, 0)
                    if slot:
                        scan(b, n)
                    if old:
                        gated(f, t, 1)
                    if slot:
                        outputs_c(b, n)
                    if old:
                        gated(f, t, 2)
                        gated(f, t, 3)
                        hidden_scales(f, t)
                    if slot:
                        inputs_b(b, n + 1)
                    if old:
                        quantise_hidden(f, t)
                        if t:
                            result(f, t - 1)

                if new:
                    conv(b, 0)
                if old:
                    head_norm(f, GROUPS - 1)
                if new:
                    conv(b, 1)
                    conv(b, 2)
                if old:
                    residual(f, 0)
                if new:
                    conv(b, 3)
                if old:
                    residual(f, 1)
                    residual(f, 2)
                if new:
                    dve.wait_ge(*xb_loaded.at(b))
                    stats(b, 0, XB)
                    normed(b, 0, XB, xn_ready)
                    split(b)
                if old:
                    residual(f, 3)
                    for r in F.all_drained_at(f, *(("wo", t) for t in range(TT))):
                        dve.wait_ge(*r)
                    stats(f, 1, X1)
                if new:
                    softplus(b, 0)
                if old:
                    gate_shift(f)
                if new:
                    for e in range(1, KT):
                        softplus(b, e)
                if old:
                    gate_mixer(f)
                if new:
                    inputs_b(b, 0)
                if old:
                    add_mixer(f)
                    for r in F.all_drained_at(f, *(("yT", t) for t in range(TT))):
                        dve.wait_ge(*r)
                    stats(f, 2, X2)
                if new:
                    scan(b, 0)
                if old:
                    normed(f, 2, X2, xn2_ready)
                    row_scales(f)
                    scale_parts(f)
                    quantise_rows(f)
                if new:
                    outputs_c(b, 0)
                    inputs_b(b, 1)
                if new and old:
                    dve.wait_ge(*bc_parts.at(b))
                tile_with_slot(0, 1)
                if not old:
                    dve.wait_ge(*A.full_at(b, "xnT", KT - 1))
                    more_setup(setup_step)
                for t in range(1, TT):
                    tile_with_slot(t, t + 1)
                if not new:
                    result(f, TT - 1)
                    return
                for g in range(GROUPS):
                    n = 5 + 3 * g
                    more = g + 1 < GROUPS
                    if not more and old:
                        dve.wait_ge(*out_stored.at(f))
                    if g:
                        inputs_b(b, n)
                    scan(b, n)
                    if g == 0 and old:
                        result(f, TT - 1)
                    feature(b, g, 0)
                    outputs_c(b, n)
                    feature(b, g, 1)
                    weights_beside(n, old)
                    n += 1
                    inputs_b(b, n)
                    scan(b, n)
                    masked(b, g, 0)
                    states(b, g)
                    if g:
                        head_norm(b, g - 1)
                    if not more:
                        masked(b, g, 1)
                    outputs_c(b, n)
                    if more:
                        masked(b, g, 1)
                    weights_beside(n, old)
                    if more:
                        n += 1
                        inputs_b(b, n)
                    masked(b, g, 2)
                    if more:
                        scan(b, n)
                    masked(b, g, 3)
                    if more:
                        outputs_c(b, n)
                        weights_beside(n, old)

            def weights_beside(n, old):
                if not old:
                    if n == 6:
                        absolute_sums()
                    if n == 7:
                        ternary_scales()
                    if n > 7:
                        for j in range(3 * (n - 8), 3 * (n - 7)):
                            ternary(j)

            setup_step = setup()
            step(0, None)
            with dve.Fori(1, BATCH) as b:
                step(b, b - 1)
            step(None, BATCH - 1)


def kernel(**inputs):
    import ml_dtypes
    import numpy as np
    import concourse.bacc as bacc
    from concourse.bass_utils import run_bass_kernel_spmd

    a = {k: np.asarray(v) for k, v in inputs.items()}
    at = {k[8:]: v for k, v in a.items() if k.startswith("L0_attn_")}
    mx = {k[9:]: v for k, v in a.items() if k.startswith("L0_xattn_")}
    ff = {k[7:]: v for k, v in a.items() if k.startswith("L0_ffn_")}

    def columns(v):
        return np.swapaxes(v.reshape(KT, P, *v.shape[1:]), 0, 1)

    fmaps = np.zeros((P, 4, P), np.float32)
    for i, n in enumerate(("fq1", "fq2", "fk1", "fk2")):
        for h in range(HPG):
            fmaps[DK * h:DK * (h + 1), i, DK * h:DK * (h + 1)] = at[n + "_w"].T

    def up(w):
        return w.T.reshape(KT, P, 2, 1024).transpose(0, 2, 1, 3).reshape(WPC, P, 1024)

    def downwards(w):
        return w.T.reshape(WPC, 2, P, D).transpose(0, 2, 1, 3).reshape(WPC, P, 1024)

    part_of_row = np.arange(P) % 64
    rows = dict(
        x=a["x"], ctxT=a["ctx_1024"].transpose(0, 2, 1), wqT=at["wq"].T, wkT=at["wk"].T, wvT=at["wv"].T,
        woT=at["wo"].T, fmaps=fmaps,
        fbias=np.stack([np.tile(at[n + "_b"], HPG) for n in ("fq1", "fq2", "fk1", "fk2")], axis=1),
        normw=np.tile(at["norm_w"], HPG)[:, None],
        inT=mx["in_proj_w"].T, convw=columns(mx["conv_w"][:, 0, :]), convb=columns(mx["conv_b"]),
        xpT=np.concatenate([mx["x_proj_w"][RANK:], mx["x_proj_w"][:RANK]], axis=0).T, dtpT=mx["dt_proj_w"].T,
        dtb=columns(mx["dt_proj_b"]), alog=columns(mx["A_log"]), dskip=columns(mx["D"]),
        wffn=np.concatenate([up(ff["gate_w"]), up(ff["val_w"]), downwards(ff["out_w"])], axis=0),
        brow=np.stack([ff["gate_b"], ff["val_b"]]), outb=ff["out_b"],
        ident=np.eye(P, dtype=np.float32), ident16=np.eye(P, dtype=ml_dtypes.bfloat16),
        id96=np.tile(np.eye(32, dtype=ml_dtypes.bfloat16), (3, 1)),
        causal=np.triu(np.ones((P, P), np.float32)),
        headones=np.kron(np.eye(HPG, dtype=np.float32), np.ones((DK, DK), np.float32)),
        rowpick=((part_of_row[:, None] < 9) & (part_of_row[:, None] % 3 == np.arange(3))).astype(np.float32),
    )
    nc = bacc.Bacc("TRN2", target_bir_lowering=False, num_devices=1)
    arrays, args = {}, {}
    for name, v in rows.items():
        v = np.ascontiguousarray(v)
        arrays[f"in_{name}"] = v
        args[name] = nc.dram_tensor(f"in_{name}", v.shape, mybir.dt.from_np(v.dtype), kind="ExternalInput").ap()
    args["out"] = nc.dram_tensor("out_dram", (BATCH, L, D), fp32, kind="ExternalOutput").ap()
    decoder_layer(nc, **args)
    return run_bass_kernel_spmd(nc, [arrays], core_ids=[0]).results[0]["out_dram"]
```

```python
from contextlib import ExitStack

import concourse.bass as bass
from concourse import mybir

fp32 = mybir.dt.float32
bf16 = mybir.dt.bfloat16
fp8 = mybir.dt.float8e4
ALU = mybir.AluOpType
ACT = mybir.ActivationFunctionType
AX = mybir.AxisListType

P = 128
BATCH, L, D = 4, 512, 512
CTX = 256
HEADS, DK = 16, 32
GROUPS = HEADS * DK // P
HPG = P // DK
TT = L // P
KT = D // P
N = 16
RANK = 16
TAPS = 4
HID = 2048
HC = HID // 512
HK = HID // P
WCH = 24
WPC = WCH // 3
SCALE = DK ** -0.5
EPS = 1e-5
MAGIC = 12582912.0
THIRD_ROOT = 3.0 ** -0.5
SMALL = 2.0 ** -6
X1_CHUNKS = WCH - 4
W_IN, W_MISC, W_ATTN = 16 * 9, 16 * 9, 16 * 4
SETUP_V = 13


class Signal:

    def __init__(self, ctx, nc, name, per_row):
        self.sem = ctx.enter_context(nc.semaphore(name))
        self.per_row = per_row

    def at(self, b, n=None):
        return self.sem, b * self.per_row + (self.per_row if n is None else n)


class Banks:

    def __init__(self, ctx, nc, name, count, products):
        self.banks = [ctx.enter_context(nc.psum_tensor(f"{name}{k}", [P, 512], fp32)) for k in range(count)]
        self.full_sem = [ctx.enter_context(nc.semaphore(f"{name}{k}_full")) for k in range(count)]
        self.drained_sem = [ctx.enter_context(nc.semaphore(f"{name}{k}_drained")) for k in range(count)]
        self.place = {key: (j % count, j // count) for j, key in enumerate(products)}
        assert len(self.place) == len(products)
        self.per_row = [len(range(k, len(products), count)) for k in range(count)]

    def bank(self, *key):
        return self.banks[self.place[key][0]]

    def full(self, *key):
        return self.full_sem[self.place[key][0]]

    def drained(self, *key):
        return self.drained_sem[self.place[key][0]]

    def opens(self, *key):
        return self.place[key][1] == 0

    def free_at(self, b, *key):
        k, r = self.place[key]
        return self.drained_sem[k], b * self.per_row[k] + r

    def full_at(self, b, *key):
        k, r = self.place[key]
        return self.full_sem[k], b * self.per_row[k] + r + 1

    def drained_at(self, b, *key):
        k, r = self.place[key]
        return self.drained_sem[k], b * self.per_row[k] + r + 1


    def all_drained_at(self, b, *keys):
        last = {}
        for key in keys:
            k, r = self.place[key]
            last[k] = max(last.get(k, -1), r)
        return [(self.drained_sem[k], b * self.per_row[k] + r + 1) for k, r in last.items()]


def row_products():
    out = [("xin", e) for e in range(KT)] + [("xdbl",)] + [("dt", e) for e in range(KT)]
    out += [("xnT", k) for k in range(KT)] + [("q", 0), ("k", 0), ("v", 0)]
    for g in range(GROUPS):
        out += [(m, g) for m in ("q1", "q2", "k1", "k2")]
        if g + 1 < GROUPS:
            out += [("q", g + 1)]
        if g:
            out += [("ms", g - 1)]
        out += [("kfT", g), ("S", g, 0), ("S", g, 1), ("kv", g)]
        if g + 1 < GROUPS:
            out += [("k", g + 1)]
        out += [("S", g, 2), ("S", g, 3)]
        if g + 1 < GROUPS:
            out += [("v", g + 1)]
    return out


def end_products():
    out = [("ms",)] + [("wo", t) for t in range(TT)] + [("yT", t) for t in range(TT)]
    out += [("rT",)] + [("xqT", k) for k in range(KT)]
    for t in range(TT):
        for c in range(HC):
            out += [("G", t, c), ("V", t, c)]
            if t and c in (1, 2):
                out += [("hT", t - 1, c - 1)]
        if t:
            out += [("O", t - 1)]
    return out + [("hT", TT - 1, 0), ("hT", TT - 1, 1), ("O", TT - 1)]


def decoder_layer(nc, x, ctxT, wqT, wkT, wvT, woT, fmaps, fbias, normw, inT, convw, convb, xpT, dtpT, dtb, alog,
                  dskip, wffn, ffbias, outb, ident, ident16, id96, causal, headones, out, parts):
    ctx = ExitStack()
    with ctx:
        def sb(name, shape, dt=fp32):
            return ctx.enter_context(nc.sbuf_tensor(name, shape, dt))

        def signal(name, per_row):
            return Signal(ctx, nc, name, per_row)

        def once(name):
            return ctx.enter_context(nc.semaphore(name))

        WQ, WK, WV, WO = (sb(n, [P, KT, D]) for n in ("WQ", "WK", "WV", "WO"))
        FM = sb("FM", [P, 4, P])
        FB = sb("FB", [P, 4])
        FBS = sb("FBS", [P, 1])
        NW = sb("NW", [P, 1])
        WIN = sb("WIN", [P, CTX // P, D])
        CW = sb("CW", [P, KT, TAPS])
        CB = sb("CB", [P, KT])
        WXP = sb("WXP", [P, KT, 2 * N + RANK])
        WDT = sb("WDT", [2 * N + RANK, D])
        DTB = sb("DTB", [P, KT])
        ACOL = sb("ACOL", [P, KT, N])
        DSK = sb("DSK", [P, KT])
        W8 = sb("W8", [P, WCH, 1024], fp8)
        BROW = sb("BROW", [P, HID], bf16)
        RP = sb("RP", [P, TT, 2, 64], bf16)
        RT = sb("RT", [P, TT, P], bf16)
        ZROW = sb("ZROW", [32, P], bf16)
        OUTB = sb("OUTB", [P, D])
        IDF = sb("IDF", [P, P])
        IDB = sb("IDB", [P, P], bf16)
        ID96 = sb("ID96", [96, 32], bf16)
        CAUSAL = sb("CAUSAL", [P, P])
        HONES = sb("HONES", [P, P])
        ONES = sb("ONES", [P, P])
        BIAS = sb("BIAS", [P, HID // 64])
        BREST = sb("BREST", [P, HID // 64])
        BPART = sb("BPART", [P, 3, HID // 64], bf16)
        EPSC = sb("EPSC", [P, 1])
        MAGICC = sb("MAGICC", [P, 1])
        MAGICN = sb("MAGICN", [P, 1])
        SHIFTC = sb("SHIFTC", [P, 1])
        ONEC = sb("ONEC", [P, 1])
        CT = sb("CT", [P, CTX // P, L])
        XBC = sb("XBC", [2 * N + RANK, L])
        BC3 = sb("BC3", [96, L], bf16)
        DT = sb("DT", [P, KT, L])
        DU = sb("DU", [P, KT, L])
        DBU = sb("DBU", [P, KT, L])
        YACC = sb("YACC", [P, KT, L])
        DA = [sb(f"DA{i}", [P, KT, L]) for i in range(2)]
        HB = [sb(f"HB{i}", [P, KT, L]) for i in range(2)]
        U, EX = HB
        X1 = sb("X1", [P, TT, D])
        X2 = sb("X2", [P, TT, D])
        XNT = sb("XNT", [P, KT, L])
        OT = sb("OT", [P, KT, L])
        ARENA = sb("ARENA", [P, 6144])
        DECAY = [DA[0], DA[1], X1, DA[0], OT] + [DA[n % 2] for n in range(5, N)]

        def part(off, n, dt=fp32):
            a = ARENA[:, off:off + n]
            return a if dt == fp32 else a.bitcast(dt)

        QT, KTT, T1, T2, QF, KF = (part(512 * i, 512) for i in range(6))
        KFN = part(3072, 512).rearrange("p (c d) -> p c d", c=TT)
        V = [part(3584 + 512 * i, 512).rearrange("p (c d) -> p c d", c=TT) for i in range(2)]
        ST = [part(4608 + 512 * i, 512) for i in range(2)]
        BCR = ST[0][0:32, :]
        BC2 = ST[1][0:32, 0:L // 2].bitcast(bf16)
        XB = part(2560, 2048).rearrange("p (t d) -> p t d", t=TT)
        Z = part(0, 2048).rearrange("p (t d) -> p t d", t=TT)
        KVB = part(5632, 384).rearrange("p (c d) -> p c d", c=3)
        XQ = part(0, 1024, bf16).rearrange("p (t d) -> p t d", t=TT)
        HQ = part(0, 1024, bf16)
        XQT = part(1024, 1024, bf16).rearrange("p (k t) -> p k t", k=KT)
        G = [part(2048 + 512 * i, 512) for i in range(2)]
        HT = part(3072, 1024, bf16).rearrange("p (k t) -> p k t", k=HK)
        H = part(4096, 2048)
        w8 = W8[:, :, :].rearrange("p c n -> p (c n)")
        halves = [a[:, 2 * i:2 * i + 2, :].rearrange("p a b -> p (a b)") for a in (X2, X1) for i in range(2)]
        ABS_STAGE = [w8[:, 4096 * i:4096 * (i + 1)].bitcast(fp32) for i in range(WCH * 1024 // 4096)] + halves[:2]
        TERN_STAGE = halves + [part(0, 1024), part(1024, 1024)]

        def tern_buffer(j):
            return j % 4 if j < X1_CHUNKS else (0, 1, 4, 5)[j - X1_CHUNKS]

        FENCE = sb("FENCE", [P, 1])
        BST = sb("BST", [P, TT, 6])
        MV = sb("MV", [P, TT, 2])
        LNV = sb("LNV", [P, TT])
        RSTD = sb("RSTD", [P, TT])
        NMR = sb("NMR", [P, TT])
        AMX = sb("AMX", [P, TT])
        AMC = sb("AMC", [P, TT])
        RIN = sb("RIN", [P, TT])
        SXQ = sb("SXQ", [P, TT])
        SDQ = sb("SDQ", [P, 2, TT])
        RSC = sb("RSC", [P, TT, 2])
        RS2 = sb("RS2", [P, TT, 2])
        RS3 = sb("RS3", [P, TT, 2])
        HAM = sb("HAM", [P, 5, TT])
        SHO = sb("SHO", [P, TT])
        ABS = sb("ABS", [P, WCH])
        ASUM = sb("ASUM", [P, 3])
        GAM = sb("GAM", [P, 3])
        GAI = sb("GAI", [P, 3])
        GA127 = sb("GA127", [P, 3])

        A = Banks(ctx, nc, "bankA", 3, row_products())
        F = Banks(ctx, nc, "bankF", 3, end_products())
        OBANK = F.banks[2]
        PB = ctx.enter_context(nc.psum_tensor("PB", [P, 512], fp32))
        PC = ctx.enter_context(nc.psum_tensor("PC", [P, 512], fp32))

        w_in = once("w_in")
        w_attn = once("w_attn")
        bias_parts = once("bias_parts")
        parts_stored = once("parts_stored")
        brow_loaded = once("brow_loaded")
        w_misc = once("w_misc")
        x_loaded = signal("x_loaded", 16)
        xb_loaded = signal("xb_loaded", 16)
        ctx_loaded = signal("ctx_loaded", 16)
        out_stored = signal("out_stored", 16 * TT)
        setup_v = once("setup_v")
        setup_a = once("setup_a")
        w_abs = [once(f"w_abs{i}") for i in range(len(ABS_STAGE))]
        w_tern = [once(f"w_tern{i}") for i in range(len(TERN_STAGE))]
        abs_done = once("abs_done")
        tern_step = once("tern_step")
        tern_done = once("tern_done")
        gsum_full = once("gsum_full")
        gam_step = once("gam_step")
        tap_done = signal("tap_done", KT)
        conv_step = signal("conv_step", KT * (TAPS - 2))
        u_ready = signal("u_ready", KT)
        split_step = signal("split_step", 5)
        bc_parts = signal("bc_parts", 1)
        dt_raw = signal("dt_raw", KT)
        ex_ready = signal("ex_ready", KT)
        series_ready = signal("series_ready", KT)
        ln_ready = signal("ln_ready", KT)
        sp_step = signal("sp_step", 3 * KT)
        dt_ready = signal("dt_ready", KT)
        du_ready = signal("du_ready", KT)
        y_init = signal("y_init", 1)
        x1_zeroed = signal("x1_zeroed", 1)
        ot_zeroed = signal("ot_zeroed", 1)
        da_ready = signal("da_ready", N)
        b_bcast = signal("b_bcast", N)
        c_bcast = signal("c_bcast", N)
        dbu_done = signal("dbu_done", N)
        scan_done = signal("scan_done", N)
        hc_done = signal("hc_done", N)
        ysum_done = signal("ysum_done", N)
        ln_stats = [signal(f"ln{i}_stats", 2 * TT) for i in range(3)]
        ln_log = [signal(f"ln{i}_log", 1) for i in range(3)]
        ln_rstd = [signal(f"ln{i}_rstd", 1) for i in range(3)]
        nmr_step = signal("nmr_step", 1)
        xn_ready = signal("xn_ready", TT)
        kv_step = signal("kv_step", GROUPS)
        kv_ready = signal("kv_ready", GROUPS)
        o_full = signal("o_full", GROUPS)
        o_drained = signal("o_drained", GROUPS)
        sq_ready = signal("sq_ready", GROUPS)
        rms_ready = signal("rms_ready", GROUPS)
        sz_ready = signal("sz_ready", TT)
        yg_ready = signal("yg_ready", 1)
        xn2_ready = signal("xn2_ready", TT)
        q_step = signal("q_step", 8)
        xr_ready = signal("xr_ready", 4)
        xq_ready = signal("xq_ready", TT)
        rp_step = signal("rp_step", 5)
        h_step = signal("h_step", 6 * TT)
        hr_ready = signal("hr_ready", TT)
        hq_ready = signal("hq_ready", TT)
        bias_added = signal("bias_added", 1)

        block = ctx.enter_context(nc.Block())

        @block.sync
        def _(sp):
            for dst, src in ((CT[:, :, :], ctxT[0].rearrange("(k p) t -> p k t", p=P)),):
                sp.dma_start(dst, src).then_inc(ctx_loaded.sem, 16)
            for dst, src in ((WIN[:, :, :], inT.rearrange("(k p) n -> p k n", p=P)),
                             (CW[:, :, :], convw), (CB[:, :], convb),
                             (WXP[:, :, :], xpT.rearrange("(k p) n -> p k n", p=P)),
                             (WDT[2 * N:, :], dtpT), (DTB[:, :], dtb), (ACOL[:, :, :], alog), (DSK[:, :], dskip),
                             (ID96[:, :], id96)):
                sp.dma_start(dst, src).then_inc(w_in, 16)
            sp.dma_start(XB, x[0].rearrange("(t p) d -> p t d", p=P)).then_inc(xb_loaded.sem, 16)
            for dst, src in ((IDF[:, :], ident), (IDB[:, :], ident16), (CAUSAL[:, :], causal),
                             (HONES[:, :], headones), (FM[:, :, :], fmaps),
                             (FB[:, :], fbias), (NW[:, :], normw), (OUTB[:, :], outb.partition_broadcast(P)),
                             (BIAS[:, :], ffbias)):
                sp.dma_start(dst, src).then_inc(w_misc, 16)
            for dst, src in ((WQ, wqT), (WK, wkT), (WV, wvT), (WO, woT)):
                sp.dma_start(dst[:, :, :], src.rearrange("(k p) n -> p k n", p=P)).then_inc(w_attn, 16)
            def next_context(b):
                sp.wait_ge(*A.full_at(b, "xin", KT - 1))
                sp.dma_start(CT[:, :, :], ctxT[b + 1].rearrange("(k p) t -> p k t", p=P)).then_inc(ctx_loaded.sem, 16)

            for i in range(WCH):
                if i >= len(ABS_STAGE):
                    sp.wait_ge(abs_done, i - len(ABS_STAGE) + 1)
                sp.dma_start(ABS_STAGE[i % len(ABS_STAGE)], wffn[i]).then_inc(w_abs[i % len(ABS_STAGE)], 16)
            sp.wait_ge(bias_parts, 6)
            for j in range(3):
                sp.dma_start(parts[j].rearrange("g (p n) -> (g p) n", p=64), BPART[:, j, :])\
                  .then_inc(parts_stored, 16)
            sp.wait_ge(parts_stored, 16 * 3)
            for g in range(2):
                for i in range(3):
                    sp.dma_start(BROW[64 * g + 3 * i:64 * g + 3 * i + 3, :], parts[:, g, :]).then_inc(brow_loaded, 16)
            next_context(0)
            sp.wait_ge(abs_done, WCH)
            sp.wait_ge(*scan_done.at(0, 3))
            for j in range(WCH):
                before = [m for m in range(j) if tern_buffer(m) == tern_buffer(j)]
                if before:
                    sp.wait_ge(tern_done, before[-1] + 1)
                elif tern_buffer(j) >= 4:
                    sp.wait_ge(*A.drained_at(0, "k2", GROUPS - 1))
                sp.dma_start(TERN_STAGE[tern_buffer(j)], wffn[j]).then_inc(w_tern[tern_buffer(j)], 16)
            sp.wait_ge(tern_done, X1_CHUNKS)
            sp.dma_start(X1[:, :, :], x[0].rearrange("(t p) d -> p t d", p=P)).then_inc(x_loaded.sem, 16)
            def row(b, more_rows=True):
                sp.wait_ge(*o_full.at(b - 1))
                sp.dma_start(XB, x[b].rearrange("(t p) d -> p t d", p=P)).then_inc(xb_loaded.sem, 16)
                if more_rows:
                    next_context(b)
                sp.wait_ge(*scan_done.at(b, 3))
                sp.dma_start(X1[:, :, :], x[b].rearrange("(t p) d -> p t d", p=P)).then_inc(x_loaded.sem, 16)
                for t in range(TT):
                    sp.wait_ge(*F.drained_at(b - 1, "O", t))
                    sp.dma_start(out[b - 1, t * P:(t + 1) * P, :], X2[:, t, :]).then_inc(out_stored.sem, 16)

            with sp.Fori(1, BATCH - 1) as b:
                row(b)
            row(BATCH - 1, more_rows=False)
            for t in range(TT):
                sp.wait_ge(*F.drained_at(BATCH - 1, "O", t))
                sp.dma_start(out[BATCH - 1, t * P:(t + 1) * P, :], X2[:, t, :]).then_inc(out_stored.sem, 16)
            sp.wait_ge(*out_stored.at(BATCH - 1))

        @block.tensor
        def _(pe):
            def wait_bank(free, *ready):
                pe.wait_ge(*free)
                for r in ready:
                    if r[0] is not free[0]:
                        pe.wait_ge(*r)

            def product(ring, b, key, terms, ready=()):
                if ring is F and ring.opens(*key):
                    for r in ready:
                        pe.wait_ge(*r)
                else:
                    wait_bank(ring.free_at(b, *key), *ready)
                for n, (o, lhs, rhs, start) in enumerate(terms):
                    last = pe.matmul(o, lhs, rhs, start=start, stop=n == len(terms) - 1)
                last.then_inc(ring.full(*key), 1)

            def over_k(o, pairs):
                return [(o, lhs, rhs, n == 0) for n, (lhs, rhs) in enumerate(pairs)]

            def xin(b, e):
                o = A.bank("xin", e)
                product(A, b, ("xin", e), over_k(o[:, :], [(WIN[:, k, e * P:(e + 1) * P], CT[:, k, :])
                                                           for k in range(CTX // P)]),
                        [ctx_loaded.at(b)])

            def xdbl(b):
                product(A, b, ("xdbl",), over_k(A.bank("xdbl")[0:2 * N + RANK, :],
                                                [(WXP[:, k, :], U[:, k, :]) for k in range(KT)]),
                        [u_ready.at(b)])

            def step_size(b, e):
                product(A, b, ("dt", e), over_k(A.bank("dt", e)[:, :],
                                                [(WDT[2 * N:, e * P:(e + 1) * P], XBC[2 * N:, :])]),
                        [A.drained_at(b, "xdbl")])

            def normed_T(b, k):
                o = A.bank("xnT", k)
                pe.wait_ge(*A.free_at(b, "xnT", k))
                pe.wait_ge(*xn_ready.at(b))
                for t in range(TT):
                    last = pe.transpose(o[:, t * P:(t + 1) * P], XB[:, t, k * P:(k + 1) * P], IDF[:, :])
                last.then_inc(A.full("xnT", k), 1)

            def qk(b, name, g):
                w = {"q": WQ, "k": WK}[name]
                product(A, b, (name, g), over_k(A.bank(name, g)[:, :],
                                                [(w[:, k, g * P:(g + 1) * P], XNT[:, k, :]) for k in range(KT)]),
                        A.all_drained_at(b, *(("xnT", k) for k in range(KT))))

            def v(b, g):
                o = A.bank("v", g)
                pe.wait_ge(*A.free_at(b, "v", g))
                for t in range(TT):
                    for k in range(KT):
                        last = pe.matmul(o[:, t * P:(t + 1) * P], XNT[:, k, t * P:(t + 1) * P],
                                         WV[:, k, g * P:(g + 1) * P], start=k == 0, stop=k == KT - 1)
                last.then_inc(A.full("v", g), 1)

            def feature(b, i, g):
                name = ("q1", "q2", "k1", "k2")[i]
                src, of = ((QT, "q"), (KTT, "k"))[i // 2]
                product(A, b, (name, g), over_k(A.bank(name, g)[:, :], [(FM[:, i, :], src)]),
                        [A.drained_at(b, of, g)])

            def keys_T(b, g):
                o = A.bank("kfT", g)
                wait_bank(A.free_at(b, "kfT", g), A.drained_at(b, "k2", g))
                for c in range(TT):
                    last = pe.transpose(o[:, c * P:(c + 1) * P], KF[:, c * P:(c + 1) * P], IDF[:, :])
                last.then_inc(A.full("kfT", g), 1)

            def kv(b, g):
                o = A.bank("kv", g)
                wait_bank(A.free_at(b, "kv", g), A.drained_at(b, "kfT", g), A.drained_at(b, "v", g))
                for c in range(TT - 1):
                    last = pe.matmul(o[:, c * P:(c + 1) * P], KFN[:, c, :], V[(g + 1) % 2][:, c, :], start=True, stop=True)
                last.then_inc(A.full("kv", g), 1)

            def scores(b, g, h):
                o = A.bank("S", g, h)
                rows = slice(DK * h, DK * (h + 1))
                wait_bank(A.free_at(b, "S", g, h), A.drained_at(b, "k2", g))
                for c in range(TT):
                    last = pe.matmul(o[:, c * P:(c + 1) * P], KF[rows, c * P:(c + 1) * P],
                                     QF[rows, c * P:(c + 1) * P], start=True, stop=True)
                last.then_inc(A.full("S", g, h), 1)

            def attend(b, g, pair):
                o = OBANK
                if pair == 0:
                    pe.wait_ge(*o_drained.at(b, g))
                    pe.wait_ge(*kv_ready.at(b, g + 1))
                    for c in range(1, TT):
                        pe.matmul(o[:, c * P:(c + 1) * P], KVB[:, c - 1, :], QF[:, c * P:(c + 1) * P],
                                  start=c == 1, stop=False, skip_group_check=True)
                heads = (2 * pair, 2 * pair + 1)
                for h in heads:
                    pe.wait_ge(*A.drained_at(b, "S", g, h))
                for c in range(TT):
                    for h in heads:
                        rows = slice(DK * h, DK * (h + 1))
                        last = pe.matmul(o[rows, c * P:(c + 1) * P], V[(g + 1) % 2][:, c, rows],
                                         ST[h % 2][:, c * P:(c + 1) * P], start=False, stop=True,
                                         skip_group_check=True)
                if pair:
                    last.then_inc(o_full.sem, 1)

            def mean_square(b, g):
                ring, key = (F, ("ms",)) if g == GROUPS - 1 else (A, ("ms", g))
                product(ring, b, key, over_k(ring.bank(*key)[:, :], [(HONES[:, :], OT[:, g, :])]),
                        [sq_ready.at(b, g + 1)])

            def project(b, t):
                product(F, b, ("wo", t), over_k(F.bank("wo", t)[:, :],
                                                [(OT[:, k, t * P:(t + 1) * P], WO[:, k, :]) for k in range(KT)]),
                        [o_drained.at(b)])

            def mixer_T(b, t):
                o = F.bank("yT", t)
                pe.wait_ge(*F.free_at(b, "yT", t))
                pe.wait_ge(*yg_ready.at(b))
                for e in range(KT):
                    last = pe.transpose(o[:, e * P:(e + 1) * P], YACC[:, e, t * P:(t + 1) * P], IDF[:, :])
                last.then_inc(F.full("yT", t), 1)

            def spread_b(b, n):
                pe.wait_ge(*dbu_done.at(b, n))
                if n == 0:
                    pe.wait_ge(*bc_parts.at(b))
                pe.matmul(PB[:, :], ID96[:, n:n + 1].broadcast_to([96, P]), BC3[:, :],
                          start=True, stop=True).then_inc(b_bcast.sem, 1)

            def spread_c(b, n):
                pe.wait_ge(*hc_done.at(b, n))
                pe.matmul(PC[:, :], ID96[:, N + n:N + n + 1].broadcast_to([96, P]), BC3[:, :],
                          start=True, stop=True).then_inc(c_bcast.sem, 1)

            def scales_T(f):
                o = F.bank("rT")[:, :].bitcast(bf16)
                pe.wait_ge(*F.free_at(f, "rT"))
                pe.wait_ge(*rp_step.at(f))
                for t in range(TT):
                    last = pe.transpose(o[:, t * P:(t + 1) * P], RP[:, t, :, :].rearrange("p g r -> p (g r)"),
                                        IDB[:, :])
                last.then_inc(F.full("rT"), 1)

            def rows_T(f, k):
                o = F.bank("xqT", k)[:, :].bitcast(bf16)
                pe.wait_ge(*F.free_at(f, "xqT", k))
                pe.wait_ge(*xq_ready.at(f))
                for t in range(TT):
                    last = pe.transpose(o[:, t * P:(t + 1) * P], XQ[:, t, k * P:(k + 1) * P], IDB[:, :])
                last.then_inc(F.full("xqT", k), 1)

            def hidden(f, t, beside):
                if t == 0:
                    for r in F.all_drained_at(f, ("rT",), *(("xqT", k) for k in range(KT))):
                        pe.wait_ge(*r)
                for c in range(HC):
                    for i, m in enumerate(("G", "V")):
                        o = F.bank(m, t, c)[:, :]
                        rows = slice(64 * i, 64 * i + 32)
                        pe.wait_ge(*F.free_at(f, m, t, c))
                        pe.matmul(o, RT[rows, t, :], BROW[rows, c * 512:(c + 1) * 512], start=True, stop=False)
                        for k in range(KT):
                            w = W8[:, WPC * i + 2 * k + c // 2, (c % 2) * 512:(c % 2) * 512 + 512]
                            last = pe.matmul(o, XQT[:, k, t * P:(t + 1) * P], w, start=False, stop=k == KT - 1)
                        last.then_inc(F.full(m, t, c), 1)
                    if c == 1:
                        beside()
                    if t and c in (1, 2):
                        hidden_T(f, t - 1, c - 1)

            def hidden_T(f, t, j):
                o = F.bank("hT", t, j)[:, :].bitcast(bf16)
                pe.wait_ge(*F.free_at(f, "hT", t, j))
                pe.wait_ge(*hq_ready.at(f, t + 1))
                for k in range(HK // 2):
                    kk = j * HK // 2 + k
                    last = pe.transpose(o[:, k * P:(k + 1) * P], HQ[:, kk * P:(kk + 1) * P], IDB[:, :])
                last.then_inc(F.full("hT", t, j), 1)

            def down(f, t):
                o = F.bank("O", t)[:, :]
                for r in F.all_drained_at(f, ("hT", t, 0), ("hT", t, 1)):
                    pe.wait_ge(*r)
                pe.wait_ge(*F.free_at(f, "O", t))
                pe.matmul(o[:, 0:2], ZROW[:, :], ZROW[:, 0:2], start=True, stop=False,
                          skip_group_check=True)
                for k in range(HK):
                    last = pe.matmul(o, HT[:, k, :], W8[:, 2 * WPC + k // 2, (k % 2) * 512:(k % 2) * 512 + 512],
                                     start=False, stop=k == HK - 1, skip_group_check=True)
                last.then_inc(F.full("O", t), 1)

            def step(b, f, more_rows=True):
                new, old = b is not None, f is not None

                def spread(n):
                    if new:
                        spread_b(b, n)
                        spread_c(b, n)

                if old:
                    mean_square(f, GROUPS - 1)
                else:
                    xin(b, 0)
                    xin(b, 1)
                if new:
                    xin(b, 2)
                if old:
                    project(f, 0)
                if new:
                    xin(b, 3)
                if old:
                    project(f, 1)
                    project(f, 2)
                if new:
                    xdbl(b)
                if old:
                    project(f, 3)
                if new:
                    for e in range(KT):
                        step_size(b, e)
                spread(0)
                if new:
                    if not old:
                        pe.wait_ge(w_misc, W_MISC)
                    for k in range(KT):
                        normed_T(b, k)
                    if not old:
                        pe.wait_ge(w_attn, W_ATTN)
                    qk(b, "q", 0)
                if old:
                    for t in range(TT):
                        mixer_T(f, t)
                if new:
                    qk(b, "k", 0)
                    spread_b(b, 1)
                    v(b, 0)
                if old:
                    scales_T(f)
                    for k in range(KT):
                        rows_T(f, k)
                for t in range(TT):
                    def beside():
                        if new:
                            spread_c(b, t + 1)
                            spread_b(b, t + 2)

                    if old:
                        hidden(f, t, beside)
                        if t:
                            down(f, t - 1)
                    else:
                        beside()
                if new:
                    spread_c(b, 5)
                if old:
                    hidden_T(f, TT - 1, 0)
                    hidden_T(f, TT - 1, 1)
                if new:
                    if not old:
                        pe.wait_ge(setup_v, SETUP_V)
                    spread_b(b, 6)
                    for i in range(4):
                        feature(b, i, 0)
                if old:
                    down(f, TT - 1)
                if not new:
                    return
                for g in range(GROUPS):
                    n = 5 + 3 * g
                    more = g + 1 < GROUPS
                    if g:
                        feature(b, 0, g)
                        feature(b, 1, g)
                        spread_b(b, n + 1)
                        feature(b, 2, g)
                        feature(b, 3, g)
                    if more:
                        qk(b, "q", g + 1)
                    if g:
                        mean_square(b, g - 1)
                    spread_c(b, n + 1)
                    keys_T(b, g)
                    scores(b, g, 0)
                    scores(b, g, 1)
                    kv(b, g)
                    if more:
                        spread_b(b, n + 2)
                        qk(b, "k", g + 1)
                        spread_c(b, n + 2)
                    attend(b, g, 0)
                    scores(b, g, 2)
                    scores(b, g, 3)
                    if more:
                        spread_b(b, n + 3)
                        v(b, g + 1)
                    elif more_rows:
                        xin(b + 1, 0)
                        xin(b + 1, 1)
                    attend(b, g, 1)
                    if g == 0 and not old:
                        pe.wait_ge(gam_step, 1)
                        pe.matmul(F.banks[0][:, 0:3], ONES[:, :], ASUM[:, :], start=True, stop=True)\
                          .then_inc(gsum_full, 1)
                    if more:
                        spread_c(b, n + 3)

            pe.wait_ge(w_in, W_IN)
            step(0, None)
            pe.wait_ge(gam_step, 2)
            pe.wait_ge(brow_loaded, 16 * 6)
            with pe.Fori(1, BATCH - 1) as b:
                step(b, b - 1)
            step(BATCH - 1, BATCH - 2, more_rows=False)
            step(None, BATCH - 1)

        @block.scalar
        def _(act):
            def drain(b, ring, key, dst, src):
                act.wait_ge(*ring.full_at(b, *key))
                act.activation(dst, src, ACT.Copy).then_inc(ring.drained(*key), 1)

            def tap(b, e, first):
                act.wait_ge(*A.full_at(b, "xin", e))
                if e == 0 and not first:
                    act.wait_ge(*ysum_done.at(b - 1, N - 1))
                act.activation(U[:, e, :], A.bank("xin", e)[:, :], ACT.Identity, bias=CB[:, e:e + 1],
                               scale=CW[:, e, TAPS - 1:TAPS]).then_inc(tap_done.sem, 1)

            def silu_u(b, e):
                act.wait_ge(*A.drained_at(b, "xin", e))
                act.activation(U[:, e, :], U[:, e, :], ACT.Silu).then_inc(u_ready.sem, 1)

            def rstd(b, i):
                act.wait_ge(*ln_stats[i].at(b))
                act.activation(LNV[:, :], MV[:, :, 1], ACT.Ln, bias=EPSC[:, :]).then_inc(ln_log[i].sem, 1)
                act.wait_ge(*ln_log[i].at(b))
                act.activation(RSTD[:, :], LNV[:, :], ACT.Exp, scale=-0.5).then_inc(ln_rstd[i].sem, 1)

            def step_size(b, e):
                act.wait_ge(*A.full_at(b, "dt", e))
                if e == 0:
                    act.wait_ge(*ysum_done.at(b, 0))
                act.activation(EX[:, e, :], A.bank("dt", e)[:, :], ACT.Abs, bias=DTB[:, e:e + 1])\
                   .then_inc(dt_raw.sem, 1)
                act.activation(DT[:, e, :], A.bank("dt", e)[:, :], ACT.Relu, bias=DTB[:, e:e + 1])\
                   .then_inc(A.drained("dt", e), 1)
                act.wait_ge(*dt_raw.at(b, e + 1))
                act.activation(EX[:, e, :], EX[:, e, :], ACT.Exp, scale=-1.0).then_inc(ex_ready.sem, 1)

            def logs(b, e):
                if e == 0:
                    act.wait_ge(*scan_done.at(b, 0))
                act.wait_ge(*ex_ready.at(b, e + 1))
                act.activation(DU[:, e, :], EX[:, e, :], ACT.Square, bias=SHIFTC[:, :], scale=THIRD_ROOT)\
                   .then_inc(series_ready.sem, 1)
                act.activation(DBU[:, e, :], EX[:, e, :], ACT.Ln, bias=ONEC[:, :]).then_inc(ln_ready.sem, 1)

            def decay(b, n):
                if n == 0:
                    act.wait_ge(*dt_ready.at(b))
                if n == 2:
                    act.wait_ge(*x1_zeroed.at(b))
                elif n == 4:
                    act.wait_ge(*ot_zeroed.at(b))
                else:
                    before = [m for m in range(n) if DECAY[m] is DECAY[n]]
                    act.wait_ge(*scan_done.at(b, before[-1] + 1 if before else 0))
                for e in range(KT):
                    last = act.activation(DECAY[n][:, e, 1:], DT[:, e, 1:], ACT.Exp, scale=ACOL[:, e, n:n + 1])
                last.then_inc(da_ready.sem, 1)

            def values(b, g):
                drain(b, A, ("v", g), V[(g + 1) % 2].rearrange("p c d -> p (c d)"), A.bank("v", g)[:, :])

            def first_factor(b, g, i):
                name, dst = (("q1", T1), ("k1", T2))[i]
                act.wait_ge(*A.full_at(b, name, g))
                act.activation(dst, A.bank(name, g)[:, :], ACT.Identity, bias=FB[:, 2:3] if i else FBS[:, :],
                               scale=1.0 if i else SCALE).then_inc(A.drained(name, g), 1)

            def square(b, g):
                act.wait_ge(*o_full.at(b, g + 1))
                act.activation(OT[:, g, :], OBANK[:, :], ACT.Square).then_inc(sq_ready.sem, 1)

            def rms(b, g):
                ring, key = (F, ("ms",)) if g == GROUPS - 1 else (A, ("ms", g))
                act.wait_ge(*ring.full_at(b, *key))
                act.activation(OT[:, g, :], ring.bank(*key)[:, :], ACT.Ln, bias=EPSC[:, :], scale=1.0 / DK)\
                   .then_inc(ring.drained(*key), 1)
                act.wait_ge(*ring.drained_at(b, *key))
                act.activation(OT[:, g, :], OT[:, g, :], ACT.Exp, scale=-0.5).then_inc(rms_ready.sem, 1)

            def gate_z(b, t):
                act.wait_ge(*nmr_step.at(b, 1))
                act.activation(Z[:, t, :], X1[:, t, :], ACT.Silu, bias=NMR[:, t:t + 1],
                               scale=RSTD[:, t:t + 1]).then_inc(sz_ready.sem, 1)

            def rows_T(f):
                drain(f, F, ("rT",), RT[:, :, :].rearrange("p t r -> p (t r)"),
                      F.bank("rT")[:, :].bitcast(bf16)[:, 0:TT * P])
                for k in range(KT):
                    drain(f, F, ("xqT", k), XQT[:, k, :], F.bank("xqT", k)[:, :].bitcast(bf16)[:, 0:L])

            def hidden_T(f, t, j):
                half = HK // 2
                drain(f, F, ("hT", t, j), HT[:, j * half:(j + 1) * half, :].rearrange("p k t -> p (k t)"),
                      F.bank("hT", t, j)[:, :].bitcast(bf16)[:, 0:half * P])

            def gate(f, t):
                for c in range(HC):
                    n = t * HC + c
                    act.wait_ge(*F.full_at(f, "G", t, c))
                    if n >= 2:
                        act.wait_ge(*F.drained_at(f, "V", (n - 2) // HC, (n - 2) % HC))
                    act.activation(G[n % 2], F.bank("G", t, c)[:, :], ACT.Silu, scale=SDQ[:, 0, t:t + 1])\
                       .then_inc(F.drained("G", t, c), 1)
                    if t and c in (1, 2):
                        hidden_T(f, t - 1, c - 1)

            def round_rows(f):
                act.wait_ge(*q_step.at(f, 4))
                for t in range(TT):
                    act.activation(OT[:, t, :], OT[:, t, :], ACT.Identity, bias=MAGICC[:, :], scale=SXQ[:, t:t + 1])\
                       .then_inc(xr_ready.sem, 1)

            def round_hidden(f, t):
                act.wait_ge(*h_step.at(f, 6 * (t + 1)))
                act.activation(H, H, ACT.Identity, bias=MAGICC[:, :], scale=HAM[:, 3, t:t + 1])\
                   .then_inc(hr_ready.sem, 1)

            def ternary(j):
                act.wait_ge(tern_step, 2 * (j + 1))
                act.activation(W8[:, j, :], TERN_STAGE[tern_buffer(j)], ACT.Identity, bias=MAGICN[:, :],
                               saturate=False).then_inc(tern_done, 1)

            def abs_sums(i):
                act.wait_ge(w_abs[i % len(ABS_STAGE)], 16 * (i // len(ABS_STAGE) + 1))
                act.wait_ge(abs_done, i)
                stage = ABS_STAGE[i % len(ABS_STAGE)]
                act.activation(stage, stage, ACT.Abs, accum_out=ABS[:, i:i + 1])\
                   .then_inc(abs_done, 1)

            def step(b, f):
                new, old = b is not None, f is not None
                if new:
                    tap(b, 0, not old)
                if old:
                    rms(f, GROUPS - 1)
                if new:
                    tap(b, 1, not old)
                    tap(b, 2, not old)
                    if old:
                        rstd(b, 0)
                    silu_u(b, 0)
                    tap(b, 3, not old)
                    for e in range(1, KT):
                        silu_u(b, e)
                    drain(b, A, ("xdbl",), XBC[:, :], A.bank("xdbl")[0:2 * N + RANK, :])
                exp_and_log()
                if not old:
                    rstd(b, 0)
                if new:
                    step_size(b, 0)
                if old:
                    rstd(f, 1)
                if new:
                    step_size(b, 1)
                    logs(b, 0)
                    step_size(b, 2)
                    logs(b, 1)
                    step_size(b, 3)
                    logs(b, 2)
                    logs(b, 3)
                    for k in range(KT):
                        drain(b, A, ("xnT", k), XNT[:, k, :], A.bank("xnT", k)[:, :])
                if old:
                    for t in range(TT):
                        gate_z(f, t)
                    exp_and_log()
                if new:
                    decay(b, 0)
                if old:
                    rstd(f, 2)
                    if not new:
                        act.preload_act_table_set("silu_and_others")
                if new:
                    decay(b, 1)
                    decay(b, 2)
                    weights_beside(2, old)
                if new:
                    decay(b, 3)
                    weights_beside(3, old)
                if old:
                    round_rows(f)
                    rows_T(f)
                if new:
                    decay(b, 4)
                    weights_beside(4, old)
                if old:
                    for t in range(TT):
                        gate(f, t)
                        if new:
                            round_hidden(f, t)
                if new:
                    exp_and_log()
                    decay(b, 5)
                    weights_beside(5, old)
                if old:
                    hidden_T(f, TT - 1, 0)
                    hidden_T(f, TT - 1, 1)
                if not new:
                    return
                if not old:
                    act.wait_ge(setup_v, SETUP_V)
                drain(b, A, ("q", 0), QT, A.bank("q", 0)[:, :])
                drain(b, A, ("k", 0), KTT, A.bank("k", 0)[:, :])
                if old:
                    act.wait_ge(*hq_ready.at(f))
                values(b, 0)
                first_factor(b, 0, 0)
                first_factor(b, 0, 1)
                decay(b, 6)
                weights_beside(6, old)
                for g in range(GROUPS):
                    n = 5 + 3 * g
                    more = g + 1 < GROUPS
                    if g:
                        first_factor(b, g, 0)
                        first_factor(b, g, 1)
                        square(b, g - 1)
                    if more:
                        drain(b, A, ("q", g + 1), QT, A.bank("q", g + 1)[:, :])
                    if g:
                        rms(b, g - 1)
                    if not more:
                        weights_beside(16, old)
                    if g == 0 and old:
                        act.wait_ge(*F.full_at(f, "O", TT - 1))
                    drain(b, A, ("kfT", g), KFN.rearrange("p c d -> p (c d)"), A.bank("kfT", g)[:, :])
                    if more:
                        decay(b, n + 2)
                        weights_beside(n + 2, old)
                        drain(b, A, ("k", g + 1), KTT, A.bank("k", g + 1)[:, :])
                        decay(b, n + 3)
                        weights_beside(n + 3, old)
                        values(b, g + 1)
                        decay(b, n + 4)
                        weights_beside(n + 4, old)
                square(b, GROUPS - 1)
                weights_beside(17, old)

            def weights_beside(n, old):
                if not old and 1 < n < 8:
                    for i in range(4 * (n - 2), 4 * (n - 1)):
                        abs_sums(i)
                if not old and n > 9:
                    for j in range(3 * (n - 10), 3 * (n - 9)):
                        ternary(j)

            def exp_and_log():
                act.preload_act_table_set("natural_log_exp_and_others")

            act.wait_ge(w_in, W_IN)
            exp_and_log()
            act.activation(ACOL[:, :, :], ACOL[:, :, :], ACT.Exp).then_inc(setup_a, 1)
            act.wait_ge(setup_v, 5)
            step(0, None)
            with act.Fori(1, BATCH) as b:
                step(b, b - 1)
            step(None, BATCH - 1)

        @block.gpsimd
        def _(pool):
            def bias(f):
                pool.wait_ge(*xn2_ready.at(f))
                pool.tensor_tensor(X2[:, :, :], X2[:, :, :], OUTB[:, :].unsqueeze(1).broadcast_to([P, TT, D]),
                                   ALU.add).then_inc(bias_added.sem, 1)

            def row(b, f=None):
                pool.wait_ge(*u_ready.at(b))
                if f is not None:
                    pool.wait_ge(*F.full_at(f, "yT", TT - 1))
                pool.tensor_tensor(YACC[:, :, :], U[:, :, :], DSK[:, :].unsqueeze(2).broadcast_to([P, KT, L]),
                                   ALU.mult).then_inc(y_init.sem, 1)
                pool.wait_ge(*y_init.at(b))
                for n in range(N):
                    pool.wait_ge(*hc_done.at(b, n + 1))
                    if n:
                        pool.wait_ge(*ysum_done.at(b, n))
                    pool.tensor_tensor(YACC[:, :, :], YACC[:, :, :], HB[n % 2][:, :, :], ALU.add)\
                        .then_inc(ysum_done.sem, 1)
                    if n == 0 and f is not None:
                        bias(f)

            pool.wait_ge(w_in, W_IN)
            row(0)
            with pool.Fori(1, BATCH) as b:
                row(b, b - 1)
            bias(BATCH - 1)

        @block.vector
        def _(dve):
            def setup():
                done = 0

                def step(ins, hold=True):
                    nonlocal done
                    done += 1
                    ins.then_inc(setup_v, 1)
                    if hold:
                        dve.wait_ge(setup_v, done)

                step(dve.memset(EPSC[:, :], EPS), False)
                step(dve.memset(ONEC[:, :], 1.0), False)
                step(dve.memset(MAGICC[:, :], MAGIC), False)
                step(dve.memset(MAGICN[:, :], -MAGIC), False)
                step(dve.memset(SHIFTC[:, :], -0.75 * THIRD_ROOT), False)
                step(dve.memset(ONES[:, :], 1.0), False)
                step(dve.memset(DA[0][:, :, 0:1], 0.0), False)
                step(dve.memset(DA[1][:, :, 0:1], 0.0), False)
                step(dve.memset(RP[:, :, :, :], 0.0), False)
                dve.wait_ge(setup_a, 1)
                step(dve.tensor_scalar(ACOL[:, :, :], ACOL[:, :, :], -1.0, None, ALU.mult), False)
                return step

            def split_biases():
                def step(ins):
                    nonlocal done
                    done += 1
                    ins.then_inc(bias_parts, 1)
                    dve.wait_ge(bias_parts, done)

                done = 0
                dve.wait_ge(w_misc, W_MISC)
                step(dve.memset(BROW[:, :], 0.0))
                step(dve.tensor_copy(BPART[:, 0, :], BIAS[:, :]))
                step(dve.tensor_tensor(BREST[:, :], BIAS[:, :], BPART[:, 0, :], ALU.subtract))
                step(dve.tensor_copy(BPART[:, 1, :], BREST[:, :]))
                step(dve.tensor_tensor(BREST[:, :], BREST[:, :], BPART[:, 1, :], ALU.subtract))
                step(dve.tensor_copy(BPART[:, 2, :], BREST[:, :]))

            def more_setup(step):
                dve.wait_ge(w_misc, W_MISC)
                step(dve.tensor_scalar(FBS[:, :], FB[:, 0:1], SCALE, None, ALU.mult), False)
                dve.wait_ge(w_attn, W_ATTN)
                step(dve.tensor_scalar(WO[:, :, :], WO[:, :, :], NW[:, 0:1], None, ALU.mult), False)
                step(dve.memset(ZROW[:, :], 0.0), False)

            def flat(a):
                return a[:, :, :].rearrange("p a b -> p (a b)")

            def sums(b, i, src, t):
                dve.bn_stats(BST[:, t, :], src[:, t, :]).then_inc(ln_stats[i].sem, 1)

            def aggregate(b, i):
                dve.wait_ge(*ln_stats[i].at(b, TT))
                dve.memset(FENCE[:, :], 0.0)
                for t in range(TT):
                    dve.bn_aggr(MV[:, t, :], BST[:, t, :]).then_inc(ln_stats[i].sem, 1)

            def normed(b, i, src, ready):
                dve.wait_ge(*ln_rstd[i].at(b))
                dst = src if i == 0 else OT
                for t in range(TT):
                    dve.tensor_scalar(dst[:, t, :], src[:, t, :], MV[:, t, 0:1], RSTD[:, t:t + 1],
                                      ALU.subtract, ALU.mult).then_inc(ready.sem, 1)

            def conv(b, e):
                dve.wait_ge(*tap_done.at(b, e + 1))
                x_in = A.bank("xin", e)
                for s in range(1, TAPS):
                    if s > 1:
                        dve.wait_ge(*conv_step.at(b, e * (TAPS - 2) + s - 1))
                    ins = dve.scalar_tensor_tensor(U[:, e, s:], x_in[:, 0:L - s], CW[:, e, TAPS - 1 - s:TAPS - s],
                                                   U[:, e, s:], ALU.mult, ALU.add)
                    ins.then_inc(conv_step.sem if s < TAPS - 1 else A.drained("xin", e), 1)

            def split(b):
                dve.wait_ge(*A.drained_at(b, "xdbl"))
                dve.tensor_copy(BC3[0:32, :], XBC[0:32, :]).then_inc(split_step.sem, 1)
                dve.wait_ge(*split_step.at(b, 1))
                dve.tensor_tensor(BCR, XBC[0:32, :], BC3[0:32, :], ALU.subtract).then_inc(split_step.sem, 1)
                dve.wait_ge(*split_step.at(b, 2))
                dve.tensor_copy(BC2, BCR).then_inc(split_step.sem, 1)
                dve.wait_ge(*split_step.at(b, 3))
                dve.tensor_tensor(BCR, BCR, BC2, ALU.subtract).then_inc(split_step.sem, 1)
                dve.tensor_copy(BC3[32:64, :], BC2).then_inc(split_step.sem, 1)
                dve.wait_ge(*split_step.at(b, 4))
                dve.tensor_copy(BC3[64:96, :], BCR).then_inc(bc_parts.sem, 1)

            def softplus(b, i):
                e, s, lg = EX[:, i, :], DU[:, i, :], DBU[:, i, :]
                dve.wait_ge(*series_ready.at(b, i + 1))
                dve.scalar_tensor_tensor(s, s, 1.0 - 0.75 ** 2 / 3, e, ALU.add, ALU.mult).then_inc(sp_step.sem, 1)
                dve.wait_ge(*ln_ready.at(b, i + 1))
                dve.scalar_tensor_tensor(lg, e, SMALL, lg, ALU.is_lt, ALU.add).then_inc(sp_step.sem, 1)
                dve.wait_ge(*sp_step.at(b, 3 * i + 2))
                dve.tensor_tensor(s, s, lg, ALU.min).then_inc(sp_step.sem, 1)
                dve.wait_ge(*sp_step.at(b, 3 * i + 3))
                dve.wait_ge(*A.drained_at(b, "dt", i))
                dve.tensor_tensor(DT[:, i, :], DT[:, i, :], s, ALU.add).then_inc(dt_ready.sem, 1)
                dve.wait_ge(*dt_ready.at(b, i + 1))
                dve.tensor_tensor(s, DT[:, i, :], U[:, i, :], ALU.mult).then_inc(du_ready.sem, 1)

            def over_e(bank):
                return bank[:, :].unsqueeze(1).broadcast_to([P, KT, L])

            def inputs_b(b, n):
                dve.wait_ge(*b_bcast.at(b, n + 1))
                if n == 0:
                    dve.wait_ge(*du_ready.at(b))
                else:
                    dve.wait_ge(*scan_done.at(b, n))
                dve.tensor_tensor(DBU[:, :, :], DU[:, :, :], over_e(PB), ALU.mult).then_inc(dbu_done.sem, 1)

            def scan(b, n):
                dve.wait_ge(*dbu_done.at(b, n + 1))
                dve.wait_ge(*da_ready.at(b, n + 1))
                if n < 2:
                    dve.wait_ge(*y_init.at(b))
                else:
                    dve.wait_ge(*ysum_done.at(b, n - 1))
                dve.tensor_tensor_scan(flat(HB[n % 2]), flat(DECAY[n]), flat(DBU), 0.0, ALU.mult, ALU.add)\
                   .then_inc(scan_done.sem, 1)

            def outputs_c(b, n):
                dve.wait_ge(*scan_done.at(b, n + 1))
                dve.wait_ge(*c_bcast.at(b, n + 1))
                dve.tensor_tensor(HB[n % 2][:, :, :], HB[n % 2][:, :, :], over_e(PC), ALU.mult)\
                   .then_inc(hc_done.sem, 1)

            def feature(b, g, i):
                two, one, bias, t, dst = (("q2", "q1", 1, T1, QF), ("k2", "k1", 3, T2, KF))[i]
                dve.wait_ge(*A.full_at(b, two, g))
                dve.wait_ge(*A.drained_at(b, one, g))
                dve.scalar_tensor_tensor(dst, A.bank(two, g)[:, :], FB[:, bias:bias + 1], t, ALU.add, ALU.mult)\
                   .then_inc(A.drained(two, g), 1)

            def states(b, g):
                dve.wait_ge(*A.full_at(b, "kv", g))
                kv = A.bank("kv", g)[:, 0:3 * P].rearrange("p (c d) -> p c d", c=TT - 1)
                dve.tensor_tensor(KVB, kv, HONES[:, :].unsqueeze(1).broadcast_to([P, TT - 1, P]), ALU.mult)\
                   .then_inc(A.drained("kv", g), 1)
                dve.wait_ge(*A.drained_at(b, "kv", g))
                dve.tensor_tensor(KVB[:, 1, :], KVB[:, 1, :], KVB[:, 0, :], ALU.add).then_inc(kv_step.sem, 1)
                dve.wait_ge(*kv_step.at(b, g + 1))
                dve.tensor_tensor(KVB[:, 2, :], KVB[:, 2, :], KVB[:, 1, :], ALU.add).then_inc(kv_ready.sem, 1)

            def masked(b, g, c):
                dve.wait_ge(*A.full_at(b, "S", g, c))
                dve.tensor_tensor(ST[c % 2].rearrange("p (h q) -> p h q", h=HPG),
                                  A.bank("S", g, c)[:, :].rearrange("p (h q) -> p h q", h=HPG),
                                  CAUSAL[:, :].unsqueeze(1).broadcast_to([P, HPG, P]), ALU.mult)\
                   .then_inc(A.drained("S", g, c), 1)

            def head_norm(b, g):
                dve.wait_ge(*rms_ready.at(b, g + 1))
                dve.tensor_tensor(OT[:, g, :], OBANK[:, :], OT[:, g, :], ALU.mult).then_inc(o_drained.sem, 1)

            def row_scales(f):
                dve.wait_ge(*xn2_ready.at(f))
                dve.tensor_reduce(AMX[:, :], OT[:, :, :], AX.X, ALU.max, apply_absolute_value=True)\
                   .then_inc(q_step.sem, 1)
                dve.wait_ge(*q_step.at(f, 1))
                dve.tensor_scalar(AMC[:, :], AMX[:, :], 1e-5, None, ALU.max).then_inc(q_step.sem, 1)
                dve.wait_ge(*q_step.at(f, 2))
                dve.reciprocal(RIN[:, :], AMC[:, :]).then_inc(q_step.sem, 1)
                dve.wait_ge(*q_step.at(f, 3))
                dve.tensor_scalar(SXQ[:, :], RIN[:, :], 127.0, None, ALU.mult).then_inc(q_step.sem, 1)
                dve.wait_ge(*q_step.at(f, 4))
                for i in range(2):
                    dve.tensor_scalar(SDQ[:, i, :], AMC[:, :], GA127[:, i:i + 1], None, ALU.mult)\
                       .then_inc(q_step.sem, 1)
                    dve.tensor_scalar(RSC[:, :, i], SXQ[:, :], GAI[:, i:i + 1], None, ALU.mult)\
                       .then_inc(q_step.sem, 1)

            def scale_parts(f):
                def times3(a):
                    return a.unsqueeze(3).broadcast_to([P, TT, 2, 3])

                dve.wait_ge(*q_step.at(f))
                dve.tensor_copy(RP[:, :, :, 0:3], times3(RSC[:, :, :])).then_inc(rp_step.sem, 1)
                dve.wait_ge(*rp_step.at(f, 1))
                dve.tensor_tensor(RS2[:, :, :], RSC[:, :, :], RP[:, :, :, 0], ALU.subtract).then_inc(rp_step.sem, 1)
                dve.wait_ge(*rp_step.at(f, 2))
                dve.tensor_copy(RP[:, :, :, 3:6], times3(RS2[:, :, :])).then_inc(rp_step.sem, 1)
                dve.wait_ge(*rp_step.at(f, 3))
                dve.tensor_tensor(RS3[:, :, :], RS2[:, :, :], RP[:, :, :, 3], ALU.subtract).then_inc(rp_step.sem, 1)
                dve.wait_ge(*rp_step.at(f, 4))
                dve.tensor_copy(RP[:, :, :, 6:9], times3(RS3[:, :, :])).then_inc(rp_step.sem, 1)

            def quantise_rows(f):
                for t in range(TT):
                    dve.wait_ge(*xr_ready.at(f, t + 1))
                    dve.tensor_scalar(XQ[:, t, :], OT[:, t, :], -MAGIC, 127.0, ALU.add, ALU.min)\
                       .then_inc(xq_ready.sem, 1)

            def gated(f, t, c):
                dve.wait_ge(*F.full_at(f, "V", t, c))
                dve.wait_ge(*F.drained_at(f, "G", t, c))
                dve.scalar_tensor_tensor(H[:, c * 512:(c + 1) * 512], F.bank("V", t, c)[:, :],
                                         SDQ[:, 1, t:t + 1], G[(t * HC + c) % 2], ALU.mult, ALU.mult)\
                   .then_inc(F.drained("V", t, c), 1)

            def largest(f, t, half):
                for r in F.all_drained_at(f, ("V", t, 2 * half), ("V", t, 2 * half + 1)):
                    dve.wait_ge(*r)
                dve.tensor_reduce(HAM[:, 4 * half, t:t + 1], H[:, half * HID // 2:(half + 1) * HID // 2], AX.X, ALU.max,
                                  apply_absolute_value=True).then_inc(h_step.sem, 1)

            def hidden_scales(f, t):
                s = 6 * t
                largest(f, t, 1)
                dve.wait_ge(*h_step.at(f, s + 2))
                dve.tensor_scalar(HAM[:, 1, t:t + 1], HAM[:, 0, t:t + 1], HAM[:, 4, t:t + 1], 1e-5, ALU.max, ALU.max)\
                   .then_inc(h_step.sem, 1)
                dve.wait_ge(*h_step.at(f, s + 3))
                dve.reciprocal(HAM[:, 2, t:t + 1], HAM[:, 1, t:t + 1]).then_inc(h_step.sem, 1)
                dve.tensor_scalar(SHO[:, t:t + 1], HAM[:, 1, t:t + 1], GA127[:, 2:3], None, ALU.mult)\
                   .then_inc(h_step.sem, 1)
                dve.wait_ge(*h_step.at(f, s + 5))
                dve.tensor_scalar(HAM[:, 3, t:t + 1], HAM[:, 2, t:t + 1], 127.0, None, ALU.mult)\
                   .then_inc(h_step.sem, 1)

            def round_hidden(f, t):
                dve.wait_ge(*h_step.at(f, 6 * (t + 1)))
                dve.tensor_scalar(H, H, HAM[:, 3, t:t + 1], MAGIC, ALU.mult, ALU.add).then_inc(hr_ready.sem, 1)

            def quantise_hidden(f, t):
                dve.wait_ge(*hr_ready.at(f, t + 1))
                if t:
                    dve.wait_ge(*F.full_at(f, "hT", t - 1, 1))
                dve.tensor_scalar(HQ, H, -MAGIC, 127.0, ALU.add, ALU.min).then_inc(hq_ready.sem, 1)

            def result(f, t):
                dve.wait_ge(*F.full_at(f, "O", t))
                if t == 0:
                    dve.wait_ge(*bias_added.at(f))
                dve.scalar_tensor_tensor(X2[:, t, :], F.bank("O", t)[:, :], SHO[:, t:t + 1], X2[:, t, :],
                                         ALU.mult, ALU.add).then_inc(F.drained("O", t), 1)


            def absolute_sums():
                dve.wait_ge(abs_done, WCH)
                dve.tensor_reduce(ASUM[:, :], ABS[:, :].rearrange("p (w c) -> p w c", w=3), AX.X, ALU.add)\
                   .then_inc(gam_step, 1)

            def ternary_scales():
                dve.wait_ge(gsum_full, 1)
                dve.tensor_scalar(GAM[:, :], F.banks[0][:, 0:3], 1.0 / (HID * D), 1e-5, ALU.mult, ALU.max)\
                   .then_inc(gam_step, 1)
                dve.wait_ge(gam_step, 2)
                dve.reciprocal(GAI[:, :], GAM[:, :]).then_inc(gam_step, 1)
                dve.tensor_scalar(GA127[:, :], GAM[:, :], 1.0 / 127, None, ALU.mult).then_inc(gam_step, 1)
                dve.wait_ge(gam_step, 4)

            def ternary(j):
                src, w = TERN_STAGE[tern_buffer(j)], j // WPC
                loads = sum(tern_buffer(m) == tern_buffer(j) for m in range(j + 1))
                dve.wait_ge(w_tern[tern_buffer(j)], 16 * loads)
                dve.tensor_scalar(src, src, GAI[:, w:w + 1], MAGIC, ALU.mult, ALU.add).then_inc(tern_step, 1)
                dve.wait_ge(tern_step, 2 * j + 1)
                dve.tensor_scalar(src, src, MAGIC - 1.0, MAGIC + 1.0, ALU.max, ALU.min).then_inc(tern_step, 1)

            def residual(f, t):
                dve.wait_ge(*F.full_at(f, "wo", t))
                if t == 0:
                    dve.wait_ge(*x_loaded.at(f))
                dve.tensor_tensor(X1[:, t, :], F.bank("wo", t)[:, :], X1[:, t, :], ALU.add)\
                   .then_inc(F.drained("wo", t), 1)

            def gate_shift(f):
                dve.wait_ge(*ln_rstd[1].at(f))
                dve.scalar_tensor_tensor(NMR[:, :], MV[:, :, 0], -1.0, RSTD[:, :], ALU.mult, ALU.mult)\
                   .then_inc(nmr_step.sem, 1)

            def gate_mixer(f):
                dve.wait_ge(*sz_ready.at(f))
                dve.wait_ge(*ysum_done.at(f))
                dve.tensor_tensor(YACC[:, :, :], YACC[:, :, :], Z, ALU.mult).then_inc(yg_ready.sem, 1)

            def add_mixer(f, t):
                dve.wait_ge(*F.full_at(f, "yT", t))
                dve.tensor_tensor(X2[:, t, :], F.bank("yT", t)[:, :], X1[:, t, :], ALU.add)\
                   .then_inc(F.drained("yT", t), 1)

            def step(b, f):
                new, old = b is not None, f is not None

                def tile_with_slot(t, n):
                    slot = new and n is not None
                    if old:
                        if t:
                            dve.wait_ge(*hq_ready.at(f, t))
                        gated(f, t, 0)
                    if slot:
                        scan(b, n)
                    if old:
                        gated(f, t, 1)
                    if slot:
                        inputs_b(b, n + 1)
                    if old:
                        gated(f, t, 2)
                        largest(f, t, 0)
                        gated(f, t, 3)
                        hidden_scales(f, t)
                    if slot:
                        outputs_c(b, n)
                    if old:
                        if not new:
                            round_hidden(f, t)
                        if t and new:
                            result(f, t - 1)
                        quantise_hidden(f, t)
                        if t and not new:
                            result(f, t - 1)

                if new:
                    conv(b, 0)
                if old:
                    head_norm(f, GROUPS - 1)
                if new:
                    conv(b, 1)
                    dve.wait_ge(*xb_loaded.at(b))
                    for t in range(TT):
                        sums(b, 0, XB, t)
                    aggregate(b, 0)
                    conv(b, 2)
                if old:
                    residual(f, 0)
                if new:
                    conv(b, 3)
                if old:
                    residual(f, 1)
                else:
                    split_biases()
                if new:
                    normed(b, 0, XB, xn_ready)
                if old:
                    residual(f, 2)
                    for t in range(TT):
                        if t == TT - 1:
                            residual(f, t)
                        dve.wait_ge(*F.drained_at(f, "wo", t))
                        sums(f, 1, X1, t)
                    aggregate(f, 1)
                if new:
                    split(b)
                    softplus(b, 0)
                if old:
                    gate_shift(f)
                if new:
                    for e in range(1, KT):
                        softplus(b, e)
                if old:
                    gate_mixer(f)
                if new:
                    inputs_b(b, 0)
                if old:
                    for t in range(TT):
                        add_mixer(f, t)
                        if t:
                            dve.wait_ge(*F.drained_at(f, "yT", t - 1))
                            sums(f, 2, X2, t - 1)
                    dve.wait_ge(*F.drained_at(f, "yT", TT - 1))
                    sums(f, 2, X2, TT - 1)
                if new:
                    dve.memset(X1[:, :, 0:1], 0.0).then_inc(x1_zeroed.sem, 1)
                if old:
                    aggregate(f, 2)
                if new:
                    scan(b, 0)
                if old:
                    normed(f, 2, X2, xn2_ready)
                    row_scales(f)
                    scale_parts(f)
                if new:
                    outputs_c(b, 0)
                if old:
                    quantise_rows(f)
                if new and old:
                    dve.wait_ge(*xq_ready.at(f))
                if new:
                    dve.memset(OT[:, :, 0:1], 0.0).then_inc(ot_zeroed.sem, 1)
                    inputs_b(b, 1)
                if new and old:
                    dve.wait_ge(*bc_parts.at(b))
                tile_with_slot(0, 1)
                if not old:
                    more_setup(setup_step)
                for t in range(1, TT):
                    tile_with_slot(t, t + 1)
                if not new:
                    result(f, TT - 1)
                    return
                for g in range(GROUPS):
                    n = 5 + 3 * g
                    more = g + 1 < GROUPS
                    if not more and old:
                        dve.wait_ge(*out_stored.at(f))
                    if g:
                        inputs_b(b, n)
                    scan(b, n)
                    if g:
                        feature(b, g, 0)
                    outputs_c(b, n)
                    if g:
                        feature(b, g, 1)
                    weights_beside(n, old)
                    n += 1
                    inputs_b(b, n)
                    if g == 0:
                        feature(b, g, 0)
                        feature(b, g, 1)
                        if old:
                            result(f, TT - 1)
                    if more:
                        scan(b, n)
                        masked(b, g, 0)
                        states(b, g)
                        if g:
                            head_norm(b, g - 1)
                        outputs_c(b, n)
                        masked(b, g, 1)
                        weights_beside(n, old)
                        n += 1
                        inputs_b(b, n)
                        masked(b, g, 2)
                        scan(b, n)
                        masked(b, g, 3)
                        outputs_c(b, n)
                    else:
                        head_norm(b, g - 1)
                        masked(b, g, 0)
                        states(b, g)
                        masked(b, g, 1)
                        scan(b, n)
                        masked(b, g, 2)
                        masked(b, g, 3)
                        outputs_c(b, n)
                    weights_beside(n, old)

            def weights_beside(n, old):
                if not old:
                    if n == 6:
                        absolute_sums()
                    if n == 7:
                        ternary_scales()
                    if n > 7:
                        for j in range(3 * (n - 8), 3 * (n - 7)):
                            ternary(j)

            setup_step = setup()
            step(0, None)
            with dve.Fori(1, BATCH) as b:
                step(b, b - 1)
            step(None, BATCH - 1)


def kernel(**inputs):
    import ml_dtypes
    import numpy as np
    import concourse.bacc as bacc
    from concourse.bass_utils import run_bass_kernel_spmd

    a = {k: np.asarray(v) for k, v in inputs.items()}
    at = {k[8:]: v for k, v in a.items() if k.startswith("L0_attn_")}
    mx = {k[9:]: v for k, v in a.items() if k.startswith("L0_xattn_")}
    ff = {k[7:]: v for k, v in a.items() if k.startswith("L0_ffn_")}

    def columns(v):
        return np.swapaxes(v.reshape(KT, P, *v.shape[1:]), 0, 1)

    fmaps = np.zeros((P, 4, P), np.float32)
    for i, n in enumerate(("fq1", "fq2", "fk1", "fk2")):
        for h in range(HPG):
            fmaps[DK * h:DK * (h + 1), i, DK * h:DK * (h + 1)] = at[n + "_w"].T

    def up(w):
        return w.T.reshape(KT, P, 2, 1024).transpose(0, 2, 1, 3).reshape(WPC, P, 1024)

    def downwards(w):
        return w.T.reshape(WPC, 2, P, D).transpose(0, 2, 1, 3).reshape(WPC, P, 1024)

    rows = dict(
        x=a["x"], ctxT=a["ctx_1024"].transpose(0, 2, 1), wqT=at["wq"].T, wkT=at["wk"].T, wvT=at["wv"].T,
        woT=at["wo"].T, fmaps=fmaps,
        fbias=np.stack([np.tile(at[n + "_b"], HPG) for n in ("fq1", "fq2", "fk1", "fk2")], axis=1),
        normw=np.tile(at["norm_w"], HPG)[:, None],
        inT=mx["in_proj_w"].T, convw=columns(mx["conv_w"][:, 0, :]), convb=columns(mx["conv_b"]),
        xpT=np.concatenate([mx["x_proj_w"][RANK:], mx["x_proj_w"][:RANK]], axis=0).T, dtpT=mx["dt_proj_w"].T,
        dtb=columns(mx["dt_proj_b"]), alog=columns(mx["A_log"]), dskip=columns(mx["D"]),
        wffn=np.concatenate([up(ff["gate_w"]), up(ff["val_w"]), downwards(ff["out_w"])], axis=0),
        ffbias=np.concatenate([ff["gate_b"], ff["val_b"]]).reshape(P, HID // 64), outb=ff["out_b"],
        ident=np.eye(P, dtype=np.float32), ident16=np.eye(P, dtype=ml_dtypes.bfloat16),
        id96=np.tile(np.eye(32, dtype=ml_dtypes.bfloat16), (3, 1)),
        causal=np.triu(np.ones((P, P), np.float32)),
        headones=np.kron(np.eye(HPG, dtype=np.float32), np.ones((DK, DK), np.float32)),
    )
    nc = bacc.Bacc("TRN2", target_bir_lowering=False, num_devices=1)
    arrays, args = {}, {}
    for name, v in rows.items():
        v = np.ascontiguousarray(v)
        arrays[f"in_{name}"] = v
        args[name] = nc.dram_tensor(f"in_{name}", v.shape, mybir.dt.from_np(v.dtype), kind="ExternalInput").ap()
    args["out"] = nc.dram_tensor("out_dram", (BATCH, L, D), fp32, kind="ExternalOutput").ap()
    args["parts"] = nc.dram_tensor("bias_parts", (3, 2, HID), bf16).ap()
    decoder_layer(nc, **args)
    return run_bass_kernel_spmd(nc, [arrays], core_ids=[0]).results[0]["out_dram"]
```
